# Optimizing a Trainium2 kernel written in Bass

```python
import numpy as np
import jax
import jax.numpy as jnp

def _softmax(x, axis=-1):
    return jax.nn.softmax(x, axis=axis)

def _gelu(x):
    return jax.nn.gelu(x, approximate=True)

def _silu(x):
    return jax.nn.silu(x)

def _sigmoid(x):
    return jax.nn.sigmoid(x)

def _layernorm(x, axis=-1, eps=1e-05):
    m = jnp.mean(x, axis=axis, keepdims=True)
    v = jnp.var(x, axis=axis, keepdims=True)
    return (x - m) / jnp.sqrt(v + eps)

def _scatter_add(tgt, idx, src, axis=0):
    return tgt.at[idx].add(src)

def _segment_sum(src, seg, n):
    return jax.ops.segment_sum(src, seg, n)
kernel_name = 'mk_gnn_resnorm_d4_gnn_r8_5413b1'

def setup_inputs(seed: int=0):
    np.random.seed(seed)
    _w = jnp.asarray

    def _rec_inputs():
        import jax
        import jax.numpy as jnp
        _gk = jax.random.key(seed)
        x = -0.000202 + 1 * jax.random.normal(jax.random.fold_in(_gk, 1), (12500, 64), jnp.float32)
        _s = jax.random.randint(jax.random.fold_in(_gk, 2), (100000,), 0, 12500, jnp.int32)
        _d = jax.random.randint(jax.random.fold_in(_gk, 3), (100000,), 0, 12500, jnp.int32)
        _loop = jnp.arange(12500, dtype=jnp.int32)
        src = jnp.concatenate([_s, _d, _loop])
        dst = jnp.concatenate([_d, _s, _loop])
        _o = jnp.argsort(dst, stable=True)
        src = src[_o]
        dst = dst[_o]
        edge_attr_64 = 5.93493e-05 + 1.00006 * jax.random.normal(jax.random.fold_in(_gk, 13), (212500, 64), jnp.float32)
        node_vec = 0.0014194 + 1.00024 * jax.random.normal(jax.random.fold_in(_gk, 15), (12500,), jnp.float32)
        return (x, src, dst, edge_attr_64, node_vec)
    x, src, dst, edge_attr_64, node_vec = _rec_inputs()

    def _L0_gnn_setup():
        import jax, jax.numpy as jnp
        import numpy as np
        N_NODES = 12500
        N_EDGES = 150000
        D_NODE = 64
        D_EDGE = 64
        HIDDEN = 128
        EPS = 1e-05

        def _layer_norm(h, g, b):
            mu = jnp.mean(h, axis=-1, keepdims=True)
            var = jnp.mean(jnp.square(h - mu), axis=-1, keepdims=True)
            return (h - mu) * jax.lax.rsqrt(var + EPS) * g + b
        key = jax.random.key(seed)
        ks = jax.random.split(key, 10)
        d_in = D_NODE + D_EDGE
        s0 = 1.0 / np.sqrt(d_in)
        s1 = 1.0 / np.sqrt(HIDDEN)
        return {'x': jax.random.normal(ks[0], (N_NODES, D_NODE), dtype=jnp.float32), 'edge_index': jax.random.randint(ks[1], (2, N_EDGES), 0, N_NODES, dtype=jnp.int64), 'edge_attr': jax.random.normal(ks[2], (N_EDGES, D_EDGE), dtype=jnp.float32), 'W0': jax.random.uniform(ks[3], (d_in, HIDDEN), jnp.float32, -s0, s0), 'b0': jnp.zeros((HIDDEN,), jnp.float32), 'W1': jax.random.uniform(ks[4], (HIDDEN, HIDDEN), jnp.float32, -s1, s1), 'b1': jnp.zeros((HIDDEN,), jnp.float32), 'W2': jax.random.uniform(ks[5], (HIDDEN, D_NODE), jnp.float32, -s1, s1), 'b2': jnp.zeros((D_NODE,), jnp.float32), 'ln_g': jnp.ones((D_NODE,), jnp.float32), 'ln_b': jnp.zeros((D_NODE,), jnp.float32)}
    _L0_gnn_all = _L0_gnn_setup()
    _L0_gnn_in = {k: v for k, v in _L0_gnn_all.items() if k in ('W0', 'b0', 'W1', 'b1', 'W2', 'b2', 'ln_g', 'ln_b')}
    del _L0_gnn_all

    def _L1_gnn_setup():
        import jax, jax.numpy as jnp
        import numpy as np
        N, E, F_IN, HID, OUT = (12500, 125000, 64, 64, 64)

        def _sage_conv(h, src, dst, W_l, b_l, W_r):
            n = h.shape[0]
            summed = jax.ops.segment_sum(h[src], dst, num_segments=n)
            cnt = jax.ops.segment_sum(jnp.ones_like(dst, dtype=h.dtype), dst, num_segments=n)
            agg = summed / jnp.maximum(cnt, 1.0)[:, None]
            return agg @ W_l.T + b_l + h @ W_r.T
        key = jax.random.key(seed)
        ks = jax.random.split(key, 8)
        s = 1.0 / np.sqrt(F_IN)
        return {'x': jax.random.normal(ks[0], (N, F_IN), dtype=jnp.float32), 'edge_index': jax.random.randint(ks[1], (2, E), 0, N, dtype=jnp.int64), 'W1_l': jax.random.normal(ks[2], (HID, F_IN), dtype=jnp.float32) * s, 'b1_l': jnp.zeros((HID,), dtype=jnp.float32), 'W1_r': jax.random.normal(ks[3], (HID, F_IN), dtype=jnp.float32) * s, 'W2_l': jax.random.normal(ks[4], (OUT, HID), dtype=jnp.float32) * s, 'b2_l': jnp.zeros((OUT,), dtype=jnp.float32), 'W2_r': jax.random.normal(ks[5], (OUT, HID), dtype=jnp.float32) * s}
    _L1_gnn_all = _L1_gnn_setup()
    _L1_gnn_in = {k: v for k, v in _L1_gnn_all.items() if k in ('W1_l', 'b1_l', 'W1_r', 'W2_l', 'b2_l', 'W2_r')}
    del _L1_gnn_all

    def _L2_gnn_setup():
        import jax, jax.numpy as jnp
        import numpy as np
        N, E, D, ED, G = (12500, 200000, 64, 64, 512)
        LN_EPS = 1e-05

        def _gine_conv(x, src, dst, edge_attr, We, be, Wm, bm, eps):
            ea = jax.nn.silu(edge_attr @ We + be)
            msg = jax.nn.silu(jnp.maximum(x[src] + ea, 0.0) @ Wm + bm)
            agg = jax.ops.segment_sum(msg, dst, num_segments=x.shape[0])
            return agg + (1.0 + eps) * x

        def _graph_norm(x, g, gamma, beta):
            f = x.shape[1]
            cnt = jax.ops.segment_sum(jnp.ones((x.shape[0],), x.dtype), g, num_segments=G) * f
            cnt = jnp.maximum(cnt, 1.0)
            mean = jax.ops.segment_sum(x.sum(-1), g, num_segments=G) / cnt
            var = jax.ops.segment_sum((x * x).sum(-1), g, num_segments=G) / cnt - mean ** 2
            xn = (x - mean[g][:, None]) / jnp.sqrt(var + LN_EPS)[g][:, None]
            return xn * gamma + beta
        key = jax.random.key(seed)
        ks = jax.random.split(key, 16)
        s_e = 1.0 / np.sqrt(ED)
        s_n = 1.0 / np.sqrt(D)
        inp = {'x': jax.random.normal(ks[0], (N, D), jnp.float32), 'edge_index': jax.random.randint(ks[1], (2, E), 0, N, dtype=jnp.int32), 'edge_attr': jax.random.normal(ks[2], (E, ED), jnp.float32), 'node2graph': jnp.sort(jax.random.randint(ks[3], (N,), 0, G, dtype=jnp.int32)), 'We1': jax.random.normal(ks[4], (ED, D), jnp.float32) * s_e, 'be1': jnp.zeros((D,), jnp.float32), 'Wm1': jax.random.normal(ks[5], (D, D), jnp.float32) * s_n, 'bm1': jnp.zeros((D,), jnp.float32), 'eps1': jnp.array([0.1], jnp.float32), 'gamma1': jnp.ones((D,), jnp.float32), 'beta1': jnp.zeros((D,), jnp.float32), 'We2': jax.random.normal(ks[6], (ED, D), jnp.float32) * s_e, 'be2': jnp.zeros((D,), jnp.float32), 'Wm2': jax.random.normal(ks[7], (D, D), jnp.float32) * s_n, 'bm2': jnp.zeros((D,), jnp.float32), 'eps2': jnp.array([0.1], jnp.float32), 'gamma2': jnp.ones((D,), jnp.float32), 'beta2': jnp.zeros((D,), jnp.float32)}
        return inp
    _L2_gnn_all = _L2_gnn_setup()
    _L2_gnn_in = {k: v for k, v in _L2_gnn_all.items() if k in ('We1', 'be1', 'Wm1', 'bm1', 'eps1', 'gamma1', 'beta1', 'We2', 'be2', 'Wm2', 'bm2', 'eps2', 'gamma2', 'beta2')}
    del _L2_gnn_all

    def _L3_gnn_setup():
        import jax, jax.numpy as jnp
        import numpy as np
        N, E, D, H = (6250, 100000, 64, 4)
        key = jax.random.key(seed)
        ks = jax.random.split(key, 10)
        scale = 1.0 / np.sqrt(D)
        return {'node_embeddings': jax.random.normal(ks[0], (N, D), jnp.float32), 'node_sign_influence': jax.random.normal(ks[1], (N,), jnp.float32), 'src': jax.random.randint(ks[2], (E,), 0, N, jnp.int32), 'tgt': jax.random.randint(ks[3], (E,), 0, N, jnp.int32), 'Wq': jax.random.normal(ks[4], (D, H * D), jnp.float32) * scale, 'bq': jnp.zeros((H * D,), jnp.float32), 'Wk': jax.random.normal(ks[5], (D, H * D), jnp.float32) * scale, 'bk': jnp.zeros((H * D,), jnp.float32), 'Wv': jax.random.normal(ks[6], (D, H * D), jnp.float32) * scale, 'bv': jnp.zeros((H * D,), jnp.float32), 'Wo': jax.random.normal(ks[7], (H * D, D), jnp.float32) * (1.0 / np.sqrt(H * D)), 'bo': jnp.zeros((D,), jnp.float32)}
    _L3_gnn_all = _L3_gnn_setup()
    _L3_gnn_in = {k: v for k, v in _L3_gnn_all.items() if k in ('Wq', 'bq', 'Wk', 'bk', 'Wv', 'bv', 'Wo', 'bo')}
    del _L3_gnn_all
    return {'x': x, 'src': src, 'dst': dst, 'edge_attr_64': edge_attr_64, 'node_vec': node_vec, 'L0_gnn_W0': _L0_gnn_in['W0'], 'L0_gnn_b0': _L0_gnn_in['b0'], 'L0_gnn_W1': _L0_gnn_in['W1'], 'L0_gnn_b1': _L0_gnn_in['b1'], 'L0_gnn_W2': _L0_gnn_in['W2'], 'L0_gnn_b2': _L0_gnn_in['b2'], 'L0_gnn_ln_g': _L0_gnn_in['ln_g'], 'L0_gnn_ln_b': _L0_gnn_in['ln_b'], 'L1_gnn_W1_l': _L1_gnn_in['W1_l'], 'L1_gnn_b1_l': _L1_gnn_in['b1_l'], 'L1_gnn_W1_r': _L1_gnn_in['W1_r'], 'L1_gnn_W2_l': _L1_gnn_in['W2_l'], 'L1_gnn_b2_l': _L1_gnn_in['b2_l'], 'L1_gnn_W2_r': _L1_gnn_in['W2_r'], 'L2_gnn_We1': _L2_gnn_in['We1'], 'L2_gnn_be1': _L2_gnn_in['be1'], 'L2_gnn_Wm1': _L2_gnn_in['Wm1'], 'L2_gnn_bm1': _L2_gnn_in['bm1'], 'L2_gnn_eps1': _L2_gnn_in['eps1'], 'L2_gnn_gamma1': _L2_gnn_in['gamma1'], 'L2_gnn_beta1': _L2_gnn_in['beta1'], 'L2_gnn_We2': _L2_gnn_in['We2'], 'L2_gnn_be2': _L2_gnn_in['be2'], 'L2_gnn_Wm2': _L2_gnn_in['Wm2'], 'L2_gnn_bm2': _L2_gnn_in['bm2'], 'L2_gnn_eps2': _L2_gnn_in['eps2'], 'L2_gnn_gamma2': _L2_gnn_in['gamma2'], 'L2_gnn_beta2': _L2_gnn_in['beta2'], 'L3_gnn_Wq': _L3_gnn_in['Wq'], 'L3_gnn_bq': _L3_gnn_in['bq'], 'L3_gnn_Wk': _L3_gnn_in['Wk'], 'L3_gnn_bk': _L3_gnn_in['bk'], 'L3_gnn_Wv': _L3_gnn_in['Wv'], 'L3_gnn_bv': _L3_gnn_in['bv'], 'L3_gnn_Wo': _L3_gnn_in['Wo'], 'L3_gnn_bo': _L3_gnn_in['bo']}

def reference(x, src, dst, edge_attr_64, node_vec, L0_gnn_W0, L0_gnn_b0, L0_gnn_W1, L0_gnn_b1, L0_gnn_W2, L0_gnn_b2, L0_gnn_ln_g, L0_gnn_ln_b, L1_gnn_W1_l, L1_gnn_b1_l, L1_gnn_W1_r, L1_gnn_W2_l, L1_gnn_b2_l, L1_gnn_W2_r, L2_gnn_We1, L2_gnn_be1, L2_gnn_Wm1, L2_gnn_bm1, L2_gnn_eps1, L2_gnn_gamma1, L2_gnn_beta1, L2_gnn_We2, L2_gnn_be2, L2_gnn_Wm2, L2_gnn_bm2, L2_gnn_eps2, L2_gnn_gamma2, L2_gnn_beta2, L3_gnn_Wq, L3_gnn_bq, L3_gnn_Wk, L3_gnn_bk, L3_gnn_Wv, L3_gnn_bv, L3_gnn_Wo, L3_gnn_bo):
    import jax
    import jax.numpy as jnp

    def _L0_gnn_ref(x, edge_index, edge_attr, W0, b0, W1, b1, W2, b2, ln_g, ln_b):
        import jax, jax.numpy as jnp
        import numpy as np
        N_NODES = 12500
        N_EDGES = 150000
        D_NODE = 64
        D_EDGE = 64
        HIDDEN = 128
        EPS = 1e-05

        def _layer_norm(h, g, b):
            mu = jnp.mean(h, axis=-1, keepdims=True)
            var = jnp.mean(jnp.square(h - mu), axis=-1, keepdims=True)
            return (h - mu) * jax.lax.rsqrt(var + EPS) * g + b
        col = edge_index[1]
        agg = jax.ops.segment_sum(edge_attr, col, num_segments=N_NODES)
        h = jnp.concatenate([x, agg], axis=-1)
        h = jax.nn.relu(h @ W0 + b0)
        h = jax.nn.relu(h @ W1 + b1)
        h = h @ W2 + b2
        h = _layer_norm(h, ln_g, ln_b)
        return h + x

    def _L1_gnn_ref(x, edge_index, W1_l, b1_l, W1_r, W2_l, b2_l, W2_r):
        import jax, jax.numpy as jnp
        import numpy as np
        N, E, F_IN, HID, OUT = (12500, 125000, 64, 64, 64)

        def _sage_conv(h, src, dst, W_l, b_l, W_r):
            n = h.shape[0]
            summed = jax.ops.segment_sum(h[src], dst, num_segments=n)
            cnt = jax.ops.segment_sum(jnp.ones_like(dst, dtype=h.dtype), dst, num_segments=n)
            agg = summed / jnp.maximum(cnt, 1.0)[:, None]
            return agg @ W_l.T + b_l + h @ W_r.T
        src, dst = (edge_index[0], edge_index[1])
        h = jax.nn.relu(_sage_conv(x, src, dst, W1_l, b1_l, W1_r))
        return _sage_conv(h, src, dst, W2_l, b2_l, W2_r)

    def _L2_gnn_ref(x, edge_index, edge_attr, node2graph, We1, be1, Wm1, bm1, eps1, gamma1, beta1, We2, be2, Wm2, bm2, eps2, gamma2, beta2):
        import jax, jax.numpy as jnp
        import numpy as np
        N, E, D, ED, G = (12500, 200000, 64, 64, 512)
        LN_EPS = 1e-05

        def _gine_conv(x, src, dst, edge_attr, We, be, Wm, bm, eps):
            ea = jax.nn.silu(edge_attr @ We + be)
            msg = jax.nn.silu(jnp.maximum(x[src] + ea, 0.0) @ Wm + bm)
            agg = jax.ops.segment_sum(msg, dst, num_segments=x.shape[0])
            return agg + (1.0 + eps) * x

        def _graph_norm(x, g, gamma, beta):
            f = x.shape[1]
            cnt = jax.ops.segment_sum(jnp.ones((x.shape[0],), x.dtype), g, num_segments=G) * f
            cnt = jnp.maximum(cnt, 1.0)
            mean = jax.ops.segment_sum(x.sum(-1), g, num_segments=G) / cnt
            var = jax.ops.segment_sum((x * x).sum(-1), g, num_segments=G) / cnt - mean ** 2
            xn = (x - mean[g][:, None]) / jnp.sqrt(var + LN_EPS)[g][:, None]
            return xn * gamma + beta
        src, dst = (edge_index[0], edge_index[1])
        identity = x
        out = _gine_conv(x, src, dst, edge_attr, We1, be1, Wm1, bm1, eps1)
        out = _graph_norm(out, node2graph, gamma1, beta1)
        out = jnp.maximum(out, 0.0)
        out = _gine_conv(x, src, dst, edge_attr, We2, be2, Wm2, bm2, eps2)
        out = _graph_norm(out, node2graph, gamma2, beta2)
        out = out + identity
        return jnp.maximum(out, 0.0)

    def _L3_gnn_ref(node_embeddings, node_sign_influence, src, tgt, Wq, bq, Wk, bk, Wv, bv, Wo, bo):
        import jax, jax.numpy as jnp
        import numpy as np
        N, D = node_embeddings.shape
        H = Wq.shape[1] // D
        sqrt_d = np.float32(np.sqrt(D))
        Q = (node_embeddings @ Wq + bq).reshape(N, H, D)
        K = (node_embeddings @ Wk + bk).reshape(N, H, D)
        V = (node_embeddings @ Wv + bv).reshape(N, H, D)
        scores = jnp.einsum('ehd,ehd->eh', Q[src], K[tgt]) / sqrt_d
        scores = scores * node_sign_influence[src][:, None]
        m = jax.ops.segment_max(scores, src, num_segments=N)
        ex = jnp.exp(scores - m[src])
        s = jax.ops.segment_sum(ex, src, num_segments=N)
        attn = ex / (s[src] + 1e-10)
        out = jax.ops.segment_sum(V[tgt] * attn[:, :, None], src, num_segments=N)
        return out.reshape(N, H * D) @ Wo + bo
    edge_index = jnp.stack([src, dst])
    batch0 = jnp.zeros((12500,), jnp.int32)
    x = _layernorm(x + _L0_gnn_ref(x, edge_index, edge_attr_64, L0_gnn_W0, L0_gnn_b0, L0_gnn_W1, L0_gnn_b1, L0_gnn_W2, L0_gnn_b2, L0_gnn_ln_g, L0_gnn_ln_b), axis=-1)
    x = _layernorm(x + _L1_gnn_ref(x, edge_index, L1_gnn_W1_l, L1_gnn_b1_l, L1_gnn_W1_r, L1_gnn_W2_l, L1_gnn_b2_l, L1_gnn_W2_r), axis=-1)
    x = _layernorm(x + _L2_gnn_ref(x, edge_index, edge_attr_64, batch0, L2_gnn_We1, L2_gnn_be1, L2_gnn_Wm1, L2_gnn_bm1, L2_gnn_eps1, L2_gnn_gamma1, L2_gnn_beta1, L2_gnn_We2, L2_gnn_be2, L2_gnn_Wm2, L2_gnn_bm2, L2_gnn_eps2, L2_gnn_gamma2, L2_gnn_beta2), axis=-1)
    x = _layernorm(x + _L3_gnn_ref(x, node_vec, src, dst, L3_gnn_Wq, L3_gnn_bq, L3_gnn_Wk, L3_gnn_bk, L3_gnn_Wv, L3_gnn_bv, L3_gnn_Wo, L3_gnn_bo), axis=-1)
    return x

_drawn_inputs = setup_inputs


def setup_inputs(seed=0):
    import zlib

    import numpy as np

    out = dict(_drawn_inputs(seed))
    spreads = {'L0_gnn_b0': (0.0, 0.387),
     'L0_gnn_b1': (0.0, 0.1),
     'L0_gnn_b2': (0.0, 0.1),
     'L0_gnn_ln_g': (1.0, 0.2),
     'L0_gnn_ln_b': (0.0, 0.1),
     'L1_gnn_b1_l': (0.0, 0.1),
     'L1_gnn_b2_l': (0.0, 0.1),
     'L2_gnn_be1': (0.0, 0.1),
     'L2_gnn_bm1': (0.0, 0.1),
     'L2_gnn_gamma1': (1.0, 0.2),
     'L2_gnn_beta1': (0.0, 0.1),
     'L2_gnn_be2': (0.0, 0.342),
     'L2_gnn_bm2': (0.0, 0.1),
     'L2_gnn_gamma2': (1.0, 0.2),
     'L2_gnn_beta2': (0.0, 0.1),
     'L3_gnn_bq': (0.0, 0.537),
     'L3_gnn_bk': (0.0, 0.8),
     'L3_gnn_bv': (0.0, 0.1),
     'L3_gnn_bo': (0.0, 0.1)}
    factors = {}
    for name, (base, spread) in spreads.items():
        noise = np.random.default_rng([zlib.crc32(name.encode()), seed]).standard_normal(out[name].shape)
        drawn = base * np.exp(spread * noise) if base else spread * noise
        out[name] = jnp.asarray(drawn.astype(out[name].dtype))
    for name, factor in factors.items():
        out[name] = (out[name] * factor).astype(out[name].dtype)
    return out
```

```python
from contextlib import ExitStack

import concourse.bass as bass
from concourse import mybir

F32 = mybir.dt.float32
BF16 = mybir.dt.bfloat16
I32 = mybir.dt.int32
ALU = mybir.AluOpType
ACT = mybir.ActivationFunctionType
AX = mybir.AxisListType

P = 128
N = 12500
D = 64
E = 212500
NT = -(-N // P)
NPAD = NT * P
TILES = -(-E // (P * 8)) * 8
LASTROW = E - (P - 1) * TILES
LO = 16


class List:

    def __init__(self, name, shift, fields):
        self.name, self.shift, self.width = name, shift, 1 << shift
        self.buckets = (NPAD >> shift) + 1
        self.hi = -(-self.buckets // LO)
        self.bins = self.hi * LO
        self.chunks = -(-(TILES + self.buckets) // 16) * 16
        self.jt = -(-self.chunks // P)
        self.fields = fields


BY_DST = List("dst", 7, 4)
BY_SRC = List("src", 5, 2)
LISTS = (BY_DST, BY_SRC)
J = 8
NG = 7
NGROUPS = NT // NG
LN_EPS = 1e-5
HEADS = 4
NO_SCORE = -1e30
NO_MAX = -1e29
ABSENT = 4096


class Count:

    def __init__(self, sem, start=0):
        self.sem, self.start, self.n = sem, start, 0

    def inc(self, ins):
        ins.then_inc(self.sem, 1)
        self.n += 1

    def wait(self, eng):
        eng.wait_ge(self.sem, self.start + self.n)


def sort_edges(nc, src, dst, tables, chunk_bucket, l_hist):
    with ExitStack() as ctx:
        def sb(name, shape, dt):
            return ctx.enter_context(nc.sbuf_tensor("sort_" + name, shape, dt))

        def ps(name, shape, dt=F32):
            return ctx.enter_context(nc.psum_tensor("sort_" + name, shape, dt))

        def sem(name):
            return ctx.enter_context(nc.semaphore("sort_" + name))

        node = {"dst": sb("dst", [P, TILES], I32), "src": sb("src", [P, TILES], I32)}
        other = {"dst": node["src"], "src": node["dst"]}
        bucket = {l.name: sb(l.name + "_bucket", [P, TILES], F32) for l in LISTS}
        row = {l.name: sb(l.name + "_row", [P, TILES, l.fields], I32) for l in LISTS}
        tmp = sb("tmp", [P, TILES], I32)
        HG = TILES // 16
        parts = {l.name: (sb(l.name + "_hi", [P, TILES], BF16), sb(l.name + "_lo", [P, TILES], BF16)) for l in LISTS}
        hot = {l.name: (sb(l.name + "_hothi", [P, HG, l.hi], BF16), sb(l.name + "_hotlo", [P, HG, LO], BF16)) for l in LISTS}
        iota_i = sb("iota_i", [P, 512], I32)
        iota_b = sb("iota_b", [P, 32], BF16)
        iota_f = sb("iota_f", [P, 512], F32)
        rowj = sb("rowj", [P, 32], F32)
        rowj_i = sb("rowj_i", [P, 32], I32)
        before = sb("before", [P, P], BF16)
        notbefore = sb("notbefore", [P, P], BF16)
        ones_row = sb("ones_row", [1, P], F32)
        hist = {l.name: ps(l.name + "_hist", [l.hi, LO]) for l in LISTS}
        hist_sb = {l.name: sb(l.name + "_histsb", [l.hi, LO], F32) for l in LISTS}
        line = {l.name: sb(l.name + "_line", [1, 6, l.bins], F32) for l in LISTS}
        line_i = {l.name: sb(l.name + "_linei", [1, l.bins], I32) for l in LISTS}
        rank = {l.name: ps(l.name + "_rank", [P, l.bins]) for l in LISTS}
        ends_ps = {l.name: ps(l.name + "_endsps", [P, l.bins]) for l in LISTS}
        ends = {l.name: sb(l.name + "_ends", [P, l.bins], F32) for l in LISTS}
        of_chunk = {l.name: sb(l.name + "_ofchunk", [P, l.jt], F32) for l in LISTS}
        of_chunk_i = {l.name: sb(l.name + "_ofchunki", [P, l.jt], I32) for l in LISTS}
        G = 8
        onehot = {l.name: sb(l.name + "_onehot", [P, 2, G, l.bins], BF16) for l in LISTS}
        prod = {l.name: sb(l.name + "_prod", [P, l.bins], F32) for l in LISTS}
        slot = {l.name: sb(l.name + "_slot", [P, G], F32) for l in LISTS}
        slot_i = {l.name: sb(l.name + "_sloti", [P, 3, G], I32) for l in LISTS}
        at = {l.name: [sb(f"{l.name}_at{k}", [P, G], I32) for k in range(2)] for l in LISTS}
        stage = {l.name: [sb(f"{l.name}_stage{k}", [P, G, l.fields], I32) for k in range(2)] for l in LISTS}
        empty = sb("empty", [P, max(l.chunks * l.fields for l in LISTS)], I32)
        cleared = sem("cleared")
        loaded = sem("loaded")
        consts = sem("consts")
        prep = sem("prep")
        hot_ready = sem("hot_ready")
        hot_used = sem("hot_used")
        hist_done = sem("hist_done")
        spilled = sem("spilled")
        line_in = sem("line_in")
        line_ready = sem("line_ready")
        filled = sem("filled")
        ends_done = sem("ends_done")
        table_ready = sem("table_ready")
        onehot_ready = sem("onehot_ready")
        rank_ready = {l.name: sem(l.name + "_rank_ready") for l in LISTS}
        rank_read = {l.name: sem(l.name + "_rank_read") for l in LISTS}
        tile_summed = sem("tile_summed")
        slot_step = sem("slot_step")
        scattered = [sem(f"scattered{k}") for k in range(2)]
        TABLE_STEPS = sum(2 + l.jt for l in LISTS) + 2
        CONSTS = 8
        LINE_STEPS = 8 * len(LISTS)
        SLOT_STEPS = 5 * len(LISTS)

        with nc.Block() as block:
            @block.sync
            def _(sp):
                sp.wait_ge(cleared, 2)
                for name, dram in (("dst", dst), ("src", src)):
                    sp.dma_start(node[name][0:P - 1, :], dram[0:(P - 1) * TILES].rearrange("(p t) -> p t", t=TILES)).then_inc(loaded, 16)
                    sp.dma_start(node[name][P - 1:P, 0:LASTROW], dram[(P - 1) * TILES:E].rearrange("(p t) -> p t", p=1)).then_inc(loaded, 16)

            @block.gpsimd
            def _(pool):
                c = Count(consts)
                c.inc(pool.iota(iota_i[:], [[1, 512]], base=0, channel_multiplier=0))
                c.inc(pool.iota(rowj_i[:], [[P, 32]], base=0, channel_multiplier=1))
                c.inc(pool.iota(tmp[:], [[1, TILES]], base=0, channel_multiplier=TILES))
                c.inc(pool.memset(before[:], 1.0))
                c.inc(pool.memset(notbefore[:], 1.0))
                c.wait(pool)
                c.inc(pool.affine_select(out=before[:], in_=before[:], compare_op=ALU.is_ge, fill=0.0, base=-1, pattern=[[1, P]], channel_multiplier=-1))
                c.inc(pool.affine_select(out=notbefore[:], in_=notbefore[:], compare_op=ALU.is_ge, fill=0.0, base=0, pattern=[[-1, P]], channel_multiplier=1))
                c.inc(pool.memset(ones_row[:], 1.0))

            @block.vector
            def _(dve):
                for name in ("dst", "src"):
                    dve.memset(node[name][:], NPAD).then_inc(cleared, 1)
                dve.wait_ge(consts, 3)
                p = Count(prep)
                p.inc(dve.tensor_copy(iota_b[:], iota_i[:, 0:32]))
                p.inc(dve.tensor_copy(iota_f[:], iota_i[:]))
                p.inc(dve.tensor_copy(rowj[:], rowj_i[:]))
                p.inc(dve.memset(row["dst"][:, :, 3:4], 0))
                p.inc(dve.tensor_scalar(row["dst"][:, :, 2:3], tmp[:].unsqueeze(2), E - 1, None, ALU.min))
                dve.wait_ge(loaded, 64)
                p.wait(dve)
                for l in LISTS:
                    key, oth, w = node[l.name], other[l.name], row[l.name]
                    p.inc(dve.tensor_scalar(w[:, :, 0:1], oth[:].unsqueeze(2), N - 1, None, ALU.min))
                    p.inc(dve.tensor_scalar(w[:, :, 1:2], key[:].unsqueeze(2), l.width - 1, None, ALU.bitwise_and))
                    p.inc(dve.tensor_scalar(tmp[:], key[:], l.shift, None, ALU.logical_shift_right))
                    p.wait(dve)
                    p.inc(dve.tensor_copy(bucket[l.name][:], tmp[:]))
                    p.wait(dve)
                    p.inc(dve.tensor_scalar(tmp[:], tmp[:], LO - 1, None, ALU.bitwise_and))
                    p.wait(dve)
                    p.inc(dve.tensor_copy(parts[l.name][1][:], tmp[:]))
                    p.wait(dve)
                    p.inc(dve.tensor_scalar(tmp[:], key[:], l.shift + 4, None, ALU.logical_shift_right))
                    p.wait(dve)
                    p.inc(dve.tensor_copy(parts[l.name][0][:], tmp[:]))
                    p.wait(dve)
                def count_onehots(i):
                    for l in LISTS:
                        for part, width, hot_part in ((parts[l.name][0], l.hi, hot[l.name][0]), (parts[l.name][1], LO, hot[l.name][1])):
                            dve.tensor_tensor(hot_part[:], part[:, bass.ds(i * HG, HG)].unsqueeze(2).broadcast_to([P, HG, width]),
                                              iota_b[:, 0:width].unsqueeze(1).broadcast_to([P, HG, width]), ALU.is_equal).then_inc(hot_ready, 1)

                count_onehots(0)
                with dve.Fori(1, 16) as i:
                    dve.wait_ge(hot_used, i * (2 * HG))
                    count_onehots(i)
                dve.wait_ge(hot_used, 2 * TILES)
                for l in LISTS:
                    dve.tensor_copy(hist_sb[l.name][:], hist[l.name][:]).then_inc(hist_done, 1)

                dve.wait_ge(line_in, 32)
                p = Count(line_ready)
                for l in LISTS:
                    ln = line[l.name]
                    p.inc(dve.tensor_copy(line_i[l.name][:], ln[:, 0, :]))
                    p.wait(dve)
                    p.inc(dve.tensor_scalar(line_i[l.name][:], line_i[l.name][:], P - 1, None, ALU.add))
                    p.wait(dve)
                    p.inc(dve.tensor_scalar(line_i[l.name][:], line_i[l.name][:], 7, None, ALU.logical_shift_right))
                    p.wait(dve)
                    p.inc(dve.tensor_copy(ln[:, 1, :], line_i[l.name][:]))
                    p.inc(dve.memset(ln[:, 4, :], 0.0))
                    p.wait(dve)
                    p.inc(dve.tensor_tensor_scan(ln[:, 2, :], ln[:, 1, :], ln[:, 4, :], 0.0, ALU.add, ALU.add))
                    p.wait(dve)
                    p.inc(dve.tensor_tensor(ln[:, 3, :], ln[:, 2, :], ln[:, 1, :], ALU.subtract))
                    p.wait(dve)
                    p.inc(dve.tensor_scalar(ln[:, 3, :], ln[:, 3, :], float(P), None, ALU.mult))
                dve.wait_ge(ends_done, 2)
                q = Count(table_ready)
                for l in LISTS:
                    q.inc(dve.tensor_copy(ends[l.name][:], ends_ps[l.name][:]))
                    q.wait(dve)
                    for j in range(l.jt):
                        q.inc(dve.tensor_scalar(prod[l.name][:], ends[l.name][:], rowj[:, j:j + 1], 0.0, ALU.is_le, ALU.add, accum_out=of_chunk[l.name][:, j:j + 1]))
                        q.wait(dve)
                    q.inc(dve.tensor_scalar(of_chunk_i[l.name][:], of_chunk[l.name][:], float(l.buckets - 1), None, ALU.min))
                empty_v = empty[:].rearrange("p (c f) -> p c f", f=2)
                q.inc(dve.memset(empty[:], 0))
                q.wait(dve)
                q.inc(dve.memset(empty_v[:, :, 1:2], ABSENT))
                assert q.n == TABLE_STEPS, q.n

                def rank_onehots(i, k):
                    for l in LISTS:
                        dve.tensor_tensor(onehot[l.name][:, k], bucket[l.name][:, bass.ds(i * G, G)].unsqueeze(2).broadcast_to([P, G, l.bins]),
                                          iota_f[:, 0:l.bins].unsqueeze(1).broadcast_to([P, G, l.bins]), ALU.is_equal).then_inc(onehot_ready, 1)

                def rank_group(i, k):
                    steps = Count(slot_step, i * SLOT_STEPS)
                    for t in range(G):
                        for l in LISTS:
                            dve.wait_ge(rank_ready[l.name], i * G + t + 1)
                            dve.tensor_tensor_reduce(prod[l.name][:], onehot[l.name][:, k, t, :], rank[l.name][:], 1.0, 0.0, ALU.mult, ALU.add,
                                                     slot[l.name][:, t:t + 1]).then_inc(rank_read[l.name], 1)
                    for l in LISTS:
                        si = slot_i[l.name]
                        dve.wait_ge(rank_read[l.name], i * G + G)
                        steps.inc(dve.tensor_copy(si[:, 0, :], slot[l.name][:]))
                        steps.wait(dve)
                        steps.inc(dve.tensor_scalar(si[:, 1, :], si[:, 0, :], P - 1, None, ALU.bitwise_and))
                        steps.inc(dve.tensor_scalar(si[:, 2, :], si[:, 0, :], 7, None, ALU.logical_shift_right))
                        steps.wait(dve)
                        steps.inc(dve.scalar_tensor_tensor(at[l.name][k][:], si[:, 1, :], float(l.chunks), si[:, 2, :], ALU.mult, ALU.add))
                        steps.wait(dve)
                        steps.inc(dve.tensor_copy(stage[l.name][k][:], row[l.name][:, bass.ds(i * G, G), :]))
                    assert steps.n == SLOT_STEPS

                GROUPS = TILES // G
                rank_onehots(0, 0)
                rank_onehots(1, 1)
                rank_group(0, 0)
                dve.wait_ge(tile_summed, 2 * G)
                rank_onehots(2, 0)
                rank_group(1, 1)
                with dve.Fori(2, GROUPS - 2, 2) as i:
                    for k in range(2):
                        dve.wait_ge(tile_summed, (i + k) * 2 * G)
                        rank_onehots(i + k + 1, 1 - k)
                        dve.wait_ge(scattered[k], (i * 8) * 2 * G)
                        rank_group(i + k, k)
                for k in range(2):
                    i = GROUPS - 2 + k
                    if k == 0:
                        dve.wait_ge(tile_summed, i * 2 * G)
                        rank_onehots(i + 1, 1)
                    dve.wait_ge(scattered[k], (GROUPS - 2) * 8 * 2 * G)
                    rank_group(i, k)

            @block.tensor
            def _(pe):
                def count_tile(t, first):
                    for l in LISTS:
                        h, w = hot[l.name]
                        pe.matmul(hist[l.name][:], h[:, t, :], w[:, t, :], start=first, stop=False, skip_group_check=True).then_inc(hot_used, 1)

                def count_rest():
                    with pe.Fori(1, HG) as t:
                        for l in LISTS:
                            h, w = hot[l.name]
                            pe.matmul(hist[l.name][:], h[:, bass.ds(t, 1), :].squeeze(1), w[:, bass.ds(t, 1), :].squeeze(1), start=False, stop=False, skip_group_check=True).then_inc(hot_used, 1)

                pe.wait_ge(hot_ready, 4)
                count_tile(0, True)
                count_rest()
                with pe.Fori(1, 16) as i:
                    pe.wait_ge(hot_ready, i * 4 + 4)
                    count_tile(0, False)
                    count_rest()

                pe.wait_ge(consts, CONSTS)
                pe.wait_ge(line_ready, LINE_STEPS)
                for l in LISTS:
                    pe.matmul(ends_ps[l.name][:], ones_row[:], line[l.name][:, 2, :], start=True, stop=True).then_inc(ends_done, 1)
                for l in LISTS:
                    pe.matmul(rank[l.name][:], ones_row[:], line[l.name][:, 3, :], start=True, stop=False, skip_group_check=True)

                def rank_group(i, k, first=False):
                    pe.wait_ge(onehot_ready, i * 2 + 2)
                    for t in range(G):
                        for l in LISTS:
                            hot_t = onehot[l.name][:, k, t, :]
                            pe.matmul(rank[l.name][:], before[:], hot_t, start=False, stop=False, skip_group_check=True).then_inc(rank_ready[l.name], 1)
                        for l in LISTS:
                            hot_t = onehot[l.name][:, k, t, :]
                            pe.wait_ge(rank_read[l.name], i * G + t + 1)
                            pe.matmul(rank[l.name][:], notbefore[:], hot_t, start=False, stop=False, skip_group_check=True).then_inc(tile_summed, 1)

                with pe.Fori(0, TILES // G, 2) as i:
                    rank_group(i, 0)
                    rank_group(i + 1, 1)

            @block.sync
            def _(sp):
                sp.wait_ge(hist_done, 2)
                for l in LISTS:
                    sp.dma_start(l_hist[l.name], hist_sb[l.name][:]).then_inc(spilled, 16)
                sp.wait_ge(spilled, 32)
                for l in LISTS:
                    sp.dma_start(line[l.name][:, 0, :], l_hist[l.name].rearrange("h l -> (h l)").unsqueeze(0)).then_inc(line_in, 16)
                sp.wait_ge(table_ready, TABLE_STEPS)
                for l in LISTS:
                    sp.dma_start(tables[l.name].rearrange("(p c) f -> p (c f)", p=P), empty[:, 0:l.chunks * l.fields]).then_inc(filled, 16)
                    sp.dma_start(chunk_bucket[l.name].rearrange("(j p) -> p j", p=P), of_chunk_i[l.name][:], allow_slow_non_contiguous=True).then_inc(filled, 16)

            @block.gpsimd
            def _(pool):
                pool.wait_ge(filled, 64)

                def scatter_group(i, k):
                    pool.wait_ge(slot_step, i * SLOT_STEPS + SLOT_STEPS)
                    pool.nop(nofuse=True)
                    for t in range(G):
                        for l in LISTS:
                            pool.indirect_dma_start(tables[l.name], bass.IndirectOffsetOnAxis(ap=at[l.name][k][:, t:t + 1], axis=0),
                                                    stage[l.name][k][:, t, :], None).then_inc(scattered[k], 16)

                with pool.Fori(0, TILES // G, 2) as i:
                    scatter_group(i, 0)
                    scatter_group(i + 1, 1)
                for k in range(2):
                    pool.wait_ge(scattered[k], TILES // G * 8 * 2 * G)


WEIGHTS = [
    ("L0_gnn_W0", (2 * D, 128)), ("L0_gnn_b0", (128,)), ("L0_gnn_W1", (128, 128)), ("L0_gnn_b1", (128,)),
    ("L0_gnn_W2", (128, D)), ("L0_gnn_b2", (D,)), ("L0_gnn_ln_g", (D,)), ("L0_gnn_ln_b", (D,)),
    ("L1_gnn_W1_l", (D, D)), ("L1_gnn_b1_l", (D,)), ("L1_gnn_W1_r", (D, D)),
    ("L1_gnn_W2_l", (D, D)), ("L1_gnn_b2_l", (D,)), ("L1_gnn_W2_r", (D, D)),
    ("L2_gnn_We2", (D, D)), ("L2_gnn_be2", (D,)), ("L2_gnn_Wm2", (D, D)), ("L2_gnn_bm2", (D,)),
    ("L2_gnn_eps2", (1,)), ("L2_gnn_gamma2", (D,)), ("L2_gnn_beta2", (D,)),
    ("L3_gnn_Wq", (D, 256)), ("L3_gnn_bq", (256,)), ("L3_gnn_Wk", (D, 256)), ("L3_gnn_bk", (256,)),
    ("L3_gnn_Wv", (D, 256)), ("L3_gnn_bv", (256,)), ("L3_gnn_Wo", (256, D)), ("L3_gnn_bo", (D,)),
]
ROWS = ("L0_gnn_b2", "L0_gnn_ln_g", "L0_gnn_ln_b", "L1_gnn_b1_l", "L1_gnn_b2_l", "L2_gnn_gamma2", "L2_gnn_beta2", "L3_gnn_bo")


def load_shared(nc, keep, by_dst, a, tables, chunk_bucket):
    s = {}

    def sb(name, shape, dt=F32, stack=keep):
        s[name] = stack.enter_context(nc.sbuf_tensor(name, shape, dt))

    with ExitStack() as ctx:
        loaded = ctx.enter_context(nc.semaphore("shared_loaded"))
        cleared = ctx.enter_context(nc.semaphore("shared_cleared"))
        made = ctx.enter_context(nc.semaphore("shared_made"))
        transposed = ctx.enter_context(nc.semaphore("shared_transposed"))
        sb("X", [P, NT, D])
        sb("W0", [2 * D, 128])
        sb("W1", [128, 128])
        sb("W2", [128, D])
        sb("b0", [128, 1])
        sb("b1", [128, 1])
        sb("sage1", [2 * D, D])
        sb("sage2", [2 * D, D])
        sb("We", [D + 1, D])
        sb("Wm", [D + 1, D])
        sb("eps", [P, 1])
        sb("rows", [P, len(ROWS), D])
        sb("ident", [P, P])
        sb("ones", [P, P])
        sb("iota_row", [P, P])
        sb("Wq", [D + 1, HEADS * D])
        sb("Wk", [D + 1, HEADS * D])
        sb("Wv", [D + 1, HEADS * D])
        sb("Wo", [D, HEADS, D])
        sb("WkT", [D, HEADS, D + 1])
        sb("influence", [P, NT])
        sb("ln_eps", [P, 1])
        sb("acc", [P, BY_DST.buckets, D + 1], stack=by_dst)
        sb("src_index", [P, BY_DST.chunks], I32, stack=by_dst)
        sb("edge_index", [P, BY_DST.chunks], I32, stack=by_dst)
        sb("dst_local", [P, BY_DST.chunks], stack=by_dst)
        sb("dst_bucket", [1, BY_DST.jt * P], I32, stack=by_dst)
        table = ctx.enter_context(nc.sbuf_tensor("shared_table", [P, BY_DST.chunks, BY_DST.fields], I32))
        iota_i = ctx.enter_context(nc.sbuf_tensor("shared_iota", [P, P], I32))
        raw = ctx.enter_context(nc.sbuf_tensor("shared_raw", [D, 4, D], F32))
        flip = [ctx.enter_context(nc.psum_tensor(f"shared_flip{i}", [D, 512], F32)) for i in range(4)]
        flip_k = ctx.enter_context(nc.psum_tensor("shared_flipk", [D, 512], F32))
        last = N - (NT - 1) * P
        n_loads = 2 + 2 + 5 + 4 + 4 + 1 + len(ROWS) + 6 + 1 + 2
        with nc.Block() as block:
            @block.sync
            def _(sp):
                def load(to, frm, **how):
                    sp.dma_start(to, frm, **how).then_inc(loaded, 16)

                sp.wait_ge(cleared, 2)
                load(s["X"][:, 0:NT - 1, :], a["x"][0:(NT - 1) * P, :].rearrange("(t p) f -> p t f", p=P))
                load(s["X"][0:last, NT - 1, :], a["x"][(NT - 1) * P:N, :])
                load(table[:], tables["dst"].rearrange("(p c) f -> p c f", p=P))
                load(s["dst_bucket"][:], chunk_bucket["dst"].unsqueeze(0))
                load(s["W0"][:], a["L0_gnn_W0"])
                load(s["W1"][:], a["L0_gnn_W1"])
                load(s["W2"][:], a["L0_gnn_W2"])
                load(s["b0"][:], a["L0_gnn_b0"].unsqueeze(1))
                load(s["b1"][:], a["L0_gnn_b1"].unsqueeze(1))
                for w, m, b in (("We", "L2_gnn_We2", "L2_gnn_be2"), ("Wm", "L2_gnn_Wm2", "L2_gnn_bm2")):
                    load(s[w][0:D, :], a[m])
                    load(s[w][D:D + 1, :], a[b].unsqueeze(0))
                for i, w in enumerate(("L1_gnn_W1_l", "L1_gnn_W1_r", "L1_gnn_W2_l", "L1_gnn_W2_r")):
                    load(raw[:, i, :], a[w])
                load(s["eps"][:], a["L2_gnn_eps2"].unsqueeze(0).broadcast_to([P, 1]))
                for i, w in enumerate(ROWS):
                    load(s["rows"][:, i, :], a[w].unsqueeze(0).broadcast_to([P, D]))
                for w in "qkv":
                    load(s["W" + w][0:D, :], a["L3_gnn_W" + w])
                    load(s["W" + w][D:D + 1, :], a["L3_gnn_b" + w].unsqueeze(0))
                load(s["Wo"][:], a["L3_gnn_Wo"].rearrange("(h d) f -> d h f", d=D))
                load(s["influence"][:, 0:NT - 1], a["node_vec"][0:(NT - 1) * P].rearrange("(t p) -> p t", p=P), allow_slow_non_contiguous=True)
                load(s["influence"][0:last, NT - 1:NT], a["node_vec"][(NT - 1) * P:N].unsqueeze(1))
                sp.wait_ge(loaded, 16 * n_loads)

            @block.gpsimd
            def _(pool):
                c = Count(made)
                c.inc(pool.iota(iota_i[:], [[1, P]], base=0, channel_multiplier=0))
                c.inc(pool.memset(s["ones"][:], 1.0))
                c.wait(pool)
                c.inc(pool.affine_select(out=s["ident"][:], in_=s["ones"][:], compare_op=ALU.is_equal, fill=0.0, base=0,
                                         pattern=[[-1, P]], channel_multiplier=1))

            @block.tensor
            def _(pe):
                pe.wait_ge(made, 3)
                pe.wait_ge(loaded, 16 * n_loads)
                for i in range(4):
                    pe.transpose(flip[i][:, 0:D], raw[:, i, :], s["ident"][0:D, 0:D]).then_inc(transposed, 1)
                for h in range(HEADS):
                    pe.matmul(flip_k[:, h * 128:h * 128 + D + 1], s["Wk"][:, h * D:(h + 1) * D], s["ident"][0:D + 1, 0:D + 1], start=True, stop=True).then_inc(transposed, 1)

            @block.vector
            def _(dve):
                dve.memset(s["X"][:], 0.0).then_inc(cleared, 1)
                dve.memset(s["influence"][:], 0.0).then_inc(cleared, 1)
                dve.memset(s["ln_eps"][:], LN_EPS).then_inc(cleared, 1)
                dve.wait_ge(made, 3)
                dve.tensor_copy(s["iota_row"][:], iota_i[:]).then_inc(cleared, 1)
                dve.wait_ge(loaded, 16 * n_loads)
                dve.tensor_copy(s["src_index"][:], table[:, :, 0:1].squeeze(2)).then_inc(cleared, 1)
                dve.tensor_copy(s["dst_local"][:], table[:, :, 1:2].squeeze(2)).then_inc(cleared, 1)
                dve.tensor_copy(s["edge_index"][:], table[:, :, 2:3].squeeze(2)).then_inc(cleared, 1)
                dve.wait_ge(transposed, 4 + HEADS)
                for h in range(HEADS):
                    dve.tensor_copy(s["WkT"][:, h, :], flip_k[:, h * 128:h * 128 + D + 1]).then_inc(cleared, 1)
                for i in range(4):
                    dve.tensor_copy(s[("sage1", "sage2")[i // 2]][(i % 2) * D:(i % 2) * D + D, :], flip[i][:, 0:D]).then_inc(cleared, 1)
                dve.wait_ge(cleared, 11 + HEADS)
    return s


def gather_sum(nc, name, s, rows, index, counted, edge=None, ea=None):
    width = D + 1 if counted else D
    groups = BY_DST.chunks // J
    with ExitStack() as ctx:
        def sb(n, shape, dt=F32):
            return [ctx.enter_context(nc.sbuf_tensor(f"{name}_{n}{k}", shape, dt)) for k in range(2)]

        def ps(n, shape):
            return [ctx.enter_context(nc.psum_tensor(f"{name}_{n}{k}", shape, F32)) for k in range(2)]

        def sem(n):
            return ctx.enter_context(nc.semaphore(f"{name}_{n}"))

        idx = sb("idx", [P, J], I32)
        got = sb("got", [P, J, width])
        onehot = sb("onehot", [P, J, P])
        banks = 2 if counted else 1
        per_bank = J // banks
        total = ps("total", [P, banks, 512])
        idx_copied = sem("idx_copied")
        gathered = [sem(f"gathered{k}") for k in range(2)]
        onehot_ready = sem("onehot_ready")
        summed = sem("summed")
        added = sem("added")
        started = sem("started")
        if edge:
            flipped = ps("flipped", [D, 512])
            turned = sb("turned", [D + 1, J, P])
            product = ps("product", [P, J, D])
            made = sb("made", [P, J, D])
            flip_ready = sem("flip_ready")
            flip_used = sem("flip_used")
            product_ready = sem("product_ready")
            made_ready = sem("made_ready")
            ea_moved = [sem(f"ea_moved{k}") for k in range(2)]
        if edge == "message":
            attr = sb("attr", [P, J, D])

        def per_group(run):
            def go(eng):
                run(0, 0, True)
                run(1, 1, True)
                with eng.Fori(2, groups - 1, 2) as g:
                    run(g, 0, False)
                    run(g + 1, 1, False)
            return go

        def dma_count(g, k, n):
            return (g - k) * (8 * n) + 16 * n

        with nc.Block() as block:
            @block.gpsimd
            def _(pool):
                def group(g, k, first):
                    if not first:
                        pool.wait_ge(summed, g - 1)
                    pool.tensor_copy(idx[k][:], index[:, bass.ds(g * J, J)]).then_inc(idx_copied, 1)
                    pool.wait_ge(idx_copied, g + 1)
                    pool.nop(nofuse=True)
                    for t in range(J):
                        pool.indirect_dma_start(got[k][:, t, 0:D], None, rows, bass.IndirectOffsetOnAxis(ap=idx[k][:, t:t + 1], axis=0)).then_inc(gathered[k], 16)

                per_group(group)(pool)

            @block.tensor
            def _(pe):
                pe.wait_ge(started, 1 + 2 * counted + 2 * bool(edge))

                def group(g, k, first):
                    pe.wait_ge(gathered[k], dma_count(g, k, J))
                    if edge == "message":
                        pe.wait_ge(ea_moved[k], dma_count(g, k, 1))
                    if edge:
                        for h in range(2):
                            if not (first and k == 0):
                                pe.wait_ge(flip_used, 2 * g - 1 + h)
                            for t in range(4 * h, 4 * h + 4):
                                to = flipped[h][:, (t - 4 * h) * P:(t - 4 * h + 1) * P]
                                ins = pe.matmul(to, got[k][:, t, 0:D], s["ident"][:], start=True, stop=edge == "attr")
                                if edge == "message":
                                    ins = pe.matmul(to, attr[k][:, t, :], s["ident"][:], start=False, stop=True)
                            ins.then_inc(flip_ready, 1)
                        if not first:
                            pe.wait_ge(made_ready, g - 1)
                        for h in range(2):
                            pe.wait_ge(flip_used, 2 * g + 1 + h)
                            for t in range(4 * h, 4 * h + 4):
                                ins = pe.matmul(product[k][:, t, :], turned[k][:, t, :], s["We" if edge == "attr" else "Wm"][:], start=True, stop=True)
                        ins.then_inc(product_ready, 1)
                    pe.wait_ge(onehot_ready, g + 1)
                    if not first:
                        pe.wait_ge(added, J * (g - 1))
                    if edge == "message":
                        pe.wait_ge(made_ready, g + 1)
                    for t in range(J):
                        what = made[k][:, t, :] if edge == "message" else got[k][:, t, :]
                        at = (t % per_bank) * width
                        ins = pe.matmul(total[k][:, t // per_bank, at:at + width], onehot[k][:, t, :], what, start=True, stop=True)
                    ins.then_inc(summed, 1)

                per_group(group)(pe)

            @block.vector
            def _(dve):
                dve.memset(s["acc"][:], 0.0).then_inc(started, 1)
                if counted:
                    for k in range(2):
                        dve.memset(got[k][:, :, D:D + 1], 1.0).then_inc(started, 1)
                if edge:
                    for k in range(2):
                        dve.memset(turned[k][D:D + 1, :, :], 1.0).then_inc(started, 1)
                dve.wait_ge(started, 1 + 2 * counted + 2 * bool(edge))

                def compare(g, k):
                    dve.tensor_tensor(onehot[k][:], s["dst_local"][:, bass.ds(g * J, J)].unsqueeze(2).broadcast_to([P, J, P]),
                                      s["iota_row"][:].unsqueeze(1).broadcast_to([P, J, P]), ALU.is_equal).then_inc(onehot_ready, 1)

                def add(g, k):
                    buckets = [dve.value_load(s["dst_bucket"][0:1, bass.ds(g * J + t, 1)], min_val=0, max_val=BY_DST.buckets - 1) for t in range(J)]
                    dve.wait_ge(summed, g + 1)
                    for t in range(J):
                        if not (isinstance(g, int) and g == 0 and t == 0):
                            dve.wait_ge(added, g * J + t)
                        at = (t % per_bank) * width
                        to = s["acc"][:, bass.ds(buckets[t], 1), 0:width].squeeze(1)
                        dve.tensor_tensor(to, to, total[k][:, t // per_bank, at:at + width], ALU.add).then_inc(added, 1)

                def group(g, k, first):
                    if not first:
                        dve.wait_ge(summed, g - 1)
                    compare(g, k)
                    add(g, k)

                per_group(group)(dve)

            if edge:
                @block.scalar
                def _(act):
                    act.wait_ge(started, 1 + 2 * counted + 2)

                    def group(g, k, first):
                        for h in range(2):
                            act.wait_ge(flip_ready, 2 * g + 1 + h)
                            if not first and h == 0:
                                act.wait_ge(product_ready, g - 1)
                            act.activation(turned[k][0:D, 4 * h:4 * h + 4, :].rearrange("d t p -> d (t p)"), flipped[h][:],
                                           ACT.Copy if edge == "attr" else ACT.Relu).then_inc(flip_used, 1)
                        act.wait_ge(product_ready, g + 1)
                        if not first:
                            if edge == "attr":
                                act.wait_ge(ea_moved[k], dma_count(g - 2, k, 1))
                            else:
                                act.wait_ge(summed, g - 1)
                        act.activation(made[k][:], product[k][:], ACT.Silu).then_inc(made_ready, 1)

                    per_group(group)(act)

                @block.sync
                def _(sp):
                    def group(g, k, first):
                        there = ea[:, bass.ds(g * J, J), :]
                        if edge == "attr":
                            sp.wait_ge(made_ready, g + 1)
                            sp.dma_start(there, made[k][:]).then_inc(ea_moved[k], 16)
                        else:
                            if not first:
                                sp.wait_ge(flip_used, 2 * g - 2)
                            sp.dma_start(attr[k][:], there).then_inc(ea_moved[k], 16)

                    per_group(group)(sp)
                    if edge == "attr":
                        for k in range(2):
                            sp.wait_ge(ea_moved[k], groups // 2 * 16)


def row(s, name, n):
    return s["rows"][:, ROWS.index(name), :].unsqueeze(1).broadcast_to([P, n, D])


class Roots:

    def __init__(self, ctx, nc, name):
        self.asked = ctx.enter_context(nc.semaphore(name + "_var_ready"))
        self.given = ctx.enter_context(nc.semaphore(name + "_root_ready"))


NORM_STEPS = 6


def layer_norm(dve, c, v, sq, stat, out, roots, n_root):
    n = v.shape[1]
    c.wait(dve)
    c.inc(dve.tensor_reduce(stat[:, 0, :], v, AX.X, ALU.add))
    c.wait(dve)
    c.inc(dve.tensor_scalar(stat[:, 1, :], stat[:, 0, :], 1.0 / D, None, ALU.mult))
    c.wait(dve)
    c.inc(dve.tensor_tensor(v, v, stat[:, 1, :].unsqueeze(2).broadcast_to([P, n, D]), ALU.subtract))
    c.wait(dve)
    c.inc(dve.tensor_tensor(sq, v, v, ALU.mult))
    c.wait(dve)
    dve.tensor_reduce(stat[:, 2, :], sq, AX.X, ALU.add).then_inc(roots.asked, 1)
    dve.wait_ge(roots.given, n_root + 1)
    c.inc(dve.reciprocal(stat[:, 3, :], stat[:, 3, :]))
    c.wait(dve)
    c.inc(dve.tensor_tensor(out, v, stat[:, 3, :].unsqueeze(2).broadcast_to([P, n, D]), ALU.mult))


def norm_root(act, s, stat, roots, n_root):
    act.wait_ge(roots.asked, n_root + 1)
    act.activation(stat[:, 3, :], stat[:, 2, :], ACT.Sqrt, bias=s["ln_eps"][:, 0:1], scale=1.0 / D).then_inc(roots.given, 1)


def nodes(nc, name, s, kind, rows_out, H=None):
    SPLIT = ((0, 4), (4, NG))
    hidden = 2 if kind == "mlp" else 0
    with ExitStack() as ctx:
        def sb(n, shape, dt=F32):
            return ctx.enter_context(nc.sbuf_tensor(f"{name}_{n}", shape, dt))

        def ps(n, shape):
            return ctx.enter_context(nc.psum_tensor(f"{name}_{n}", shape, F32))

        def sem(n):
            return ctx.enter_context(nc.semaphore(f"{name}_{n}"))

        joined = sb("joined", [P, NG, 2 * D])
        flipped = ps("flipped", [P, 2, 512])
        act_in = [sb(f"in{n}", [P, NG, P]) for n in range(1 + hidden)]
        dense = [ps(f"dense{n}", [P, 2, 512]) for n in range(hidden)]
        y_ps = ps("y", [P, NG, D])
        v = sb("v", [P, NG, D])
        sq = sb("sq", [P, NG, D])
        stat = sb("stat", [P, 4, NG])
        count = sb("count", [P, NG])
        joined_ready = sem("joined_ready")
        dense_ready = sem("dense_ready")
        act_ready = sem("act_ready")
        y_ready = sem("y_ready")
        step = sem("step")
        stored = sem("stored")
        roots = Roots(ctx, nc, name)
        norms = {"mlp": 2, "sage1": 0, "sage2": 1}[kind]
        if kind == "mlp":
            STEPS, JOIN, weights = 6 + 2 * NORM_STEPS, 2, (s["W0"], s["W1"])
        elif kind == "sage1":
            STEPS, JOIN, weights = 6, 4, ()
        else:
            STEPS, JOIN, weights = 6 + NORM_STEPS, 4, ()

        with nc.Block() as block:
            @block.vector
            def _(dve):
                with dve.Fori(0, NGROUPS) as i:
                    c = Count(step, i * STEPS)
                    tiles = bass.ds(i * NG, NG)
                    if kind == "mlp":
                        c.inc(dve.tensor_copy(joined[:, :, 0:D], s["X"][:, tiles, :]))
                        c.inc(dve.tensor_copy(joined[:, :, D:], s["acc"][:, tiles, 0:D]))
                    else:
                        c.inc(dve.tensor_scalar(count[:], s["acc"][:, tiles, D:D + 1].squeeze(2), 1.0, None, ALU.max))
                        c.wait(dve)
                        c.inc(dve.reciprocal(count[:], count[:]))
                        c.wait(dve)
                        c.inc(dve.tensor_tensor(joined[:, :, 0:D], s["acc"][:, tiles, 0:D], count[:].unsqueeze(2).broadcast_to([P, NG, D]), ALU.mult))
                        c.inc(dve.tensor_copy(joined[:, :, D:], (s["X"] if kind == "sage1" else H)[:, tiles, :]))
                    dve.wait_ge(y_ready, i + 1)
                    if kind == "mlp":
                        c.inc(dve.tensor_tensor(v[:], y_ps[:], row(s, "L0_gnn_b2", NG), ALU.add))
                        layer_norm(dve, c, v[:], sq[:], stat, v[:], roots, i * 2)
                        c.wait(dve)
                        c.inc(dve.tensor_tensor(v[:], v[:], row(s, "L0_gnn_ln_g", NG), ALU.mult))
                        c.wait(dve)
                        c.inc(dve.tensor_tensor(v[:], v[:], row(s, "L0_gnn_ln_b", NG), ALU.add))
                        c.wait(dve)
                        c.inc(dve.scalar_tensor_tensor(v[:], s["X"][:, tiles, :], 2.0, v[:], ALU.mult, ALU.add))
                        layer_norm(dve, c, v[:], sq[:], stat, s["X"][:, tiles, :], roots, i * norms + norms - 1)
                    elif kind == "sage1":
                        c.inc(dve.tensor_tensor(v[:], y_ps[:], row(s, "L1_gnn_b1_l", NG), ALU.add))
                        c.wait(dve)
                        c.inc(dve.tensor_scalar(H[:, tiles, :], v[:], 0.0, None, ALU.max))
                    else:
                        c.inc(dve.tensor_tensor(v[:], y_ps[:], row(s, "L1_gnn_b2_l", NG), ALU.add))
                        c.wait(dve)
                        c.inc(dve.tensor_tensor(v[:], v[:], s["X"][:, tiles, :], ALU.add))
                        layer_norm(dve, c, v[:], sq[:], stat, s["X"][:, tiles, :], roots, i * norms + norms - 1)
                    assert c.n == STEPS, c.n

            @block.tensor
            def _(pe):
                with pe.Fori(0, NGROUPS) as i:
                    pe.wait_ge(step, i * STEPS + JOIN)
                    for b, (t0, t1) in enumerate(SPLIT):
                        for t in range(t0, t1):
                            ins = pe.matmul(flipped[:, b, (t - t0) * P:(t - t0 + 1) * P], joined[:, t, :], s["ident"][:], start=True, stop=True)
                    ins.then_inc(dense_ready, 1)
                    for n, w in enumerate(weights):
                        pe.wait_ge(act_ready, (i * (1 + hidden) + n) * 2 + 2)
                        for b, (t0, t1) in enumerate(SPLIT):
                            ins = pe.matmul(dense[n][:, b, 0:(t1 - t0) * P], w[:], act_in[n][:, t0:t1, :].rearrange("k t p -> k (t p)"), start=True, stop=True)
                        ins.then_inc(dense_ready, 1)
                    pe.wait_ge(act_ready, (i * (1 + hidden) + hidden) * 2 + 2)
                    w = s[{"mlp": "W2", "sage1": "sage1", "sage2": "sage2"}[kind]]
                    for t in range(NG):
                        ins = pe.matmul(y_ps[:, t, :], act_in[hidden][:, t, :], w[:], start=True, stop=True)
                    ins.then_inc(y_ready, 1)

            @block.scalar
            def _(act):
                with act.Fori(0, NGROUPS) as i:
                    for n in range(1 + hidden):
                        act.wait_ge(dense_ready, i * (1 + hidden) + n + 1)
                        frm = dense[n - 1] if n else flipped
                        for b, (t0, t1) in enumerate(SPLIT):
                            to = act_in[n][:, t0:t1, :].rearrange("k t p -> k (t p)")
                            if n:
                                ins = act.activation(to, frm[:, b, 0:(t1 - t0) * P], ACT.Relu, bias=s["b0" if n == 1 else "b1"][:, 0:1])
                            else:
                                ins = act.activation(to, frm[:, b, 0:(t1 - t0) * P], ACT.Copy)
                            ins.then_inc(act_ready, 1)
                    for r in range(norms):
                        norm_root(act, s, stat, roots, i * norms + r)

            @block.sync
            def _(sp):
                with sp.Fori(0, NGROUPS) as i:
                    sp.wait_ge(step, i * STEPS + STEPS)
                    sp.dma_start(rows_out.rearrange("(t p) f -> p t f", p=P)[:, bass.ds(i * NG, NG), :],
                                 (H if kind == "sage1" else s["X"])[:, bass.ds(i * NG, NG), :]).then_inc(stored, 16)
                sp.wait_ge(stored, NGROUPS * 16)


def graph_norm(nc, s, o, rows_out):
    with ExitStack() as ctx:
        def sb(n, shape, dt=F32):
            return ctx.enter_context(nc.sbuf_tensor(f"norm_{n}", shape, dt))

        def sem(n):
            return ctx.enter_context(nc.semaphore(f"norm_{n}"))

        sq = sb("sq", [P, NT, D])
        part = sb("part", [P, 2])
        st = sb("st", [P, 8])
        real = sb("real", [P, 1])
        stat = sb("stat", [P, 4, NT])
        tot = ctx.enter_context(nc.psum_tensor("norm_tot", [P, 2], F32))
        step = sem("step")
        masked = sem("masked")
        parts_ready = sem("parts_ready")
        tot_ready = sem("tot_ready")
        STEPS = 12 + NORM_STEPS
        stored = sem("stored")
        var_ready = sem("all_var_ready")
        root_ready = sem("all_root_ready")
        roots = Roots(ctx, nc, "norm")
        with nc.Block() as block:
            @block.scalar
            def _(act):
                act.wait_ge(var_ready, 1)
                act.activation(st[:, 5:6], st[:, 4:5], ACT.Sqrt, bias=s["ln_eps"][:, 0:1]).then_inc(root_ready, 1)
                norm_root(act, s, stat, roots, 0)

            @block.gpsimd
            def _(pool):
                pool.affine_select(out=real[:], in_=s["ones"][:, 0:1], compare_op=ALU.is_ge, fill=0.0, base=N - (NT - 1) * P - 1,
                                   pattern=[[0, 1]], channel_multiplier=-1).then_inc(masked, 1)

            @block.tensor
            def _(pe):
                pe.wait_ge(parts_ready, 2)
                pe.matmul(tot[:], s["ones"][:], part[:], start=True, stop=True).then_inc(tot_ready, 1)

            @block.vector
            def _(dve):
                c = Count(step)
                X, acc = s["X"], s["acc"][:, 0:NT, 0:D]
                c.inc(dve.tensor_scalar(st[:, 0:1], s["eps"][:], 1.0, None, ALU.add))
                c.wait(dve)
                c.inc(dve.scalar_tensor_tensor(o[:], X[:], st[:, 0:1], acc, ALU.mult, ALU.add))
                dve.wait_ge(masked, 1)
                c.wait(dve)
                c.inc(dve.tensor_scalar(o[:, NT - 1, :], o[:, NT - 1, :], real[:, 0:1], None, ALU.mult))
                c.wait(dve)
                dve.tensor_reduce(part[:, 0:1], o[:].rearrange("p t f -> p (t f)"), AX.X, ALU.add).then_inc(parts_ready, 1)
                c.inc(dve.tensor_tensor(sq[:], o[:], o[:], ALU.mult))
                c.wait(dve)
                dve.tensor_reduce(part[:, 1:2], sq[:].rearrange("p t f -> p (t f)"), AX.X, ALU.add).then_inc(parts_ready, 1)
                dve.wait_ge(tot_ready, 1)
                c.inc(dve.tensor_scalar(st[:, 1:3], tot[:], 1.0 / (N * D), None, ALU.mult))
                c.wait(dve)
                c.inc(dve.tensor_tensor(st[:, 3:4], st[:, 1:2], st[:, 1:2], ALU.mult))
                c.wait(dve)
                dve.tensor_tensor(st[:, 4:5], st[:, 2:3], st[:, 3:4], ALU.subtract).then_inc(var_ready, 1)
                dve.wait_ge(root_ready, 1)
                c.inc(dve.reciprocal(st[:, 5:6], st[:, 5:6]))
                c.wait(dve)
                c.inc(dve.tensor_scalar(o[:], o[:], st[:, 1:2], st[:, 5:6], ALU.subtract, ALU.mult))
                c.wait(dve)
                c.inc(dve.tensor_tensor(o[:], o[:], row(s, "L2_gnn_gamma2", NT), ALU.mult))
                c.wait(dve)
                c.inc(dve.tensor_tensor(o[:], o[:], row(s, "L2_gnn_beta2", NT), ALU.add))
                c.wait(dve)
                c.inc(dve.tensor_tensor(o[:], o[:], X[:], ALU.add))
                c.wait(dve)
                c.inc(dve.scalar_tensor_tensor(o[:], o[:], 0.0, X[:], ALU.max, ALU.add))
                layer_norm(dve, c, o[:], sq[:], stat, X[:], roots, 0)
                assert c.n == STEPS, c.n

            @block.sync
            def _(sp):
                sp.wait_ge(step, STEPS)
                sp.dma_start(rows_out.rearrange("(t p) f -> p t f", p=P), s["X"][:]).then_inc(stored, 16)
                sp.wait_ge(stored, 16)


def score_tables(nc, s, T):
    per_tile = P // BY_SRC.width
    SPLIT = ((0, 4), (4, NG))
    with ExitStack() as ctx:
        def sb(n, shape, dt=F32):
            return ctx.enter_context(nc.sbuf_tensor(f"keys_{n}", shape, dt))

        def ps(n, shape):
            return ctx.enter_context(nc.psum_tensor(f"keys_{n}", shape, F32))

        def sem(n):
            return ctx.enter_context(nc.semaphore(f"keys_{n}"))

        scale = sb("scale", [P, NT])
        xs = sb("xs", [P, NG, D + 1])
        xs_ps = ps("xs_ps", [D + 1, 2, 512])
        xsT = sb("xsT", [D + 1, NG, P])
        q_ps = ps("q_ps", [D, 2, 512])
        qT = sb("qT", [D, NG, P])
        t_ps = ps("t_ps", [D + 1, 2, 512])
        Tt = sb("Tt", [D + 1, NG * per_tile, HEADS, BY_SRC.width])
        zero = sb("zero", [D + 1, P])
        scaled = sem("scaled")
        xs_ready = sem("xs_ready")
        dense_ready = sem("dense_ready")
        act_ready = sem("act_ready")
        t_ready = sem("t_ready")
        t_copied = sem("t_copied")
        stored = sem("stored")
        K = 1 + HEADS
        with nc.Block() as block:
            @block.vector
            def _(dve):
                dve.tensor_scalar(scale[:], s["influence"][:], float(D) ** -0.5, None, ALU.mult).then_inc(scaled, 1)
                dve.memset(zero[:], 0.0).then_inc(scaled, 1)
                dve.wait_ge(scaled, 2)
                with dve.Fori(0, NGROUPS) as i:
                    tiles = bass.ds(i * NG, NG)
                    sc = scale[:, tiles].unsqueeze(2)
                    dve.tensor_tensor(xs[:, :, 0:D], s["X"][:, tiles, :], sc.broadcast_to([P, NG, D]), ALU.mult).then_inc(xs_ready, 1)
                    dve.tensor_copy(xs[:, :, D:D + 1], sc).then_inc(xs_ready, 1)
                    for h in range(HEADS):
                        dve.wait_ge(t_ready, i * HEADS + h + 1)
                        if h == 0:
                            dve.wait_ge(stored, i * 16 + 16)
                        for b, (t0, t1) in enumerate(SPLIT):
                            dve.tensor_copy(Tt[:, t0 * per_tile:t1 * per_tile, h, :],
                                            t_ps[:, b, 0:(t1 - t0) * P].rearrange("k (b n) -> k b n", n=BY_SRC.width)).then_inc(t_copied, 1)

            @block.tensor
            def _(pe):
                with pe.Fori(0, NGROUPS) as i:
                    pe.wait_ge(xs_ready, i * 2 + 2)
                    for b, (t0, t1) in enumerate(SPLIT):
                        for t in range(t0, t1):
                            ins = pe.matmul(xs_ps[:, b, (t - t0) * P:(t - t0 + 1) * P], xs[:, t, :], s["ident"][:], start=True, stop=True)
                    ins.then_inc(dense_ready, 1)
                    for h in range(HEADS):
                        pe.wait_ge(act_ready, (i * K + h) * 2 + 2)
                        for b, (t0, t1) in enumerate(SPLIT):
                            ins = pe.matmul(q_ps[:, b, 0:(t1 - t0) * P], s["Wq"][:, h * D:(h + 1) * D], xsT[:, t0:t1, :].rearrange("k t p -> k (t p)"), start=True, stop=True)
                        ins.then_inc(dense_ready, 1)
                        pe.wait_ge(act_ready, (i * K + h + 1) * 2 + 2)
                        if h:
                            pe.wait_ge(t_copied, (i * HEADS + h) * 2)
                        for b, (t0, t1) in enumerate(SPLIT):
                            ins = pe.matmul(t_ps[:, b, 0:(t1 - t0) * P], s["WkT"][:, h, :], qT[:, t0:t1, :].rearrange("k t p -> k (t p)"), start=True, stop=True)
                        ins.then_inc(t_ready, 1)

            @block.scalar
            def _(act):
                with act.Fori(0, NGROUPS) as i:
                    for n in range(K):
                        act.wait_ge(dense_ready, i * K + n + 1)
                        for b, (t0, t1) in enumerate(SPLIT):
                            to = (qT if n else xsT)[:, t0:t1, :].rearrange("k t p -> k (t p)")
                            if n > 1 and b == 0:
                                act.wait_ge(t_ready, i * HEADS + n - 1)
                            act.activation(to, (q_ps if n else xs_ps)[:, b, 0:(t1 - t0) * P], ACT.Copy).then_inc(act_ready, 1)

            @block.sync
            def _(sp):
                sp.wait_ge(scaled, 2)
                sp.dma_start(T[:, BY_SRC.buckets - 1, :], zero[:]).then_inc(stored, 16)
                with sp.Fori(0, NGROUPS) as i:
                    sp.wait_ge(t_copied, (i + 1) * HEADS * 2)
                    sp.dma_start(T[:, bass.ds(i * (NG * per_tile), NG * per_tile), :], Tt[:].rearrange("k b h n -> k b (h n)")).then_inc(stored, 16)
                sp.wait_ge(stored, (NGROUPS + 1) * 16)


def load_src_list(nc, keep, s, tables, chunk_bucket):
    def sb(name, shape, dt=F32):
        s[name] = keep.enter_context(nc.sbuf_tensor(name, shape, dt))

    sb("dst_index", [P, BY_SRC.chunks], I32)
    sb("src_local", [P, BY_SRC.chunks])
    sb("src_bucket", [1, BY_SRC.jt * P], I32)
    sb("U", [P, BY_SRC.buckets, D + 1])
    sb("M", [P, BY_SRC.buckets])
    with nc.sbuf_tensor("list_table", [P, BY_SRC.chunks, BY_SRC.fields], I32) as table, \
            nc.semaphore("list_loaded") as loaded, nc.semaphore("list_ready") as ready, nc.Block() as block:
        @block.sync
        def _(sp):
            sp.dma_start(table[:], tables["src"].rearrange("(p c) f -> p c f", p=P)).then_inc(loaded, 16)
            sp.dma_start(s["src_bucket"][:], chunk_bucket["src"].unsqueeze(0)).then_inc(loaded, 16)
            sp.wait_ge(loaded, 32)

        @block.vector
        def _(dve):
            dve.memset(s["U"][:], 0.0).then_inc(ready, 1)
            dve.memset(s["M"][:], NO_MAX).then_inc(ready, 1)
            dve.wait_ge(loaded, 32)
            dve.tensor_copy(s["dst_index"][:], table[:, :, 0:1].squeeze(2)).then_inc(ready, 1)
            dve.tensor_copy(s["src_local"][:], table[:, :, 1:2].squeeze(2)).then_inc(ready, 1)
            dve.wait_ge(ready, 4)


def attention(nc, s, rows, T):
    W = BY_SRC.width
    K = D + 1 + W
    groups = BY_SRC.chunks // J
    HALF = J // 2
    with ExitStack() as ctx:
        def sb1(n, shape, dt=F32):
            return ctx.enter_context(nc.sbuf_tensor(f"att_{n}", shape, dt))

        def sb(n, shape, dt=F32):
            return [sb1(f"{n}{k}", shape, dt) for k in range(2)]

        def ps(n):
            return ctx.enter_context(nc.psum_tensor(f"att_{n}", [P, 2, HALF, P], F32))

        def sem(n):
            return ctx.enter_context(nc.semaphore(f"att_{n}"))

        idx = sb("idx", [P, J], I32)
        got = sb("got", [P, J, K])
        Tt = sb("Tt", [K, J, P])
        turned = sb1("turned", [K, J, P])
        probs = sb1("probs", [P, J, P])
        probsT = sb1("probsT", [P, J, P])
        top = sb1("top", [P, J])
        before = sb1("before", [P, J])
        after = sb1("after", [P, J])
        minus = sb1("minus", [P, J])
        drop = sb1("drop", [P, J])
        keep = sb1("keep", [P, J])
        maskrow = sb1("maskrow", [W, HEADS, W])
        flipped, scores, flipped2, sums = ps("flipped"), ps("scores"), ps("flipped2"), ps("sums")
        started = sem("started")
        idx_copied = sem("idx_copied")
        gathered = [sem(f"gathered{k}") for k in range(2)]
        T_loaded = [sem(f"T_loaded{k}") for k in range(2)]
        masked = sem("masked")
        flip_ready = sem("flip_ready")
        turned_ready = sem("turned_ready")
        scores_ready = sem("scores_ready")
        step = sem("step")
        probs_ready = sem("probs_ready")
        keep_ready = sem("keep_ready")
        flip2_ready = sem("flip2_ready")
        probsT_ready = sem("probsT_ready")
        sums_ready = sem("sums_ready")
        added = sem("added")
        mask_set = sem("mask_set")
        STEPS = 2 + 3 * J + 2

        def per_group(eng, run):
            run(0, 0, True)
            run(1, 1, True)
            with eng.Fori(2, groups - 1, 2) as g:
                run(g, 0, False)
                run(g + 1, 1, False)

        def dma_count(g, k, n):
            return (g - k) * (8 * n) + 16 * n

        with nc.Block() as block:
            @block.gpsimd
            def _(pool):
                pool.memset(maskrow[:], 0.0).then_inc(mask_set, 1)
                pool.wait_ge(mask_set, 1)
                pool.affine_select(out=maskrow[:], in_=maskrow[:], compare_op=ALU.not_equal, fill=NO_SCORE, base=0,
                                   pattern=[[0, HEADS], [-1, W]], channel_multiplier=1).then_inc(mask_set, 1)

                def group(g, k, first):
                    if not first:
                        pool.wait_ge(sums_ready, g - 1)
                    pool.tensor_copy(idx[k][:], s["dst_index"][:, bass.ds(g * J, J)]).then_inc(idx_copied, 1)
                    pool.wait_ge(idx_copied, g + 1)
                    pool.nop(nofuse=True)
                    for t in range(J):
                        pool.indirect_dma_start(got[k][:, t, 0:D], None, rows, bass.IndirectOffsetOnAxis(ap=idx[k][:, t:t + 1], axis=0)).then_inc(gathered[k], 16)

                per_group(pool, group)

            @block.sync
            def _(sp):
                sp.wait_ge(mask_set, 2)
                for k in range(2):
                    for t in range(J):
                        sp.dma_start(Tt[k][D + 1:K, t, :], maskrow[:].rearrange("k h n -> k (h n)")).then_inc(started, 16)

                def group(g, k, first):
                    if not first:
                        sp.wait_ge(scores_ready, 2 * g - 2)
                    for t in range(J):
                        b = sp.value_load(s["src_bucket"][0:1, bass.ds(g * J + t, 1)], min_val=0, max_val=BY_SRC.buckets - 1)
                        sp.dma_start(Tt[k][0:D + 1, t, :], T[:, bass.ds(b, 1), :].squeeze(1)).then_inc(T_loaded[k], 16)

                per_group(sp, group)

            @block.tensor
            def _(pe):
                pe.wait_ge(started, 2 * J * 16 + 2)

                def group(g, k, first):
                    pe.wait_ge(gathered[k], dma_count(g, k, J))
                    pe.wait_ge(masked, g + 1)
                    for h in range(2):
                        if not (first and k == 0):
                            pe.wait_ge(turned_ready, 2 * g - 1 + h)
                        for t in range(h * HALF, (h + 1) * HALF):
                            ins = pe.matmul(flipped[0:K, h, t - h * HALF, :], got[k][:, t, :], s["ident"][:], start=True, stop=True)
                        ins.then_inc(flip_ready, 1)
                    pe.wait_ge(T_loaded[k], dma_count(g, k, J))
                    if not (first and k == 0):
                        pe.wait_ge(probs_ready, g * J)
                    for h in range(2):
                        pe.wait_ge(turned_ready, 2 * g + 1 + h)
                        for t in range(h * HALF, (h + 1) * HALF):
                            ins = pe.matmul(scores[:, h, t - h * HALF, :], Tt[k][:, t, :], turned[:, t, :], start=True, stop=True)
                        ins.then_inc(scores_ready, 1)
                    for h in range(2):
                        pe.wait_ge(probs_ready, g * J + (h + 1) * HALF)
                        for t in range(h * HALF, (h + 1) * HALF):
                            ins = pe.matmul(flipped2[:, h, t - h * HALF, :], probs[:, t, :], s["ident"][:], start=True, stop=True)
                        ins.then_inc(flip2_ready, 1)
                    if not (first and k == 0):
                        pe.wait_ge(added, g * J)
                    for h in range(2):
                        pe.wait_ge(probsT_ready, 2 * g + 1 + h)
                        for t in range(h * HALF, (h + 1) * HALF):
                            ins = pe.matmul(sums[:, h, t - h * HALF, 0:D + 1], probsT[:, t, :], got[k][:, t, 0:D + 1], start=True, stop=True)
                    ins.then_inc(sums_ready, 1)

                per_group(pe, group)

            @block.scalar
            def _(act):
                def group(g, k, first):
                    for h in range(2):
                        act.wait_ge(flip_ready, 2 * g + 1 + h)
                        if not (first and k == 0) and h == 0:
                            act.wait_ge(scores_ready, 2 * g)
                        act.activation(turned[:, h * HALF:(h + 1) * HALF, :], flipped[0:K, h], ACT.Copy).then_inc(turned_ready, 1)
                    act.wait_ge(step, g * STEPS + STEPS)
                    if not (first and k == 0):
                        act.wait_ge(flip2_ready, 2 * g)
                    for t in range(J):
                        act.activation(probs[:, t, :], scores[:, t // HALF, t % HALF, :], ACT.Exp, bias=minus[:, t:t + 1]).then_inc(probs_ready, 1)
                    if not (first and k == 0):
                        act.wait_ge(added, g * J)
                    act.activation(keep[:], drop[:], ACT.Exp).then_inc(keep_ready, 1)
                    for h in range(2):
                        act.wait_ge(flip2_ready, 2 * g + 1 + h)
                        if not (first and k == 0) and h == 0:
                            act.wait_ge(sums_ready, g)
                        act.activation(probsT[:, h * HALF:(h + 1) * HALF, :], flipped2[:, h], ACT.Copy).then_inc(probsT_ready, 1)

                per_group(act, group)

            @block.vector
            def _(dve):
                for k in range(2):
                    dve.memset(got[k][:, :, D:D + 1], 1.0).then_inc(started, 1)

                def group(g, k, first):
                    if not first:
                        dve.wait_ge(sums_ready, g - 1)
                    local = s["src_local"][:, bass.ds(g * J, J)].unsqueeze(2).broadcast_to([P, J, W])
                    dve.tensor_tensor(got[k][:, :, D + 1:K], local, s["iota_row"][:, 0:W].unsqueeze(1).broadcast_to([P, J, W]),
                                      ALU.not_equal).then_inc(masked, 1)
                    buckets = [dve.value_load(s["src_bucket"][0:1, bass.ds(g * J + t, 1)], min_val=0, max_val=BY_SRC.buckets - 1) for t in range(J)]
                    c = Count(step, g * STEPS)
                    if not (first and k == 0):
                        dve.wait_ge(keep_ready, g)
                    for h in range(2):
                        dve.wait_ge(scores_ready, 2 * g + 1 + h)
                        c.inc(dve.tensor_reduce(top[:, h * HALF:(h + 1) * HALF], scores[:, h], AX.X, ALU.max))
                    for t in range(J):
                        m = s["M"][:, bass.ds(buckets[t], 1)]
                        c.wait(dve)
                        c.inc(dve.tensor_tensor(before[:, t:t + 1], m, m, ALU.max))
                        c.inc(dve.tensor_tensor(after[:, t:t + 1], m, top[:, t:t + 1], ALU.max))
                        c.wait(dve)
                        c.inc(dve.tensor_tensor(m, after[:, t:t + 1], after[:, t:t + 1], ALU.max))
                    c.wait(dve)
                    c.inc(dve.tensor_scalar(minus[:], after[:], -1.0, None, ALU.mult))
                    c.inc(dve.tensor_tensor(drop[:], before[:], after[:], ALU.subtract))
                    assert c.n == STEPS, c.n
                    dve.wait_ge(keep_ready, g + 1)
                    dve.wait_ge(sums_ready, g + 1)
                    for t in range(J):
                        u = s["U"][:, bass.ds(buckets[t], 1), :].squeeze(1)
                        if not (first and k == 0 and t == 0):
                            dve.wait_ge(added, g * J + t)
                        dve.scalar_tensor_tensor(u, u, keep[:, t:t + 1], sums[:, t // HALF, t % HALF, 0:D + 1], ALU.mult, ALU.add).then_inc(added, 1)

                per_group(dve, group)


def attention_out(nc, s, out):
    B = P // BY_SRC.width
    last = N - (NT - 1) * P
    with ExitStack() as ctx:
        def sb(n, shape, dt=F32):
            return ctx.enter_context(nc.sbuf_tensor(f"fin_{n}", shape, dt))

        def ps(n, shape):
            return [ctx.enter_context(nc.psum_tensor(f"fin_{n}{k}", shape, F32)) for k in range(2)]

        def sem(n):
            return ctx.enter_context(nc.semaphore(f"fin_{n}"))

        inv = sb("inv", [P, NG * B])
        un = sb("un", [P, NG * B, D + 1])
        flipped = ps("flipped", [D + 1, B, HEADS, BY_SRC.width])
        uT = [sb(f"uT{k}", [D + 1, HEADS, B, BY_SRC.width]) for k in range(2)]
        o_ps = ps("o", [D, HEADS, P])
        oT = [sb(f"oT{k}", [D, HEADS, P]) for k in range(2)]
        y_ps = ctx.enter_context(nc.psum_tensor("fin_y", [P, NG, D], F32))
        v = sb("v", [P, NG, D])
        res = sb("res", [P, NG, D])
        sq = sb("sq", [P, NG, D])
        stat = sb("stat", [P, 4, NG])
        step = sem("step")
        flip_ready = sem("flip_ready")
        uT_ready = sem("uT_ready")
        o_ready = sem("o_ready")
        oT_ready = sem("oT_ready")
        y_ready = sem("y_ready")
        stored = sem("stored")
        roots = Roots(ctx, nc, "fin")
        DIV = 3
        STEPS = DIV + 2 + NORM_STEPS
        with nc.Block() as block:
            @block.vector
            def _(dve):
                def group(i):
                    c = Count(step, i * STEPS)
                    tiles = bass.ds(i * NG, NG)
                    u = s["U"][:, bass.ds(i * (NG * B), NG * B), :]
                    c.inc(dve.tensor_scalar(inv[:], u[:, :, D:D + 1].squeeze(2), 1e-10, None, ALU.add))
                    c.wait(dve)
                    c.inc(dve.reciprocal(inv[:], inv[:]))
                    c.wait(dve)
                    c.inc(dve.tensor_tensor(un[:], u, inv[:].unsqueeze(2).broadcast_to([P, NG * B, D + 1]), ALU.mult))
                    dve.wait_ge(y_ready, i + 1)
                    c.inc(dve.tensor_tensor(v[:], y_ps[:], row(s, "L3_gnn_bo", NG), ALU.add))
                    c.wait(dve)
                    c.inc(dve.tensor_tensor(v[:], v[:], s["X"][:, tiles, :], ALU.add))
                    if not isinstance(i, int):
                        dve.wait_ge(stored, i * 16)
                    layer_norm(dve, c, v[:], sq[:], stat, res[:], roots, i)
                    assert c.n == STEPS

                group(0)
                with dve.Fori(1, NGROUPS) as i:
                    group(i)

            @block.tensor
            def _(pe):
                with pe.Fori(0, NGROUPS) as i:
                    pe.wait_ge(step, i * STEPS + DIV)
                    for t in range(NG + 2):
                        if t < NG:
                            for b in range(B):
                                ins = pe.matmul(flipped[t % 2][:, b].rearrange("k h n -> k (h n)"), un[:, t * B + b, :], s["ident"][:], start=True, stop=True)
                            ins.then_inc(flip_ready, 1)
                        if 1 <= t < NG + 1:
                            n = t - 1
                            pe.wait_ge(uT_ready, i * NG + n + 1)
                            for h in range(HEADS):
                                ins = pe.matmul(o_ps[n % 2][:, h, :], s["Wv"][:, h * D:(h + 1) * D], uT[n % 2][:, h].rearrange("k b n -> k (b n)"), start=True, stop=True)
                            ins.then_inc(o_ready, 1)
                        if t >= 2:
                            n = t - 2
                            pe.wait_ge(oT_ready, i * NG + n + 1)
                            for h in range(HEADS):
                                ins = pe.matmul(y_ps[:, n, :], oT[n % 2][:, h, :], s["Wo"][:, h, :], start=(h == 0), stop=(h == HEADS - 1))
                    ins.then_inc(y_ready, 1)

            @block.scalar
            def _(act):
                with act.Fori(0, NGROUPS) as i:
                    for t in range(NG + 1):
                        if t < NG:
                            act.wait_ge(flip_ready, i * NG + t + 1)
                            act.activation(uT[t % 2][:].rearrange("k h b n -> k b h n"), flipped[t % 2][:], ACT.Copy).then_inc(uT_ready, 1)
                        if t >= 1:
                            act.wait_ge(o_ready, i * NG + t)
                            act.activation(oT[(t - 1) % 2][:], o_ps[(t - 1) % 2][:], ACT.Copy).then_inc(oT_ready, 1)
                    norm_root(act, s, stat, roots, i)

            @block.sync
            def _(sp):
                with sp.Fori(0, NGROUPS - 1) as i:
                    sp.wait_ge(step, i * STEPS + STEPS)
                    sp.dma_start(out[0:(NT - NG) * P, :].rearrange("(t p) f -> p t f", p=P)[:, bass.ds(i * NG, NG), :], res[:]).then_inc(stored, 16)
                sp.wait_ge(step, NGROUPS * STEPS)
                sp.dma_start(out[(NT - NG) * P:(NT - 1) * P, :].rearrange("(t p) f -> p t f", p=P), res[:, 0:NG - 1, :]).then_inc(stored, 16)
                sp.dma_start(out[(NT - 1) * P:N, :], res[0:last, NG - 1, :]).then_inc(stored, 16)
                sp.wait_ge(stored, (NGROUPS + 1) * 16)


def gnn(nc, a, out):
    def dram(name, shape, dt=F32):
        return nc.dram_tensor(name, shape, dt, kind="Internal").ap()

    tables = {l.name: dram(l.name + "_table", [P * l.chunks, l.fields], I32) for l in LISTS}
    chunk_bucket = {l.name: dram(l.name + "_chunk_bucket", [P * l.jt], I32) for l in LISTS}
    hist = {l.name: dram(l.name + "_hist", [l.hi, LO]) for l in LISTS}
    ea = dram("ea", [P, BY_DST.chunks, D])
    rows = [dram(f"rows{i}", [NPAD, D]) for i in range(4)]
    T = dram("T", [D + 1, BY_SRC.buckets, P])
    sort_edges(nc, a["src"], a["dst"], tables, chunk_bucket, hist)
    with ExitStack() as keep:
        with ExitStack() as by_dst:
            s = load_shared(nc, keep, by_dst, a, tables, chunk_bucket)
            H = by_dst.enter_context(nc.sbuf_tensor("H", [P, NT, D], F32))
            gather_sum(nc, "l0", s, a["edge_attr_64"], s["edge_index"], False, "attr", ea)
            nodes(nc, "n0", s, "mlp", rows[0])
            gather_sum(nc, "l1a", s, rows[0], s["src_index"], True)
            nodes(nc, "n1a", s, "sage1", rows[1], H)
            gather_sum(nc, "l1b", s, rows[1], s["src_index"], True)
            nodes(nc, "n1b", s, "sage2", rows[2], H)
            gather_sum(nc, "l2", s, rows[2], s["src_index"], False, "message", ea)
            graph_norm(nc, s, H, rows[3])
        score_tables(nc, s, T)
        load_src_list(nc, keep, s, tables, chunk_bucket)
        attention(nc, s, rows[3], T)
        attention_out(nc, s, out)


_INS = ["x", "src", "dst", "edge_attr_64", "node_vec"] + [n for n, _ in WEIGHTS]


def kernel(**inputs):
    import numpy as _np
    import concourse.bacc as _bacc
    from concourse import mybir as _mybir
    from concourse.bass_utils import run_bass_kernel_spmd as _run

    nc = _bacc.Bacc("TRN2", target_bir_lowering=False, num_devices=1)
    arrays, aps = {}, {}
    for name in _INS:
        a = _np.ascontiguousarray(inputs[name])
        arrays[f"in_{name}_dram"] = a
        aps[name] = nc.dram_tensor(f"in_{name}_dram", a.shape, _mybir.dt.from_np(a.dtype), kind="ExternalInput").ap()
    out = nc.dram_tensor("out_0_dram", (N, D), _mybir.dt.float32, kind="ExternalOutput").ap()
    gnn(nc, aps, out)
    r = _run(nc, [arrays], core_ids=[0])
    return r.results[0]["out_0_dram"]
```

```python
from contextlib import ExitStack

import concourse.bass as bass
from concourse import mybir

F32 = mybir.dt.float32
BF16 = mybir.dt.bfloat16
I32 = mybir.dt.int32
ALU = mybir.AluOpType
ACT = mybir.ActivationFunctionType
AX = mybir.AxisListType

P = 128
N = 12500
D = 64
E = 212500
NT = -(-N // P)
NPAD = NT * P
TILES = -(-E // (P * 8)) * 8
LASTROW = E - (P - 1) * TILES
LO = 16


class List:

    def __init__(self, name, shift, fields):
        self.name, self.shift, self.width = name, shift, 1 << shift
        self.buckets = (NPAD >> shift) + 1
        self.hi = -(-self.buckets // LO)
        self.bins = self.hi * LO
        self.chunks = -(-(TILES + self.buckets) // 32) * 32
        self.jt = -(-self.chunks // P)
        self.fields = fields


BY_DST = List("dst", 7, 4)
BY_SRC = List("src", 5, 2)
LISTS = (BY_DST, BY_SRC)
J = 8
NG = 7
NGROUPS = NT // NG
LN_EPS = 1e-5
HEADS = 4
NO_SCORE = -1e30
NO_MAX = -1e29
ABSENT = 4096


class Count:

    def __init__(self, sem, start=0):
        self.sem, self.start, self.n = sem, start, 0

    def inc(self, ins):
        ins.then_inc(self.sem, 1)
        self.n += 1

    def wait(self, eng):
        eng.wait_ge(self.sem, self.start + self.n)


def sort_edges(nc, src, dst, tables, chunk_bucket, l_hist):
    with ExitStack() as ctx:
        def sb(name, shape, dt):
            return ctx.enter_context(nc.sbuf_tensor("sort_" + name, shape, dt))

        def ps(name, shape, dt=F32):
            return ctx.enter_context(nc.psum_tensor("sort_" + name, shape, dt))

        def sem(name):
            return ctx.enter_context(nc.semaphore("sort_" + name))

        node = {"dst": sb("dst", [P, TILES], I32), "src": sb("src", [P, TILES], I32)}
        other = {"dst": node["src"], "src": node["dst"]}
        bucket = {l.name: sb(l.name + "_bucket", [P, TILES], F32) for l in LISTS}
        row = {l.name: sb(l.name + "_row", [P, TILES, l.fields], I32) for l in LISTS}
        tmp = sb("tmp", [P, TILES], I32)
        HG = TILES // 16
        HU = 8
        parts = {l.name: (sb(l.name + "_hi", [P, TILES], BF16), sb(l.name + "_lo", [P, TILES], BF16)) for l in LISTS}
        hot = {l.name: (sb(l.name + "_hothi", [P, HG, l.hi], BF16), sb(l.name + "_hotlo", [P, HG, LO], BF16)) for l in LISTS}
        iota_i = sb("iota_i", [P, 512], I32)
        iota_b = sb("iota_b", [P, 32], BF16)
        iota_f = sb("iota_f", [P, 512], F32)
        rowj = sb("rowj", [P, 32], F32)
        rowj_i = sb("rowj_i", [P, 32], I32)
        before = sb("before", [P, P], BF16)
        notbefore = sb("notbefore", [P, P], BF16)
        ones_row = sb("ones_row", [1, P], F32)
        hist = {l.name: ps(l.name + "_hist", [l.hi, LO]) for l in LISTS}
        hist_sb = {l.name: sb(l.name + "_histsb", [l.hi, LO], F32) for l in LISTS}
        line = {l.name: sb(l.name + "_line", [1, 6, l.bins], F32) for l in LISTS}
        line_i = {l.name: sb(l.name + "_linei", [1, l.bins], I32) for l in LISTS}
        rank = {l.name: ps(l.name + "_rank", [P, l.bins]) for l in LISTS}
        ends_ps = {l.name: ps(l.name + "_endsps", [P, l.bins]) for l in LISTS}
        ends = {l.name: sb(l.name + "_ends", [P, l.bins], F32) for l in LISTS}
        of_chunk = {l.name: sb(l.name + "_ofchunk", [P, l.jt], F32) for l in LISTS}
        of_chunk_i = {l.name: sb(l.name + "_ofchunki", [P, l.jt], I32) for l in LISTS}
        G = 8
        onehot = {l.name: sb(l.name + "_onehot", [P, 2, G, l.bins], BF16) for l in LISTS}
        prod = {l.name: sb(l.name + "_prod", [P, l.bins], F32) for l in LISTS}
        slot = {l.name: sb(l.name + "_slot", [P, G], F32) for l in LISTS}
        slot_i = {l.name: sb(l.name + "_sloti", [P, 3, G], I32) for l in LISTS}
        at = {l.name: [sb(f"{l.name}_at{k}", [P, G], I32) for k in range(2)] for l in LISTS}
        stage = {l.name: [sb(f"{l.name}_stage{k}", [P, G, l.fields], I32) for k in range(2)] for l in LISTS}
        empty = sb("empty", [P, max(l.chunks * l.fields for l in LISTS)], I32)
        cleared = sem("cleared")
        loaded = sem("loaded")
        consts = sem("consts")
        prep = sem("prep")
        hot_ready = sem("hot_ready")
        hot_used = sem("hot_used")
        hist_done = sem("hist_done")
        spilled = sem("spilled")
        line_in = sem("line_in")
        line_ready = sem("line_ready")
        filled = sem("filled")
        ends_done = sem("ends_done")
        table_ready = sem("table_ready")
        onehot_ready = sem("onehot_ready")
        rank_ready = {l.name: sem(l.name + "_rank_ready") for l in LISTS}
        rank_read = {l.name: sem(l.name + "_rank_read") for l in LISTS}
        tile_summed = sem("tile_summed")
        slot_step = sem("slot_step")
        scattered = [sem(f"scattered{k}") for k in range(2)]
        TABLE_STEPS = sum(2 + l.jt for l in LISTS) + 2
        CONSTS = 8
        LINE_STEPS = 8 * len(LISTS)
        SLOT_STEPS = 5 * len(LISTS)

        with nc.Block() as block:
            @block.sync
            def _(sp):
                sp.wait_ge(cleared, 2)
                for name, dram in (("dst", dst), ("src", src)):
                    sp.dma_start(node[name][0:P - 1, :], dram[0:(P - 1) * TILES].rearrange("(p t) -> p t", t=TILES)).then_inc(loaded, 16)
                    sp.dma_start(node[name][P - 1:P, 0:LASTROW], dram[(P - 1) * TILES:E].rearrange("(p t) -> p t", p=1)).then_inc(loaded, 16)

            @block.gpsimd
            def _(pool):
                c = Count(consts)
                c.inc(pool.iota(iota_i[:], [[1, 512]], base=0, channel_multiplier=0))
                c.inc(pool.iota(rowj_i[:], [[P, 32]], base=0, channel_multiplier=1))
                c.inc(pool.iota(tmp[:], [[1, TILES]], base=0, channel_multiplier=TILES))
                c.inc(pool.memset(before[:], 1.0))
                c.inc(pool.memset(notbefore[:], 1.0))
                c.wait(pool)
                c.inc(pool.affine_select(out=before[:], in_=before[:], compare_op=ALU.is_ge, fill=0.0, base=-1, pattern=[[1, P]], channel_multiplier=-1))
                c.inc(pool.affine_select(out=notbefore[:], in_=notbefore[:], compare_op=ALU.is_ge, fill=0.0, base=0, pattern=[[-1, P]], channel_multiplier=1))
                c.inc(pool.memset(ones_row[:], 1.0))

            @block.vector
            def _(dve):
                for name in ("dst", "src"):
                    dve.memset(node[name][:], NPAD).then_inc(cleared, 1)
                dve.wait_ge(consts, 3)
                p = Count(prep)
                p.inc(dve.tensor_copy(iota_b[:], iota_i[:, 0:32]))
                p.inc(dve.tensor_copy(iota_f[:], iota_i[:]))
                p.inc(dve.tensor_copy(rowj[:], rowj_i[:]))
                p.inc(dve.memset(row["dst"][:, :, 3:4], 0))
                p.inc(dve.tensor_scalar(row["dst"][:, :, 2:3], tmp[:].unsqueeze(2), E - 1, None, ALU.min))
                dve.wait_ge(loaded, 64)
                p.wait(dve)
                for l in LISTS:
                    key, oth, w = node[l.name], other[l.name], row[l.name]
                    p.inc(dve.tensor_scalar(w[:, :, 0:1], oth[:].unsqueeze(2), N - 1, None, ALU.min))
                    p.inc(dve.tensor_scalar(w[:, :, 1:2], key[:].unsqueeze(2), l.width - 1, None, ALU.bitwise_and))
                    p.inc(dve.tensor_scalar(tmp[:], key[:], l.shift, None, ALU.logical_shift_right))
                    p.wait(dve)
                    p.inc(dve.tensor_copy(bucket[l.name][:], tmp[:]))
                    p.wait(dve)
                    p.inc(dve.tensor_scalar(tmp[:], tmp[:], LO - 1, None, ALU.bitwise_and))
                    p.wait(dve)
                    p.inc(dve.tensor_copy(parts[l.name][1][:], tmp[:]))
                    p.wait(dve)
                    p.inc(dve.tensor_scalar(tmp[:], key[:], l.shift + 4, None, ALU.logical_shift_right))
                    p.wait(dve)
                    p.inc(dve.tensor_copy(parts[l.name][0][:], tmp[:]))
                    p.wait(dve)
                def count_onehots(i):
                    for l in LISTS:
                        for part, width, hot_part in ((parts[l.name][0], l.hi, hot[l.name][0]), (parts[l.name][1], LO, hot[l.name][1])):
                            dve.tensor_tensor(hot_part[:], part[:, bass.ds(i * HG, HG)].unsqueeze(2).broadcast_to([P, HG, width]),
                                              iota_b[:, 0:width].unsqueeze(1).broadcast_to([P, HG, width]), ALU.is_equal).then_inc(hot_ready, 1)

                count_onehots(0)
                with dve.Fori(1, 16) as i:
                    dve.wait_ge(hot_used, i * (2 * HG))
                    count_onehots(i)
                dve.wait_ge(hot_used, 2 * TILES)
                for l in LISTS:
                    dve.tensor_copy(hist_sb[l.name][:], hist[l.name][:]).then_inc(hist_done, 1)

                dve.wait_ge(line_in, 32)
                p = Count(line_ready)
                for l in LISTS:
                    ln = line[l.name]
                    p.inc(dve.tensor_copy(line_i[l.name][:], ln[:, 0, :]))
                    p.wait(dve)
                    p.inc(dve.tensor_scalar(line_i[l.name][:], line_i[l.name][:], P - 1, None, ALU.add))
                    p.wait(dve)
                    p.inc(dve.tensor_scalar(line_i[l.name][:], line_i[l.name][:], 7, None, ALU.logical_shift_right))
                    p.wait(dve)
                    p.inc(dve.tensor_copy(ln[:, 1, :], line_i[l.name][:]))
                    p.inc(dve.memset(ln[:, 4, :], 0.0))
                    p.wait(dve)
                    p.inc(dve.tensor_tensor_scan(ln[:, 2, :], ln[:, 1, :], ln[:, 4, :], 0.0, ALU.add, ALU.add))
                    p.wait(dve)
                    p.inc(dve.tensor_tensor(ln[:, 3, :], ln[:, 2, :], ln[:, 1, :], ALU.subtract))
                    p.wait(dve)
                    p.inc(dve.tensor_scalar(ln[:, 3, :], ln[:, 3, :], float(P), None, ALU.mult))
                dve.wait_ge(ends_done, 2)
                q = Count(table_ready)
                for l in LISTS:
                    q.inc(dve.tensor_copy(ends[l.name][:], ends_ps[l.name][:]))
                    q.wait(dve)
                    for j in range(l.jt):
                        q.inc(dve.tensor_scalar(prod[l.name][:], ends[l.name][:], rowj[:, j:j + 1], 0.0, ALU.is_le, ALU.add, accum_out=of_chunk[l.name][:, j:j + 1]))
                        q.wait(dve)
                    q.inc(dve.tensor_scalar(of_chunk_i[l.name][:], of_chunk[l.name][:], float(l.buckets - 1), None, ALU.min))
                empty_v = empty[:].rearrange("p (c f) -> p c f", f=2)
                q.inc(dve.memset(empty[:], 0))
                q.wait(dve)
                q.inc(dve.memset(empty_v[:, :, 1:2], ABSENT))
                assert q.n == TABLE_STEPS, q.n

                def rank_onehots(i, k):
                    for l in LISTS:
                        dve.tensor_tensor(onehot[l.name][:, k], bucket[l.name][:, bass.ds(i * G, G)].unsqueeze(2).broadcast_to([P, G, l.bins]),
                                          iota_f[:, 0:l.bins].unsqueeze(1).broadcast_to([P, G, l.bins]), ALU.is_equal).then_inc(onehot_ready, 1)

                def rank_group(i, k):
                    steps = Count(slot_step, i * SLOT_STEPS)
                    for t in range(G):
                        for l in LISTS:
                            dve.wait_ge(rank_ready[l.name], i * G + t + 1)
                            dve.tensor_tensor_reduce(prod[l.name][:], onehot[l.name][:, k, t, :], rank[l.name][:], 1.0, 0.0, ALU.mult, ALU.add,
                                                     slot[l.name][:, t:t + 1]).then_inc(rank_read[l.name], 1)
                    for l in LISTS:
                        si = slot_i[l.name]
                        dve.wait_ge(rank_read[l.name], i * G + G)
                        steps.inc(dve.tensor_copy(si[:, 0, :], slot[l.name][:]))
                        steps.wait(dve)
                        steps.inc(dve.tensor_scalar(si[:, 1, :], si[:, 0, :], P - 1, None, ALU.bitwise_and))
                        steps.inc(dve.tensor_scalar(si[:, 2, :], si[:, 0, :], 7, None, ALU.logical_shift_right))
                        steps.wait(dve)
                        steps.inc(dve.scalar_tensor_tensor(at[l.name][k][:], si[:, 1, :], float(l.chunks), si[:, 2, :], ALU.mult, ALU.add))
                        steps.wait(dve)
                        steps.inc(dve.tensor_copy(stage[l.name][k][:], row[l.name][:, bass.ds(i * G, G), :]))
                    assert steps.n == SLOT_STEPS

                GROUPS = TILES // G
                rank_onehots(0, 0)
                rank_onehots(1, 1)
                rank_group(0, 0)
                dve.wait_ge(tile_summed, 2 * G)
                rank_onehots(2, 0)
                rank_group(1, 1)
                with dve.Fori(2, GROUPS - 2, 2) as i:
                    for k in range(2):
                        dve.wait_ge(tile_summed, (i + k) * 2 * G)
                        rank_onehots(i + k + 1, 1 - k)
                        dve.wait_ge(scattered[k], (i * 8) * 2 * G)
                        rank_group(i + k, k)
                for k in range(2):
                    i = GROUPS - 2 + k
                    if k == 0:
                        dve.wait_ge(tile_summed, i * 2 * G)
                        rank_onehots(i + 1, 1)
                    dve.wait_ge(scattered[k], (GROUPS - 2) * 8 * 2 * G)
                    rank_group(i, k)

            @block.tensor
            def _(pe):
                def count_tile(t, first):
                    for l in LISTS:
                        h, w = hot[l.name]
                        pe.matmul(hist[l.name][:], h[:, t, :], w[:, t, :], start=first, stop=False, skip_group_check=True).then_inc(hot_used, 1)

                def count_rest():
                    for t in range(1, HU):
                        count_tile(t, False)
                    with pe.Fori(HU, HG - HU + 1, HU) as t:
                        for l in LISTS:
                            h, w = hot[l.name]
                            for j in range(HU):
                                ins = pe.matmul(hist[l.name][:], h[:, bass.ds(t + j, 1), :].squeeze(1), w[:, bass.ds(t + j, 1), :].squeeze(1), start=False, stop=False, skip_group_check=True)
                            ins.then_inc(hot_used, HU)

                pe.wait_ge(hot_ready, 4)
                count_tile(0, True)
                count_rest()
                with pe.Fori(1, 16) as i:
                    pe.wait_ge(hot_ready, i * 4 + 4)
                    count_tile(0, False)
                    count_rest()

                pe.wait_ge(consts, CONSTS)
                pe.wait_ge(line_ready, LINE_STEPS)
                for l in LISTS:
                    pe.matmul(ends_ps[l.name][:], ones_row[:], line[l.name][:, 2, :], start=True, stop=True).then_inc(ends_done, 1)
                for l in LISTS:
                    pe.matmul(rank[l.name][:], ones_row[:], line[l.name][:, 3, :], start=True, stop=False, skip_group_check=True)

                def rank_group(i, k, first=False):
                    pe.wait_ge(onehot_ready, i * 2 + 2)
                    for t in range(G):
                        for l in LISTS:
                            hot_t = onehot[l.name][:, k, t, :]
                            pe.matmul(rank[l.name][:], before[:], hot_t, start=False, stop=False, skip_group_check=True).then_inc(rank_ready[l.name], 1)
                        for l in LISTS:
                            hot_t = onehot[l.name][:, k, t, :]
                            pe.wait_ge(rank_read[l.name], i * G + t + 1)
                            pe.matmul(rank[l.name][:], notbefore[:], hot_t, start=False, stop=False, skip_group_check=True).then_inc(tile_summed, 1)

                with pe.Fori(0, TILES // G, 2) as i:
                    rank_group(i, 0)
                    rank_group(i + 1, 1)

            @block.sync
            def _(sp):
                sp.wait_ge(hist_done, 2)
                for l in LISTS:
                    sp.dma_start(l_hist[l.name], hist_sb[l.name][:]).then_inc(spilled, 16)
                sp.wait_ge(spilled, 32)
                for l in LISTS:
                    sp.dma_start(line[l.name][:, 0, :], l_hist[l.name].rearrange("h l -> (h l)").unsqueeze(0)).then_inc(line_in, 16)
                sp.wait_ge(table_ready, TABLE_STEPS)
                for l in LISTS:
                    sp.dma_start(tables[l.name].rearrange("(p c) f -> p (c f)", p=P), empty[:, 0:l.chunks * l.fields]).then_inc(filled, 16)
                    sp.dma_start(chunk_bucket[l.name].rearrange("(j p) -> p j", p=P), of_chunk_i[l.name][:], allow_slow_non_contiguous=True).then_inc(filled, 16)

            @block.gpsimd
            def _(pool):
                pool.wait_ge(filled, 64)

                def scatter_group(i, k):
                    pool.wait_ge(slot_step, i * SLOT_STEPS + SLOT_STEPS)
                    pool.nop(nofuse=True)
                    for t in range(G):
                        for l in LISTS:
                            pool.indirect_dma_start(tables[l.name], bass.IndirectOffsetOnAxis(ap=at[l.name][k][:, t:t + 1], axis=0),
                                                    stage[l.name][k][:, t, :], None).then_inc(scattered[k], 16)

                with pool.Fori(0, TILES // G, 2) as i:
                    scatter_group(i, 0)
                    scatter_group(i + 1, 1)
                for k in range(2):
                    pool.wait_ge(scattered[k], TILES // G * 8 * 2 * G)


WEIGHTS = [
    ("L0_gnn_W0", (2 * D, 128)), ("L0_gnn_b0", (128,)), ("L0_gnn_W1", (128, 128)), ("L0_gnn_b1", (128,)),
    ("L0_gnn_W2", (128, D)), ("L0_gnn_b2", (D,)), ("L0_gnn_ln_g", (D,)), ("L0_gnn_ln_b", (D,)),
    ("L1_gnn_W1_l", (D, D)), ("L1_gnn_b1_l", (D,)), ("L1_gnn_W1_r", (D, D)),
    ("L1_gnn_W2_l", (D, D)), ("L1_gnn_b2_l", (D,)), ("L1_gnn_W2_r", (D, D)),
    ("L2_gnn_We2", (D, D)), ("L2_gnn_be2", (D,)), ("L2_gnn_Wm2", (D, D)), ("L2_gnn_bm2", (D,)),
    ("L2_gnn_eps2", (1,)), ("L2_gnn_gamma2", (D,)), ("L2_gnn_beta2", (D,)),
    ("L3_gnn_Wq", (D, 256)), ("L3_gnn_bq", (256,)), ("L3_gnn_Wk", (D, 256)), ("L3_gnn_bk", (256,)),
    ("L3_gnn_Wv", (D, 256)), ("L3_gnn_bv", (256,)), ("L3_gnn_Wo", (256, D)), ("L3_gnn_bo", (D,)),
]
ROWS = ("L0_gnn_b2", "L0_gnn_ln_g", "L0_gnn_ln_b", "L1_gnn_b1_l", "L1_gnn_b2_l", "L2_gnn_gamma2", "L2_gnn_beta2", "L3_gnn_bo")


def load_shared(nc, keep, by_dst, a, tables, chunk_bucket):
    s = {}

    def sb(name, shape, dt=F32, stack=keep):
        s[name] = stack.enter_context(nc.sbuf_tensor(name, shape, dt))

    with ExitStack() as ctx:
        loaded = ctx.enter_context(nc.semaphore("shared_loaded"))
        cleared = ctx.enter_context(nc.semaphore("shared_cleared"))
        made = ctx.enter_context(nc.semaphore("shared_made"))
        transposed = ctx.enter_context(nc.semaphore("shared_transposed"))
        sb("X", [P, NT, D])
        sb("W0", [2 * D, 128])
        sb("W1", [128, 128])
        sb("W2", [128, D])
        sb("b0", [128, 1])
        sb("b1", [128, 1])
        sb("sage1", [2 * D, D])
        sb("sage2", [2 * D, D])
        sb("We", [D + 1, D])
        sb("Wm", [D + 1, D])
        sb("eps", [P, 1])
        sb("rows", [P, len(ROWS), D])
        sb("ident", [P, P])
        sb("ones", [P, P])
        sb("iota_row", [P, P])
        sb("Wq", [D + 1, HEADS * D])
        sb("Wk", [D + 1, HEADS * D])
        sb("Wv", [D + 1, HEADS * D])
        sb("Wo", [D, HEADS, D])
        sb("WkT", [D, HEADS, D + 1])
        sb("influence", [P, NT])
        sb("ln_eps", [P, 1])
        sb("acc", [P, BY_DST.buckets, D + 1], stack=by_dst)
        sb("src_index", [P, BY_DST.chunks], I32, stack=by_dst)
        sb("edge_index", [P, BY_DST.chunks], I32, stack=by_dst)
        sb("dst_local", [P, BY_DST.chunks], stack=by_dst)
        sb("dst_bucket", [1, BY_DST.jt * P], I32, stack=by_dst)
        table = ctx.enter_context(nc.sbuf_tensor("shared_table", [P, BY_DST.chunks, BY_DST.fields], I32))
        iota_i = ctx.enter_context(nc.sbuf_tensor("shared_iota", [P, P], I32))
        raw = ctx.enter_context(nc.sbuf_tensor("shared_raw", [D, 4, D], F32))
        flip = [ctx.enter_context(nc.psum_tensor(f"shared_flip{i}", [D, 512], F32)) for i in range(4)]
        flip_k = ctx.enter_context(nc.psum_tensor("shared_flipk", [D, 512], F32))
        last = N - (NT - 1) * P
        n_loads = 2 + 2 + 5 + 4 + 4 + 1 + len(ROWS) + 6 + 1 + 2
        with nc.Block() as block:
            @block.sync
            def _(sp):
                def load(to, frm, **how):
                    sp.dma_start(to, frm, **how).then_inc(loaded, 16)

                sp.wait_ge(cleared, 2)
                load(s["X"][:, 0:NT - 1, :], a["x"][0:(NT - 1) * P, :].rearrange("(t p) f -> p t f", p=P))
                load(s["X"][0:last, NT - 1, :], a["x"][(NT - 1) * P:N, :])
                load(table[:], tables["dst"].rearrange("(p c) f -> p c f", p=P))
                load(s["dst_bucket"][:], chunk_bucket["dst"].unsqueeze(0))
                load(s["W0"][:], a["L0_gnn_W0"])
                load(s["W1"][:], a["L0_gnn_W1"])
                load(s["W2"][:], a["L0_gnn_W2"])
                load(s["b0"][:], a["L0_gnn_b0"].unsqueeze(1))
                load(s["b1"][:], a["L0_gnn_b1"].unsqueeze(1))
                for w, m, b in (("We", "L2_gnn_We2", "L2_gnn_be2"), ("Wm", "L2_gnn_Wm2", "L2_gnn_bm2")):
                    load(s[w][0:D, :], a[m])
                    load(s[w][D:D + 1, :], a[b].unsqueeze(0))
                for i, w in enumerate(("L1_gnn_W1_l", "L1_gnn_W1_r", "L1_gnn_W2_l", "L1_gnn_W2_r")):
                    load(raw[:, i, :], a[w])
                load(s["eps"][:], a["L2_gnn_eps2"].unsqueeze(0).broadcast_to([P, 1]))
                for i, w in enumerate(ROWS):
                    load(s["rows"][:, i, :], a[w].unsqueeze(0).broadcast_to([P, D]))
                for w in "qkv":
                    load(s["W" + w][0:D, :], a["L3_gnn_W" + w])
                    load(s["W" + w][D:D + 1, :], a["L3_gnn_b" + w].unsqueeze(0))
                load(s["Wo"][:], a["L3_gnn_Wo"].rearrange("(h d) f -> d h f", d=D))
                load(s["influence"][:, 0:NT - 1], a["node_vec"][0:(NT - 1) * P].rearrange("(t p) -> p t", p=P), allow_slow_non_contiguous=True)
                load(s["influence"][0:last, NT - 1:NT], a["node_vec"][(NT - 1) * P:N].unsqueeze(1))
                sp.wait_ge(loaded, 16 * n_loads)

            @block.gpsimd
            def _(pool):
                c = Count(made)
                c.inc(pool.iota(iota_i[:], [[1, P]], base=0, channel_multiplier=0))
                c.inc(pool.memset(s["ones"][:], 1.0))
                c.wait(pool)
                c.inc(pool.affine_select(out=s["ident"][:], in_=s["ones"][:], compare_op=ALU.is_equal, fill=0.0, base=0,
                                         pattern=[[-1, P]], channel_multiplier=1))

            @block.tensor
            def _(pe):
                pe.wait_ge(made, 3)
                pe.wait_ge(loaded, 16 * n_loads)
                for i in range(4):
                    pe.transpose(flip[i][:, 0:D], raw[:, i, :], s["ident"][0:D, 0:D]).then_inc(transposed, 1)
                for h in range(HEADS):
                    pe.matmul(flip_k[:, h * 128:h * 128 + D + 1], s["Wk"][:, h * D:(h + 1) * D], s["ident"][0:D + 1, 0:D + 1], start=True, stop=True).then_inc(transposed, 1)

            @block.vector
            def _(dve):
                dve.memset(s["X"][:], 0.0).then_inc(cleared, 1)
                dve.memset(s["influence"][:], 0.0).then_inc(cleared, 1)
                dve.memset(s["ln_eps"][:], LN_EPS).then_inc(cleared, 1)
                dve.wait_ge(made, 3)
                dve.tensor_copy(s["iota_row"][:], iota_i[:]).then_inc(cleared, 1)
                dve.wait_ge(loaded, 16 * n_loads)
                dve.tensor_copy(s["src_index"][:], table[:, :, 0:1].squeeze(2)).then_inc(cleared, 1)
                dve.tensor_copy(s["dst_local"][:], table[:, :, 1:2].squeeze(2)).then_inc(cleared, 1)
                dve.tensor_copy(s["edge_index"][:], table[:, :, 2:3].squeeze(2)).then_inc(cleared, 1)
                dve.wait_ge(transposed, 4 + HEADS)
                for h in range(HEADS):
                    dve.tensor_copy(s["WkT"][:, h, :], flip_k[:, h * 128:h * 128 + D + 1]).then_inc(cleared, 1)
                for i in range(4):
                    dve.tensor_copy(s[("sage1", "sage2")[i // 2]][(i % 2) * D:(i % 2) * D + D, :], flip[i][:, 0:D]).then_inc(cleared, 1)
                dve.wait_ge(cleared, 11 + HEADS)
    return s


def gather_sum(nc, name, s, rows, index, counted, edge=None, ea=None):
    width = D + 1 if counted else D
    groups = BY_DST.chunks // J
    with ExitStack() as ctx:
        def sb(n, shape, dt=F32):
            return [ctx.enter_context(nc.sbuf_tensor(f"{name}_{n}{k}", shape, dt)) for k in range(2)]

        def ps(n, shape):
            return [ctx.enter_context(nc.psum_tensor(f"{name}_{n}{k}", shape, F32)) for k in range(2)]

        def sem(n):
            return ctx.enter_context(nc.semaphore(f"{name}_{n}"))

        idx = sb("idx", [P, J], I32)
        got = sb("got", [P, J, width])
        onehot = sb("onehot", [P, J, P])
        banks = 2 if counted else 1
        per_bank = J // banks
        total = ps("total", [P, banks, 512])
        idx_copied = sem("idx_copied")
        gathered = [sem(f"gathered{k}") for k in range(2)]
        onehot_ready = sem("onehot_ready")
        summed = sem("summed")
        added = sem("added")
        started = sem("started")
        if edge:
            flipped = ps("flipped", [D, 512])
            turned = sb("turned", [D + 1, J, P])
            product = ps("product", [P, J, D])
            made = sb("made", [P, J, D])
            flip_ready = sem("flip_ready")
            flip_used = sem("flip_used")
            product_ready = sem("product_ready")
            made_ready = sem("made_ready")
            ea_moved = [sem(f"ea_moved{k}") for k in range(2)]
        if edge == "message":
            attr = sb("attr", [P, J, D])

        def per_group(run):
            def go(eng):
                run(0, 0, True)
                run(1, 1, True)
                with eng.Fori(2, groups - 1, 2) as g:
                    run(g, 0, False)
                    run(g + 1, 1, False)
            return go

        def dma_count(g, k, n):
            return (g - k) * (8 * n) + 16 * n

        with nc.Block() as block:
            @block.gpsimd
            def _(pool):
                def group(g, k, first):
                    if not first:
                        pool.wait_ge(summed, g - 1)
                    pool.tensor_copy(idx[k][:], index[:, bass.ds(g * J, J)]).then_inc(idx_copied, 1)
                    pool.wait_ge(idx_copied, g + 1)
                    pool.nop(nofuse=True)
                    for t in range(J):
                        pool.indirect_dma_start(got[k][:, t, 0:D], None, rows, bass.IndirectOffsetOnAxis(ap=idx[k][:, t:t + 1], axis=0)).then_inc(gathered[k], 16)

                per_group(group)(pool)

            @block.tensor
            def _(pe):
                pe.wait_ge(started, 1 + 2 * counted + 2 * bool(edge))

                def group(g, k, first):
                    pe.wait_ge(gathered[k], dma_count(g, k, J))
                    if edge == "message":
                        pe.wait_ge(ea_moved[k], dma_count(g, k, 1))
                    if edge:
                        for h in range(2):
                            if not (first and k == 0):
                                pe.wait_ge(flip_used, 2 * g - 1 + h)
                            for t in range(4 * h, 4 * h + 4):
                                to = flipped[h][:, (t - 4 * h) * P:(t - 4 * h + 1) * P]
                                ins = pe.matmul(to, got[k][:, t, 0:D], s["ident"][:], start=True, stop=edge == "attr")
                                if edge == "message":
                                    ins = pe.matmul(to, attr[k][:, t, :], s["ident"][:], start=False, stop=True)
                            ins.then_inc(flip_ready, 1)
                        if not first:
                            pe.wait_ge(made_ready, g - 1)
                        for h in range(2):
                            pe.wait_ge(flip_used, 2 * g + 1 + h)
                            for t in range(4 * h, 4 * h + 4):
                                ins = pe.matmul(product[k][:, t, :], turned[k][:, t, :], s["We" if edge == "attr" else "Wm"][:], start=True, stop=True)
                        ins.then_inc(product_ready, 1)
                    pe.wait_ge(onehot_ready, g + 1)
                    if not first:
                        pe.wait_ge(added, J * (g - 1))
                    if edge == "message":
                        pe.wait_ge(made_ready, g + 1)
                    for t in range(J):
                        what = made[k][:, t, :] if edge == "message" else got[k][:, t, :]
                        at = (t % per_bank) * width
                        ins = pe.matmul(total[k][:, t // per_bank, at:at + width], onehot[k][:, t, :], what, start=True, stop=True)
                    ins.then_inc(summed, 1)

                per_group(group)(pe)

            @block.vector
            def _(dve):
                dve.memset(s["acc"][:], 0.0).then_inc(started, 1)
                if counted:
                    for k in range(2):
                        dve.memset(got[k][:, :, D:D + 1], 1.0).then_inc(started, 1)
                if edge:
                    for k in range(2):
                        dve.memset(turned[k][D:D + 1, :, :], 1.0).then_inc(started, 1)
                dve.wait_ge(started, 1 + 2 * counted + 2 * bool(edge))

                def compare(g, k):
                    dve.tensor_tensor(onehot[k][:], s["dst_local"][:, bass.ds(g * J, J)].unsqueeze(2).broadcast_to([P, J, P]),
                                      s["iota_row"][:].unsqueeze(1).broadcast_to([P, J, P]), ALU.is_equal).then_inc(onehot_ready, 1)

                def add(g, k):
                    buckets = [dve.value_load(s["dst_bucket"][0:1, bass.ds(g * J + t, 1)], min_val=0, max_val=BY_DST.buckets - 1) for t in range(J)]
                    dve.wait_ge(summed, g + 1)
                    for t in range(J):
                        if not (isinstance(g, int) and g == 0 and t == 0):
                            dve.wait_ge(added, g * J + t)
                        at = (t % per_bank) * width
                        to = s["acc"][:, bass.ds(buckets[t], 1), 0:width].squeeze(1)
                        dve.tensor_tensor(to, to, total[k][:, t // per_bank, at:at + width], ALU.add).then_inc(added, 1)

                def group(g, k, first):
                    if not first:
                        dve.wait_ge(summed, g - 1)
                    compare(g, k)
                    add(g, k)

                per_group(group)(dve)

            if edge:
                @block.scalar
                def _(act):
                    act.wait_ge(started, 1 + 2 * counted + 2)

                    def group(g, k, first):
                        for h in range(2):
                            act.wait_ge(flip_ready, 2 * g + 1 + h)
                            if not first and h == 0:
                                act.wait_ge(product_ready, g - 1)
                            act.activation(turned[k][0:D, 4 * h:4 * h + 4, :].rearrange("d t p -> d (t p)"), flipped[h][:],
                                           ACT.Copy if edge == "attr" else ACT.Relu).then_inc(flip_used, 1)
                        act.wait_ge(product_ready, g + 1)
                        if not first:
                            if edge == "attr":
                                act.wait_ge(ea_moved[k], dma_count(g - 2, k, 1))
                            else:
                                act.wait_ge(summed, g - 1)
                        act.activation(made[k][:], product[k][:], ACT.Silu).then_inc(made_ready, 1)

                    per_group(group)(act)

                @block.sync
                def _(sp):
                    def group(g, k, first):
                        there = ea[:, bass.ds(g * J, J), :]
                        if edge == "attr":
                            sp.wait_ge(made_ready, g + 1)
                            sp.dma_start(there, made[k][:]).then_inc(ea_moved[k], 16)
                        else:
                            if not first:
                                sp.wait_ge(flip_used, 2 * g - 2)
                            sp.dma_start(attr[k][:], there).then_inc(ea_moved[k], 16)

                    per_group(group)(sp)
                    if edge == "attr":
                        for k in range(2):
                            sp.wait_ge(ea_moved[k], groups // 2 * 16)


def row(s, name, n):
    return s["rows"][:, ROWS.index(name), :].unsqueeze(1).broadcast_to([P, n, D])


class Roots:

    def __init__(self, ctx, nc, name):
        self.asked = ctx.enter_context(nc.semaphore(name + "_var_ready"))
        self.given = ctx.enter_context(nc.semaphore(name + "_root_ready"))


NORM_STEPS = 6


def layer_norm(dve, c, v, sq, stat, out, roots, n_root):
    n = v.shape[1]
    c.wait(dve)
    c.inc(dve.tensor_reduce(stat[:, 0, :], v, AX.X, ALU.add))
    c.wait(dve)
    c.inc(dve.tensor_scalar(stat[:, 1, :], stat[:, 0, :], 1.0 / D, None, ALU.mult))
    c.wait(dve)
    c.inc(dve.tensor_tensor(v, v, stat[:, 1, :].unsqueeze(2).broadcast_to([P, n, D]), ALU.subtract))
    c.wait(dve)
    c.inc(dve.tensor_tensor(sq, v, v, ALU.mult))
    c.wait(dve)
    dve.tensor_reduce(stat[:, 2, :], sq, AX.X, ALU.add).then_inc(roots.asked, 1)
    dve.wait_ge(roots.given, n_root + 1)
    c.inc(dve.reciprocal(stat[:, 3, :], stat[:, 3, :]))
    c.wait(dve)
    c.inc(dve.tensor_tensor(out, v, stat[:, 3, :].unsqueeze(2).broadcast_to([P, n, D]), ALU.mult))


def norm_root(act, s, stat, roots, n_root):
    act.wait_ge(roots.asked, n_root + 1)
    act.activation(stat[:, 3, :], stat[:, 2, :], ACT.Sqrt, bias=s["ln_eps"][:, 0:1], scale=1.0 / D).then_inc(roots.given, 1)


def nodes(nc, name, s, kind, rows_out, H=None):
    SPLIT = ((0, 4), (4, NG))
    hidden = 2 if kind == "mlp" else 0
    with ExitStack() as ctx:
        def sb(n, shape, dt=F32):
            return ctx.enter_context(nc.sbuf_tensor(f"{name}_{n}", shape, dt))

        def ps(n, shape):
            return ctx.enter_context(nc.psum_tensor(f"{name}_{n}", shape, F32))

        def sem(n):
            return ctx.enter_context(nc.semaphore(f"{name}_{n}"))

        joined = sb("joined", [P, NG, 2 * D])
        flipped = ps("flipped", [P, 2, 512])
        act_in = [sb(f"in{n}", [P, NG, P]) for n in range(1 + hidden)]
        dense = [ps(f"dense{n}", [P, 2, 512]) for n in range(hidden)]
        y_ps = ps("y", [P, NG, D])
        v = sb("v", [P, NG, D])
        sq = sb("sq", [P, NG, D])
        stat = sb("stat", [P, 4, NG])
        count = sb("count", [P, NG])
        joined_ready = sem("joined_ready")
        dense_ready = sem("dense_ready")
        act_ready = sem("act_ready")
        y_ready = sem("y_ready")
        step = sem("step")
        stored = sem("stored")
        roots = Roots(ctx, nc, name)
        norms = {"mlp": 2, "sage1": 0, "sage2": 1}[kind]
        if kind == "mlp":
            STEPS, JOIN, weights = 6 + 2 * NORM_STEPS, 2, (s["W0"], s["W1"])
        elif kind == "sage1":
            STEPS, JOIN, weights = 6, 4, ()
        else:
            STEPS, JOIN, weights = 6 + NORM_STEPS, 4, ()

        with nc.Block() as block:
            @block.vector
            def _(dve):
                with dve.Fori(0, NGROUPS) as i:
                    c = Count(step, i * STEPS)
                    tiles = bass.ds(i * NG, NG)
                    if kind == "mlp":
                        c.inc(dve.tensor_copy(joined[:, :, 0:D], s["X"][:, tiles, :]))
                        c.inc(dve.tensor_copy(joined[:, :, D:], s["acc"][:, tiles, 0:D]))
                    else:
                        c.inc(dve.tensor_scalar(count[:], s["acc"][:, tiles, D:D + 1].squeeze(2), 1.0, None, ALU.max))
                        c.wait(dve)
                        c.inc(dve.reciprocal(count[:], count[:]))
                        c.wait(dve)
                        c.inc(dve.tensor_tensor(joined[:, :, 0:D], s["acc"][:, tiles, 0:D], count[:].unsqueeze(2).broadcast_to([P, NG, D]), ALU.mult))
                        c.inc(dve.tensor_copy(joined[:, :, D:], (s["X"] if kind == "sage1" else H)[:, tiles, :]))
                    dve.wait_ge(y_ready, i + 1)
                    if kind == "mlp":
                        c.inc(dve.tensor_tensor(v[:], y_ps[:], row(s, "L0_gnn_b2", NG), ALU.add))
                        layer_norm(dve, c, v[:], sq[:], stat, v[:], roots, i * 2)
                        c.wait(dve)
                        c.inc(dve.tensor_tensor(v[:], v[:], row(s, "L0_gnn_ln_g", NG), ALU.mult))
                        c.wait(dve)
                        c.inc(dve.tensor_tensor(v[:], v[:], row(s, "L0_gnn_ln_b", NG), ALU.add))
                        c.wait(dve)
                        c.inc(dve.scalar_tensor_tensor(v[:], s["X"][:, tiles, :], 2.0, v[:], ALU.mult, ALU.add))
                        layer_norm(dve, c, v[:], sq[:], stat, s["X"][:, tiles, :], roots, i * norms + norms - 1)
                    elif kind == "sage1":
                        c.inc(dve.tensor_tensor(v[:], y_ps[:], row(s, "L1_gnn_b1_l", NG), ALU.add))
                        c.wait(dve)
                        c.inc(dve.tensor_scalar(H[:, tiles, :], v[:], 0.0, None, ALU.max))
                    else:
                        c.inc(dve.tensor_tensor(v[:], y_ps[:], row(s, "L1_gnn_b2_l", NG), ALU.add))
                        c.wait(dve)
                        c.inc(dve.tensor_tensor(v[:], v[:], s["X"][:, tiles, :], ALU.add))
                        layer_norm(dve, c, v[:], sq[:], stat, s["X"][:, tiles, :], roots, i * norms + norms - 1)
                    assert c.n == STEPS, c.n

            @block.tensor
            def _(pe):
                with pe.Fori(0, NGROUPS) as i:
                    pe.wait_ge(step, i * STEPS + JOIN)
                    for b, (t0, t1) in enumerate(SPLIT):
                        for t in range(t0, t1):
                            ins = pe.matmul(flipped[:, b, (t - t0) * P:(t - t0 + 1) * P], joined[:, t, :], s["ident"][:], start=True, stop=True)
                    ins.then_inc(dense_ready, 1)
                    for n, w in enumerate(weights):
                        pe.wait_ge(act_ready, (i * (1 + hidden) + n) * 2 + 2)
                        for b, (t0, t1) in enumerate(SPLIT):
                            ins = pe.matmul(dense[n][:, b, 0:(t1 - t0) * P], w[:], act_in[n][:, t0:t1, :].rearrange("k t p -> k (t p)"), start=True, stop=True)
                        ins.then_inc(dense_ready, 1)
                    pe.wait_ge(act_ready, (i * (1 + hidden) + hidden) * 2 + 2)
                    w = s[{"mlp": "W2", "sage1": "sage1", "sage2": "sage2"}[kind]]
                    for t in range(NG):
                        ins = pe.matmul(y_ps[:, t, :], act_in[hidden][:, t, :], w[:], start=True, stop=True)
                    ins.then_inc(y_ready, 1)

            @block.scalar
            def _(act):
                with act.Fori(0, NGROUPS) as i:
                    for n in range(1 + hidden):
                        act.wait_ge(dense_ready, i * (1 + hidden) + n + 1)
                        frm = dense[n - 1] if n else flipped
                        for b, (t0, t1) in enumerate(SPLIT):
                            to = act_in[n][:, t0:t1, :].rearrange("k t p -> k (t p)")
                            if n:
                                ins = act.activation(to, frm[:, b, 0:(t1 - t0) * P], ACT.Relu, bias=s["b0" if n == 1 else "b1"][:, 0:1])
                            else:
                                ins = act.activation(to, frm[:, b, 0:(t1 - t0) * P], ACT.Copy)
                            ins.then_inc(act_ready, 1)
                    for r in range(norms):
                        norm_root(act, s, stat, roots, i * norms + r)

            @block.sync
            def _(sp):
                with sp.Fori(0, NGROUPS) as i:
                    sp.wait_ge(step, i * STEPS + STEPS)
                    sp.dma_start(rows_out.rearrange("(t p) f -> p t f", p=P)[:, bass.ds(i * NG, NG), :],
                                 (H if kind == "sage1" else s["X"])[:, bass.ds(i * NG, NG), :]).then_inc(stored, 16)
                sp.wait_ge(stored, NGROUPS * 16)


def graph_norm(nc, s, o, rows_out):
    with ExitStack() as ctx:
        def sb(n, shape, dt=F32):
            return ctx.enter_context(nc.sbuf_tensor(f"norm_{n}", shape, dt))

        def sem(n):
            return ctx.enter_context(nc.semaphore(f"norm_{n}"))

        sq = sb("sq", [P, NT, D])
        part = sb("part", [P, 2])
        st = sb("st", [P, 8])
        real = sb("real", [P, 1])
        stat = sb("stat", [P, 4, NT])
        tot = ctx.enter_context(nc.psum_tensor("norm_tot", [P, 2], F32))
        step = sem("step")
        masked = sem("masked")
        parts_ready = sem("parts_ready")
        tot_ready = sem("tot_ready")
        STEPS = 12 + NORM_STEPS
        stored = sem("stored")
        var_ready = sem("all_var_ready")
        root_ready = sem("all_root_ready")
        roots = Roots(ctx, nc, "norm")
        with nc.Block() as block:
            @block.scalar
            def _(act):
                act.wait_ge(var_ready, 1)
                act.activation(st[:, 5:6], st[:, 4:5], ACT.Sqrt, bias=s["ln_eps"][:, 0:1]).then_inc(root_ready, 1)
                norm_root(act, s, stat, roots, 0)

            @block.gpsimd
            def _(pool):
                pool.affine_select(out=real[:], in_=s["ones"][:, 0:1], compare_op=ALU.is_ge, fill=0.0, base=N - (NT - 1) * P - 1,
                                   pattern=[[0, 1]], channel_multiplier=-1).then_inc(masked, 1)

            @block.tensor
            def _(pe):
                pe.wait_ge(parts_ready, 2)
                pe.matmul(tot[:], s["ones"][:], part[:], start=True, stop=True).then_inc(tot_ready, 1)

            @block.vector
            def _(dve):
                c = Count(step)
                X, acc = s["X"], s["acc"][:, 0:NT, 0:D]
                c.inc(dve.tensor_scalar(st[:, 0:1], s["eps"][:], 1.0, None, ALU.add))
                c.wait(dve)
                c.inc(dve.scalar_tensor_tensor(o[:], X[:], st[:, 0:1], acc, ALU.mult, ALU.add))
                dve.wait_ge(masked, 1)
                c.wait(dve)
                c.inc(dve.tensor_scalar(o[:, NT - 1, :], o[:, NT - 1, :], real[:, 0:1], None, ALU.mult))
                c.wait(dve)
                dve.tensor_reduce(part[:, 0:1], o[:].rearrange("p t f -> p (t f)"), AX.X, ALU.add).then_inc(parts_ready, 1)
                c.inc(dve.tensor_tensor(sq[:], o[:], o[:], ALU.mult))
                c.wait(dve)
                dve.tensor_reduce(part[:, 1:2], sq[:].rearrange("p t f -> p (t f)"), AX.X, ALU.add).then_inc(parts_ready, 1)
                dve.wait_ge(tot_ready, 1)
                c.inc(dve.tensor_scalar(st[:, 1:3], tot[:], 1.0 / (N * D), None, ALU.mult))
                c.wait(dve)
                c.inc(dve.tensor_tensor(st[:, 3:4], st[:, 1:2], st[:, 1:2], ALU.mult))
                c.wait(dve)
                dve.tensor_tensor(st[:, 4:5], st[:, 2:3], st[:, 3:4], ALU.subtract).then_inc(var_ready, 1)
                dve.wait_ge(root_ready, 1)
                c.inc(dve.reciprocal(st[:, 5:6], st[:, 5:6]))
                c.wait(dve)
                c.inc(dve.tensor_scalar(o[:], o[:], st[:, 1:2], st[:, 5:6], ALU.subtract, ALU.mult))
                c.wait(dve)
                c.inc(dve.tensor_tensor(o[:], o[:], row(s, "L2_gnn_gamma2", NT), ALU.mult))
                c.wait(dve)
                c.inc(dve.tensor_tensor(o[:], o[:], row(s, "L2_gnn_beta2", NT), ALU.add))
                c.wait(dve)
                c.inc(dve.tensor_tensor(o[:], o[:], X[:], ALU.add))
                c.wait(dve)
                c.inc(dve.scalar_tensor_tensor(o[:], o[:], 0.0, X[:], ALU.max, ALU.add))
                layer_norm(dve, c, o[:], sq[:], stat, X[:], roots, 0)
                assert c.n == STEPS, c.n

            @block.sync
            def _(sp):
                sp.wait_ge(step, STEPS)
                sp.dma_start(rows_out.rearrange("(t p) f -> p t f", p=P), s["X"][:]).then_inc(stored, 16)
                sp.wait_ge(stored, 16)


def score_tables(nc, s, T):
    per_tile = P // BY_SRC.width
    SPLIT = ((0, 4), (4, NG))
    with ExitStack() as ctx:
        def sb(n, shape, dt=F32):
            return ctx.enter_context(nc.sbuf_tensor(f"keys_{n}", shape, dt))

        def ps(n, shape):
            return ctx.enter_context(nc.psum_tensor(f"keys_{n}", shape, F32))

        def sem(n):
            return ctx.enter_context(nc.semaphore(f"keys_{n}"))

        scale = sb("scale", [P, NT])
        xs = sb("xs", [P, NG, D + 1])
        xs_ps = ps("xs_ps", [D + 1, 2, 512])
        xsT = sb("xsT", [D + 1, NG, P])
        q_ps = ps("q_ps", [D, 2, 512])
        qT = sb("qT", [D, NG, P])
        t_ps = ps("t_ps", [D + 1, 2, 512])
        Tt = sb("Tt", [D + 1, NG * per_tile, HEADS, BY_SRC.width])
        zero = sb("zero", [D + 1, P])
        scaled = sem("scaled")
        xs_ready = sem("xs_ready")
        dense_ready = sem("dense_ready")
        act_ready = sem("act_ready")
        t_ready = sem("t_ready")
        t_copied = sem("t_copied")
        stored = sem("stored")
        K = 1 + HEADS
        with nc.Block() as block:
            @block.vector
            def _(dve):
                dve.tensor_scalar(scale[:], s["influence"][:], float(D) ** -0.5, None, ALU.mult).then_inc(scaled, 1)
                dve.memset(zero[:], 0.0).then_inc(scaled, 1)
                dve.wait_ge(scaled, 2)
                with dve.Fori(0, NGROUPS) as i:
                    tiles = bass.ds(i * NG, NG)
                    sc = scale[:, tiles].unsqueeze(2)
                    dve.tensor_tensor(xs[:, :, 0:D], s["X"][:, tiles, :], sc.broadcast_to([P, NG, D]), ALU.mult).then_inc(xs_ready, 1)
                    dve.tensor_copy(xs[:, :, D:D + 1], sc).then_inc(xs_ready, 1)
                    for h in range(HEADS):
                        dve.wait_ge(t_ready, i * HEADS + h + 1)
                        if h == 0:
                            dve.wait_ge(stored, i * 16 + 16)
                        for b, (t0, t1) in enumerate(SPLIT):
                            dve.tensor_copy(Tt[:, t0 * per_tile:t1 * per_tile, h, :],
                                            t_ps[:, b, 0:(t1 - t0) * P].rearrange("k (b n) -> k b n", n=BY_SRC.width)).then_inc(t_copied, 1)

            @block.tensor
            def _(pe):
                with pe.Fori(0, NGROUPS) as i:
                    pe.wait_ge(xs_ready, i * 2 + 2)
                    for b, (t0, t1) in enumerate(SPLIT):
                        for t in range(t0, t1):
                            ins = pe.matmul(xs_ps[:, b, (t - t0) * P:(t - t0 + 1) * P], xs[:, t, :], s["ident"][:], start=True, stop=True)
                    ins.then_inc(dense_ready, 1)
                    for h in range(HEADS):
                        pe.wait_ge(act_ready, (i * K + h) * 2 + 2)
                        for b, (t0, t1) in enumerate(SPLIT):
                            ins = pe.matmul(q_ps[:, b, 0:(t1 - t0) * P], s["Wq"][:, h * D:(h + 1) * D], xsT[:, t0:t1, :].rearrange("k t p -> k (t p)"), start=True, stop=True)
                        ins.then_inc(dense_ready, 1)
                        pe.wait_ge(act_ready, (i * K + h + 1) * 2 + 2)
                        if h:
                            pe.wait_ge(t_copied, (i * HEADS + h) * 2)
                        for b, (t0, t1) in enumerate(SPLIT):
                            ins = pe.matmul(t_ps[:, b, 0:(t1 - t0) * P], s["WkT"][:, h, :], qT[:, t0:t1, :].rearrange("k t p -> k (t p)"), start=True, stop=True)
                        ins.then_inc(t_ready, 1)

            @block.scalar
            def _(act):
                with act.Fori(0, NGROUPS) as i:
                    for n in range(K):
                        act.wait_ge(dense_ready, i * K + n + 1)
                        for b, (t0, t1) in enumerate(SPLIT):
                            to = (qT if n else xsT)[:, t0:t1, :].rearrange("k t p -> k (t p)")
                            if n > 1 and b == 0:
                                act.wait_ge(t_ready, i * HEADS + n - 1)
                            act.activation(to, (q_ps if n else xs_ps)[:, b, 0:(t1 - t0) * P], ACT.Copy).then_inc(act_ready, 1)

            @block.sync
            def _(sp):
                sp.wait_ge(scaled, 2)
                sp.dma_start(T[:, BY_SRC.buckets - 1, :], zero[:]).then_inc(stored, 16)
                with sp.Fori(0, NGROUPS) as i:
                    sp.wait_ge(t_copied, (i + 1) * HEADS * 2)
                    sp.dma_start(T[:, bass.ds(i * (NG * per_tile), NG * per_tile), :], Tt[:].rearrange("k b h n -> k b (h n)")).then_inc(stored, 16)
                sp.wait_ge(stored, (NGROUPS + 1) * 16)


def load_src_list(nc, keep, s, tables, chunk_bucket):
    def sb(name, shape, dt=F32):
        s[name] = keep.enter_context(nc.sbuf_tensor(name, shape, dt))

    sb("dst_index", [P, BY_SRC.chunks], I32)
    sb("src_local", [P, BY_SRC.chunks + J])
    sb("src_bucket", [1, BY_SRC.jt * P], I32)
    sb("U", [P, BY_SRC.buckets, D + 1])
    sb("M", [P, BY_SRC.buckets])
    with nc.sbuf_tensor("list_table", [P, BY_SRC.chunks, BY_SRC.fields], I32) as table, \
            nc.semaphore("list_loaded") as loaded, nc.semaphore("list_ready") as ready, nc.Block() as block:
        @block.sync
        def _(sp):
            sp.dma_start(table[:], tables["src"].rearrange("(p c) f -> p c f", p=P)).then_inc(loaded, 16)
            sp.dma_start(s["src_bucket"][:], chunk_bucket["src"].unsqueeze(0)).then_inc(loaded, 16)
            sp.wait_ge(loaded, 32)

        @block.vector
        def _(dve):
            dve.memset(s["U"][:], 0.0).then_inc(ready, 1)
            dve.memset(s["M"][:], NO_MAX).then_inc(ready, 1)
            dve.wait_ge(loaded, 32)
            dve.tensor_copy(s["dst_index"][:], table[:, :, 0:1].squeeze(2)).then_inc(ready, 1)
            dve.tensor_copy(s["src_local"][:, 0:BY_SRC.chunks], table[:, :, 1:2].squeeze(2)).then_inc(ready, 1)
            dve.memset(s["src_local"][:, BY_SRC.chunks:], ABSENT).then_inc(ready, 1)
            dve.wait_ge(ready, 5)


def attention(nc, s, rows, T):
    W = BY_SRC.width
    K = D + 1 + W
    UNIT = J // 2
    GB = 4
    BODY = 2 * GB
    groups = BY_SRC.chunks // J
    units = 2 * groups
    assert groups % GB == 0
    with ExitStack() as ctx:
        def sb1(n, shape, dt=F32):
            return ctx.enter_context(nc.sbuf_tensor(f"att_{n}", shape, dt))

        def sb(n, shape, dt=F32, count=2):
            return [sb1(f"{n}{k}", shape, dt) for k in range(count)]

        def ps(n):
            return [ctx.enter_context(nc.psum_tensor(f"att_{n}{k}", [P, UNIT, P], F32)) for k in range(2)]

        def sem(n):
            return ctx.enter_context(nc.semaphore(f"att_{n}"))

        idx = sb("idx", [P, J], I32, GB)
        got = sb("got", [P, J, K], F32, GB)
        Tt = sb("Tt", [K, J, P])
        turned = sb("turned", [K, UNIT, P])
        probs = sb("probs", [P, UNIT, P])
        probsT = sb("probsT", [P, UNIT, P])
        top = sb1("top", [P, UNIT])
        before = sb1("before", [P, UNIT])
        after = sb1("after", [P, UNIT])
        minus = sb("minus", [P, UNIT])
        drop = sb("drop", [P, UNIT])
        keep = sb("keep", [P, UNIT], F32, 4)
        maskrow = sb1("maskrow", [W, HEADS, W])
        flipped, scores, flipped2, sums = ps("flipped"), ps("scores"), ps("flipped2"), ps("sums")
        started = sem("started")
        mask_set = sem("mask_set")
        idx_copied = sem("idx_copied")
        gathered = [sem(f"gathered{k}") for k in range(GB)]
        T_loaded = [sem(f"T_loaded{k}") for k in range(2)]
        masked = [sem(f"masked{k}") for k in range(GB)]
        flip_ready = sem("flip_ready")
        turned_ready = sem("turned_ready")
        scores_ready = sem("scores_ready")
        step = sem("step")
        probs_ready = sem("probs_ready")
        keep_ready = sem("keep_ready")
        flip2_ready = sem("flip2_ready")
        probsT_ready = sem("probsT_ready")
        sums_ready = sem("sums_ready")
        added = sem("added")
        STEPS = 1 + 3 * UNIT + 2

        def known(n):
            return isinstance(n, int)

        def wait(eng, semaphore, value):
            if not known(value) or value > 0:
                eng.wait_ge(semaphore, value)

        def in_steps(eng, run):
            for u in range(BODY):
                run(u, u)
            with eng.Fori(BODY, units - BODY + 1, BODY) as base:
                for r in range(BODY):
                    run(base + r, r)
            for u in range(units, units + 3):
                run(u, u % BODY)

        def there(v):
            return not known(v) or 0 <= v < units

        def in_groups(eng, n, run):
            for g in range(n):
                run(g, g)
            with eng.Fori(n, groups - n + 1, n) as base:
                for k in range(n):
                    run(base + k, k)

        with nc.Block() as block:
            @block.gpsimd
            def _(pool):
                pool.memset(maskrow[:], 0.0).then_inc(mask_set, 1)
                pool.wait_ge(mask_set, 1)
                pool.affine_select(out=maskrow[:], in_=maskrow[:], compare_op=ALU.not_equal, fill=NO_SCORE, base=0,
                                   pattern=[[0, HEADS], [-1, W]], channel_multiplier=1).then_inc(mask_set, 1)

                def gather(g, k):
                    wait(pool, sums_ready, 2 * g - 2 * GB + 2)
                    pool.tensor_copy(idx[k][:], s["dst_index"][:, bass.ds(g * J, J)]).then_inc(idx_copied, 1)
                    pool.wait_ge(idx_copied, g + 1)
                    pool.nop(nofuse=True)
                    for t in range(J):
                        pool.indirect_dma_start(got[k][:, t, 0:D], None, rows, bass.IndirectOffsetOnAxis(ap=idx[k][:, t:t + 1], axis=0)).then_inc(gathered[k], 16)

                in_groups(pool, GB, gather)

            @block.sync
            def _(sp):
                sp.wait_ge(mask_set, 2)
                for k in range(2):
                    for t in range(J):
                        sp.dma_start(Tt[k][D + 1:K, t, :], maskrow[:].rearrange("k h n -> k (h n)")).then_inc(started, 16)

                def load(g, k):
                    wait(sp, scores_ready, 2 * g - 2)
                    for t in range(J):
                        b = sp.value_load(s["src_bucket"][0:1, bass.ds(g * J + t, 1)], min_val=0, max_val=BY_SRC.buckets - 1)
                        sp.dma_start(Tt[k][0:D + 1, t, :], T[:, bass.ds(b, 1), :].squeeze(1)).then_inc(T_loaded[k], 16)

                in_groups(sp, 2, load)

            @block.tensor
            def _(pe):
                pe.wait_ge(started, 2 * J * 16 + GB)

                def turn(v, r):
                    k, half = r // 2, r % 2
                    if half == 0:
                        pe.wait_ge(gathered[k], (v - r) * J * 2 + J * 16)
                        pe.wait_ge(masked[k], (v - r) + BODY)
                    wait(pe, turned_ready, v - 1)
                    for t in range(UNIT):
                        ins = pe.matmul(flipped[r % 2][0:K, t, :], got[k][:, half * UNIT + t, :], s["ident"][:], start=True, stop=True)
                    ins.then_inc(flip_ready, 1)

                def turn_probs(v, r):
                    pe.wait_ge(probs_ready, v + 1)
                    wait(pe, probsT_ready, v - 1)
                    for t in range(UNIT):
                        ins = pe.matmul(flipped2[r % 2][:, t, :], probs[r % 2][:, t, :], s["ident"][:], start=True, stop=True)
                    ins.then_inc(flip2_ready, 1)

                def score(v, r):
                    k, half = (r // 2) % 2, r % 2
                    if half == 0:
                        pe.wait_ge(T_loaded[k], (v - r) * (J * 4) + (r // 4 + 1) * J * 16)
                    pe.wait_ge(turned_ready, v + 1)
                    wait(pe, probs_ready, v - 1)
                    for t in range(UNIT):
                        ins = pe.matmul(scores[r % 2][:, t, :], Tt[k][:, half * UNIT + t, :], turned[r % 2][:, t, :], start=True, stop=True)
                    ins.then_inc(scores_ready, 1)

                def sum_up(v, r):
                    k, half = r // 2, r % 2
                    pe.wait_ge(probsT_ready, v + 1)
                    wait(pe, added, (v - 1) * UNIT)
                    for t in range(UNIT):
                        ins = pe.matmul(sums[r % 2][:, t, 0:D + 1], probsT[r % 2][:, t, :], got[k][:, half * UNIT + t, 0:D + 1], start=True, stop=True)
                    ins.then_inc(sums_ready, 1)

                def run(u, r):
                    for lag, what in ((0, turn), (2, turn_probs), (1, score), (3, sum_up)):
                        if there(u - lag):
                            what(u - lag, (r - lag) % BODY)

                in_steps(pe, run)

            @block.scalar
            def _(act):
                def copy_turned(v, r):
                    act.wait_ge(flip_ready, v + 1)
                    wait(act, scores_ready, v - 1)
                    act.activation(turned[r % 2][:], flipped[r % 2][0:K], ACT.Copy).then_inc(turned_ready, 1)

                def copy_probs(v, r):
                    act.wait_ge(flip2_ready, v + 1)
                    wait(act, sums_ready, v - 1)
                    act.activation(probsT[r % 2][:], flipped2[r % 2][:], ACT.Copy).then_inc(probsT_ready, 1)

                def exponentials(v, r):
                    act.wait_ge(step, v * STEPS + STEPS)
                    wait(act, flip2_ready, v - 1)
                    for t in range(UNIT):
                        ins = act.activation(probs[r % 2][:, t, :], scores[r % 2][:, t, :], ACT.Exp, bias=minus[r % 2][:, t:t + 1])
                    ins.then_inc(probs_ready, 1)
                    wait(act, added, (v - 3) * UNIT)
                    act.activation(keep[r % 4][:], drop[r % 2][:], ACT.Exp).then_inc(keep_ready, 1)

                def run(u, r):
                    for lag, what in ((0, copy_turned), (2, copy_probs), (1, exponentials)):
                        if there(u - lag):
                            what(u - lag, (r - lag) % BODY)

                in_steps(act, run)

            @block.vector
            def _(dve):
                for k in range(GB):
                    dve.memset(got[k][:, :, D:D + 1], 1.0).then_inc(started, 1)

                def mask(v, k):
                    wait(dve, sums_ready, v - 2 * GB + 2)
                    local = s["src_local"][:, bass.ds(v * UNIT, J)].unsqueeze(2).broadcast_to([P, J, W])
                    dve.tensor_tensor(got[k][:, :, D + 1:K], local, s["iota_row"][:, 0:W].unsqueeze(1).broadcast_to([P, J, W]),
                                      ALU.not_equal).then_inc(masked[k], BODY)

                def buckets_of(v):
                    return [dve.value_load(s["src_bucket"][0:1, bass.ds(v * UNIT + t, 1)], min_val=0, max_val=BY_SRC.buckets - 1) for t in range(UNIT)]

                def maxima(v, r):
                    buckets = buckets_of(v)
                    c = Count(step, v * STEPS)
                    wait(dve, keep_ready, v - 1)
                    dve.wait_ge(scores_ready, v + 1)
                    c.inc(dve.tensor_reduce(top[:], scores[r % 2][:], AX.X, ALU.max))
                    for t in range(UNIT):
                        m = s["M"][:, bass.ds(buckets[t], 1)]
                        c.wait(dve)
                        c.inc(dve.tensor_tensor(before[:, t:t + 1], m, m, ALU.max))
                        c.inc(dve.tensor_tensor(after[:, t:t + 1], m, top[:, t:t + 1], ALU.max))
                        c.wait(dve)
                        c.inc(dve.tensor_tensor(m, after[:, t:t + 1], after[:, t:t + 1], ALU.max))
                    c.wait(dve)
                    c.inc(dve.tensor_scalar(minus[r % 2][:], after[:], -1.0, None, ALU.mult))
                    c.inc(dve.tensor_tensor(drop[r % 2][:], before[:], after[:], ALU.subtract))
                    assert c.n == STEPS, c.n

                def add(v, r):
                    buckets = buckets_of(v)
                    dve.wait_ge(keep_ready, v + 1)
                    dve.wait_ge(sums_ready, v + 1)
                    for t in range(UNIT):
                        u = s["U"][:, bass.ds(buckets[t], 1), :].squeeze(1)
                        wait(dve, added, v * UNIT + t)
                        dve.scalar_tensor_tensor(u, u, keep[r % 4][:, t:t + 1], sums[r % 2][:, t, 0:D + 1], ALU.mult, ALU.add).then_inc(added, 1)

                mask(0, 0)

                def run(u, r):
                    if there(u + 2) and r % 2 == 0:
                        mask(u + 2, (r // 2 + 1) % GB)
                    for lag, what in ((1, maxima), (3, add)):
                        if there(u - lag):
                            what(u - lag, (r - lag) % BODY)

                in_steps(dve, run)


def attention_out(nc, s, out):
    B = P // BY_SRC.width
    last = N - (NT - 1) * P
    with ExitStack() as ctx:
        def sb(n, shape, dt=F32):
            return ctx.enter_context(nc.sbuf_tensor(f"fin_{n}", shape, dt))

        def ps(n, shape):
            return [ctx.enter_context(nc.psum_tensor(f"fin_{n}{k}", shape, F32)) for k in range(2)]

        def sem(n):
            return ctx.enter_context(nc.semaphore(f"fin_{n}"))

        inv = sb("inv", [P, NG * B])
        un = sb("un", [P, NG * B, D + 1])
        flipped = ps("flipped", [D + 1, B, HEADS, BY_SRC.width])
        uT = [sb(f"uT{k}", [D + 1, HEADS, B, BY_SRC.width]) for k in range(2)]
        o_ps = ps("o", [D, HEADS, P])
        oT = [sb(f"oT{k}", [D, HEADS, P]) for k in range(2)]
        y_ps = ctx.enter_context(nc.psum_tensor("fin_y", [P, NG, D], F32))
        v = sb("v", [P, NG, D])
        res = sb("res", [P, NG, D])
        sq = sb("sq", [P, NG, D])
        stat = sb("stat", [P, 4, NG])
        step = sem("step")
        flip_ready = sem("flip_ready")
        uT_ready = sem("uT_ready")
        o_ready = sem("o_ready")
        oT_ready = sem("oT_ready")
        y_ready = sem("y_ready")
        stored = sem("stored")
        roots = Roots(ctx, nc, "fin")
        DIV = 3
        STEPS = DIV + 2 + NORM_STEPS
        with nc.Block() as block:
            @block.vector
            def _(dve):
                def group(i):
                    c = Count(step, i * STEPS)
                    tiles = bass.ds(i * NG, NG)
                    u = s["U"][:, bass.ds(i * (NG * B), NG * B), :]
                    c.inc(dve.tensor_scalar(inv[:], u[:, :, D:D + 1].squeeze(2), 1e-10, None, ALU.add))
                    c.wait(dve)
                    c.inc(dve.reciprocal(inv[:], inv[:]))
                    c.wait(dve)
                    c.inc(dve.tensor_tensor(un[:], u, inv[:].unsqueeze(2).broadcast_to([P, NG * B, D + 1]), ALU.mult))
                    dve.wait_ge(y_ready, i + 1)
                    c.inc(dve.tensor_tensor(v[:], y_ps[:], row(s, "L3_gnn_bo", NG), ALU.add))
                    c.wait(dve)
                    c.inc(dve.tensor_tensor(v[:], v[:], s["X"][:, tiles, :], ALU.add))
                    if not isinstance(i, int):
                        dve.wait_ge(stored, i * 16)
                    layer_norm(dve, c, v[:], sq[:], stat, res[:], roots, i)
                    assert c.n == STEPS

                group(0)
                with dve.Fori(1, NGROUPS) as i:
                    group(i)

            @block.tensor
            def _(pe):
                with pe.Fori(0, NGROUPS) as i:
                    pe.wait_ge(step, i * STEPS + DIV)
                    for t in range(NG + 2):
                        if t < NG:
                            for b in range(B):
                                ins = pe.matmul(flipped[t % 2][:, b].rearrange("k h n -> k (h n)"), un[:, t * B + b, :], s["ident"][:], start=True, stop=True)
                            ins.then_inc(flip_ready, 1)
                        if 1 <= t < NG + 1:
                            n = t - 1
                            pe.wait_ge(uT_ready, i * NG + n + 1)
                            for h in range(HEADS):
                                ins = pe.matmul(o_ps[n % 2][:, h, :], s["Wv"][:, h * D:(h + 1) * D], uT[n % 2][:, h].rearrange("k b n -> k (b n)"), start=True, stop=True)
                            ins.then_inc(o_ready, 1)
                        if t >= 2:
                            n = t - 2
                            pe.wait_ge(oT_ready, i * NG + n + 1)
                            for h in range(HEADS):
                                ins = pe.matmul(y_ps[:, n, :], oT[n % 2][:, h, :], s["Wo"][:, h, :], start=(h == 0), stop=(h == HEADS - 1))
                    ins.then_inc(y_ready, 1)

            @block.scalar
            def _(act):
                with act.Fori(0, NGROUPS) as i:
                    for t in range(NG + 1):
                        if t < NG:
                            act.wait_ge(flip_ready, i * NG + t + 1)
                            act.activation(uT[t % 2][:].rearrange("k h b n -> k b h n"), flipped[t % 2][:], ACT.Copy).then_inc(uT_ready, 1)
                        if t >= 1:
                            act.wait_ge(o_ready, i * NG + t)
                            act.activation(oT[(t - 1) % 2][:], o_ps[(t - 1) % 2][:], ACT.Copy).then_inc(oT_ready, 1)
                    norm_root(act, s, stat, roots, i)

            @block.sync
            def _(sp):
                with sp.Fori(0, NGROUPS - 1) as i:
                    sp.wait_ge(step, i * STEPS + STEPS)
                    sp.dma_start(out[0:(NT - NG) * P, :].rearrange("(t p) f -> p t f", p=P)[:, bass.ds(i * NG, NG), :], res[:]).then_inc(stored, 16)
                sp.wait_ge(step, NGROUPS * STEPS)
                sp.dma_start(out[(NT - NG) * P:(NT - 1) * P, :].rearrange("(t p) f -> p t f", p=P), res[:, 0:NG - 1, :]).then_inc(stored, 16)
                sp.dma_start(out[(NT - 1) * P:N, :], res[0:last, NG - 1, :]).then_inc(stored, 16)
                sp.wait_ge(stored, (NGROUPS + 1) * 16)


def gnn(nc, a, out):
    def dram(name, shape, dt=F32):
        return nc.dram_tensor(name, shape, dt, kind="Internal").ap()

    tables = {l.name: dram(l.name + "_table", [P * l.chunks, l.fields], I32) for l in LISTS}
    chunk_bucket = {l.name: dram(l.name + "_chunk_bucket", [P * l.jt], I32) for l in LISTS}
    hist = {l.name: dram(l.name + "_hist", [l.hi, LO]) for l in LISTS}
    ea = dram("ea", [P, BY_DST.chunks, D])
    rows = [dram(f"rows{i}", [NPAD, D]) for i in range(4)]
    T = dram("T", [D + 1, BY_SRC.buckets, P])
    sort_edges(nc, a["src"], a["dst"], tables, chunk_bucket, hist)
    with ExitStack() as keep:
        with ExitStack() as by_dst:
            s = load_shared(nc, keep, by_dst, a, tables, chunk_bucket)
            H = by_dst.enter_context(nc.sbuf_tensor("H", [P, NT, D], F32))
            gather_sum(nc, "l0", s, a["edge_attr_64"], s["edge_index"], False, "attr", ea)
            nodes(nc, "n0", s, "mlp", rows[0])
            gather_sum(nc, "l1a", s, rows[0], s["src_index"], True)
            nodes(nc, "n1a", s, "sage1", rows[1], H)
            gather_sum(nc, "l1b", s, rows[1], s["src_index"], True)
            nodes(nc, "n1b", s, "sage2", rows[2], H)
            gather_sum(nc, "l2", s, rows[2], s["src_index"], False, "message", ea)
            graph_norm(nc, s, H, rows[3])
        score_tables(nc, s, T)
        load_src_list(nc, keep, s, tables, chunk_bucket)
        attention(nc, s, rows[3], T)
        attention_out(nc, s, out)


_INS = ["x", "src", "dst", "edge_attr_64", "node_vec"] + [n for n, _ in WEIGHTS]


def kernel(**inputs):
    import numpy as _np
    import concourse.bacc as _bacc
    from concourse import mybir as _mybir
    from concourse.bass_utils import run_bass_kernel_spmd as _run

    nc = _bacc.Bacc("TRN2", target_bir_lowering=False, num_devices=1)
    arrays, aps = {}, {}
    for name in _INS:
        a = _np.ascontiguousarray(inputs[name])
        arrays[f"in_{name}_dram"] = a
        aps[name] = nc.dram_tensor(f"in_{name}_dram", a.shape, _mybir.dt.from_np(a.dtype), kind="ExternalInput").ap()
    out = nc.dram_tensor("out_0_dram", (N, D), _mybir.dt.float32, kind="ExternalOutput").ap()
    gnn(nc, aps, out)
    r = _run(nc, [arrays], core_ids=[0])
    return r.results[0]["out_0_dram"]
```

```python
from contextlib import ExitStack

import concourse.bass as bass
from concourse import mybir

F32 = mybir.dt.float32
BF16 = mybir.dt.bfloat16
I32 = mybir.dt.int32
ALU = mybir.AluOpType
ACT = mybir.ActivationFunctionType
AX = mybir.AxisListType

P = 128
N = 12500
D = 64
E = 212500
NT = -(-N // P)
NPAD = NT * P
TILES = -(-E // (P * 8)) * 8
LASTROW = E - (P - 1) * TILES
LO = 16


class List:

    def __init__(self, name, shift, fields):
        self.name, self.shift, self.width = name, shift, 1 << shift
        self.buckets = (NPAD >> shift) + 1
        self.hi = -(-self.buckets // LO)
        self.bins = self.hi * LO
        self.chunks = -(-(TILES + self.buckets) // 32) * 32
        self.jt = -(-self.chunks // P)
        self.fields = fields


BY_DST = List("dst", 7, 4)
BY_SRC = List("src", 5, 2)
LISTS = (BY_DST, BY_SRC)
J = 8
GB = 4
NG = 7
NGROUPS = NT // NG
LN_EPS = 1e-5
HEADS = 4
NO_SCORE = -1e30
NO_MAX = -1e29
ABSENT = 4096


class Count:

    def __init__(self, sem, start=0):
        self.sem, self.start, self.n = sem, start, 0

    def inc(self, ins):
        ins.then_inc(self.sem, 1)
        self.n += 1

    def wait(self, eng):
        eng.wait_ge(self.sem, self.start + self.n)


def load_flag(eng, flag, name):
    reg = eng.alloc_register(name)
    eng.reg_load(reg, flag[0:1, 0:1])
    return reg


def sort_edges(nc, src, dst, tables, chunk_bucket, l_hist, edge_rows, chunk_start, chunk_from, unsorted):
    with ExitStack() as ctx:
        def sb(name, shape, dt):
            return ctx.enter_context(nc.sbuf_tensor("sort_" + name, shape, dt))

        def ps(name, shape, dt=F32):
            return ctx.enter_context(nc.psum_tensor("sort_" + name, shape, dt))

        def sem(name):
            return ctx.enter_context(nc.semaphore("sort_" + name))

        node = {"dst": sb("dst", [P, TILES], I32), "src": sb("src", [P, TILES], I32)}
        other = {"dst": node["src"], "src": node["dst"]}
        bucket = {l.name: sb(l.name + "_bucket", [P, TILES], F32) for l in LISTS}
        row = {l.name: sb(l.name + "_row", [P, TILES, l.fields], I32) for l in LISTS}
        tmp = sb("tmp", [P, TILES], I32)
        after = sb("after", [P, TILES], I32)
        falls = sb("falls", [P, 1], F32)
        flags = sb("flags", [P, 2], F32)
        ones = sb("ones", [P, P], F32)
        falls_ps = ps("falls_ps", [P, 1])
        pads_ps = ps("pads_ps", [P, BY_DST.bins])
        pads = sb("pads", [P, BY_DST.bins], F32)
        pads_before = sb("pads_before", [P, BY_DST.jt], F32)
        start_f = sb("start_f", [P, 2, BY_DST.jt], F32)
        start_i = sb("start_i", [P, BY_DST.jt], I32)
        HG = TILES // 16
        HU = 8
        parts = {l.name: (sb(l.name + "_hi", [P, TILES], BF16), sb(l.name + "_lo", [P, TILES], BF16)) for l in LISTS}
        his, los = sum(l.hi for l in LISTS), LO * len(LISTS)
        first_hi = {"dst": 0, "src": BY_DST.hi}
        first_lo = {"dst": 0, "src": LO}
        hot_hi = [sb(f"hot_hi{k}", [P, HG, his], BF16) for k in range(2)]
        hot_lo = [sb(f"hot_lo{k}", [P, HG, los], BF16) for k in range(2)]
        iota_i = sb("iota_i", [P, 512], I32)
        iota_b = sb("iota_b", [P, 32], BF16)
        iota_f = sb("iota_f", [P, 512], F32)
        rowj = sb("rowj", [P, 32], F32)
        rowj_i = sb("rowj_i", [P, 32], I32)
        before = sb("before", [P, P], BF16)
        notbefore = sb("notbefore", [P, P], BF16)
        ones_row = sb("ones_row", [1, P], F32)
        hist = ps("hist", [his, los])
        hist_sb = sb("hist_sb", [his, los], F32)
        line = {l.name: sb(l.name + "_line", [1, 6, l.bins], F32) for l in LISTS}
        line_i = {l.name: sb(l.name + "_linei", [1, l.bins], I32) for l in LISTS}
        rank = {l.name: ps(l.name + "_rank", [P, l.bins]) for l in LISTS}
        ends_ps = {l.name: ps(l.name + "_endsps", [P, l.bins]) for l in LISTS}
        ends = {l.name: sb(l.name + "_ends", [P, l.bins], F32) for l in LISTS}
        of_chunk = {l.name: sb(l.name + "_ofchunk", [P, l.jt], F32) for l in LISTS}
        of_chunk_i = {l.name: sb(l.name + "_ofchunki", [P, l.jt], I32) for l in LISTS}
        G = 8
        onehot = {l.name: sb(l.name + "_onehot", [P, 2, G, l.bins], BF16) for l in LISTS}
        prod = {l.name: sb(l.name + "_prod", [P, l.bins], F32) for l in LISTS}
        slot = {l.name: sb(l.name + "_slot", [P, G], F32) for l in LISTS}
        slot_i = {l.name: sb(l.name + "_sloti", [P, 3, G], I32) for l in LISTS}
        at = {l.name: [sb(f"{l.name}_at{k}", [P, G], I32) for k in range(2)] for l in LISTS}
        stage = {l.name: [sb(f"{l.name}_stage{k}", [P, G, l.fields], I32) for k in range(2)] for l in LISTS}
        empty = sb("empty", [P, max(l.chunks * l.fields for l in LISTS)], I32)
        cleared = sem("cleared")
        loaded = sem("loaded")
        consts = sem("consts")
        prep = sem("prep")
        hot_ready = sem("hot_ready")
        hot_used = sem("hot_used")
        hist_done = sem("hist_done")
        spilled = sem("spilled")
        line_in = sem("line_in")
        line_ready = sem("line_ready")
        filled = sem("filled")
        ends_done = sem("ends_done")
        table_ready = sem("table_ready")
        onehot_ready = sem("onehot_ready")
        rank_ready = {l.name: sem(l.name + "_rank_ready") for l in LISTS}
        rank_read = {l.name: sem(l.name + "_rank_read") for l in LISTS}
        tile_summed = sem("tile_summed")
        slot_step = sem("slot_step")
        scattered = {l.name: [sem(f"{l.name}_scattered{k}") for k in range(2)] for l in LISTS}
        falls_ready = sem("falls_ready")
        falls_done = sem("falls_done")
        flag_ready = sem("flag_ready")
        TABLE_STEPS = sum(2 + l.jt for l in LISTS) + 2 + 1 + BY_DST.jt + 3
        CONSTS = 8
        LINE_STEPS = 9 * len(LISTS)
        SLOT_STEPS = 5

        with nc.Block() as block:
            @block.sync
            def _(sp):
                sp.wait_ge(cleared, 3)
                sp.dma_start(after[0:P - 1, :], dst[1:1 + (P - 1) * TILES].rearrange("(p t) -> p t", t=TILES)).then_inc(loaded, 16)
                sp.dma_start(after[P - 1:P, 0:LASTROW - 1], dst[(P - 1) * TILES + 1:E].rearrange("(p t) -> p t", p=1)).then_inc(loaded, 16)
                for name, dram in (("dst", dst), ("src", src)):
                    sp.dma_start(node[name][0:P - 1, :], dram[0:(P - 1) * TILES].rearrange("(p t) -> p t", t=TILES)).then_inc(loaded, 16)
                    sp.dma_start(node[name][P - 1:P, 0:LASTROW], dram[(P - 1) * TILES:E].rearrange("(p t) -> p t", p=1)).then_inc(loaded, 16)

            @block.gpsimd
            def _(pool):
                c = Count(consts)
                c.inc(pool.iota(iota_i[:], [[1, 512]], base=0, channel_multiplier=0))
                c.inc(pool.iota(rowj_i[:], [[P, 32]], base=0, channel_multiplier=1))
                c.inc(pool.iota(tmp[:], [[1, TILES]], base=0, channel_multiplier=TILES))
                c.inc(pool.memset(before[:], 1.0))
                c.inc(pool.memset(notbefore[:], 1.0))
                c.wait(pool)
                c.inc(pool.affine_select(out=before[:], in_=before[:], compare_op=ALU.is_ge, fill=0.0, base=-1, pattern=[[1, P]], channel_multiplier=-1))
                c.inc(pool.affine_select(out=notbefore[:], in_=notbefore[:], compare_op=ALU.is_ge, fill=0.0, base=0, pattern=[[-1, P]], channel_multiplier=1))
                c.inc(pool.memset(ones_row[:], 1.0))

            @block.vector
            def _(dve):
                for name in ("dst", "src"):
                    dve.memset(node[name][:], NPAD).then_inc(cleared, 1)
                dve.memset(after[:], NPAD).then_inc(cleared, 1)
                dve.wait_ge(consts, 3)
                p = Count(prep)
                p.inc(dve.tensor_copy(iota_b[:], iota_i[:, 0:32]))
                p.inc(dve.tensor_copy(iota_f[:], iota_i[:]))
                p.inc(dve.tensor_copy(rowj[:], rowj_i[:]))
                p.inc(dve.tensor_scalar(row["dst"][:, :, 2:3], tmp[:].unsqueeze(2), E - 1, None, ALU.min))
                dve.wait_ge(loaded, 96)
                p.inc(dve.memset(ones[:], 1.0))
                p.inc(dve.tensor_tensor(after[:], node["dst"][:], after[:], ALU.is_gt))
                p.wait(dve)
                dve.tensor_reduce(falls[:], after[:], AX.X, ALU.max).then_inc(falls_ready, 1)
                p.wait(dve)
                for l in LISTS:
                    key, oth, w = node[l.name], other[l.name], row[l.name]
                    p.inc(dve.tensor_scalar(w[:, :, 0:1], oth[:].unsqueeze(2), N - 1, None, ALU.min))
                    p.inc(dve.tensor_scalar(w[:, :, 1:2], key[:].unsqueeze(2), l.width - 1, None, ALU.bitwise_and))
                    p.inc(dve.tensor_scalar(tmp[:], key[:], l.shift, None, ALU.logical_shift_right))
                    p.wait(dve)
                    p.inc(dve.tensor_copy(bucket[l.name][:], tmp[:]))
                    if l is BY_DST:
                        p.inc(dve.tensor_copy(w[:, :, 3:4], tmp[:].unsqueeze(2)))
                    p.wait(dve)
                    p.inc(dve.tensor_scalar(tmp[:], tmp[:], LO - 1, None, ALU.bitwise_and))
                    p.wait(dve)
                    p.inc(dve.tensor_copy(parts[l.name][1][:], tmp[:]))
                    p.wait(dve)
                    p.inc(dve.tensor_scalar(tmp[:], key[:], l.shift + 4, None, ALU.logical_shift_right))
                    p.wait(dve)
                    p.inc(dve.tensor_copy(parts[l.name][0][:], tmp[:]))
                    p.wait(dve)
                def count_onehots(i, k):
                    for l in LISTS:
                        for part, width, to in ((parts[l.name][0], l.hi, hot_hi[k][:, :, first_hi[l.name]:first_hi[l.name] + l.hi]),
                                                (parts[l.name][1], LO, hot_lo[k][:, :, first_lo[l.name]:first_lo[l.name] + LO])):
                            dve.tensor_tensor(to, part[:, bass.ds(i * HG, HG)].unsqueeze(2).broadcast_to([P, HG, width]),
                                              iota_b[:, 0:width].unsqueeze(1).broadcast_to([P, HG, width]), ALU.is_equal).then_inc(hot_ready, 1)

                count_onehots(0, 0)
                count_onehots(1, 1)
                with dve.Fori(2, 15, 2) as i:
                    for k in range(2):
                        dve.wait_ge(hot_used, (i + k - 1) * HG)
                        count_onehots(i + k, k)
                dve.wait_ge(hot_used, TILES)
                dve.tensor_copy(hist_sb[:], hist[:]).then_inc(hist_done, 1)

                dve.wait_ge(falls_done, 1)
                dve.tensor_scalar(unsorted[:], falls_ps[0:1, :], 1.0, None, ALU.min).then_inc(flag_ready, 1)
                dve.tensor_scalar(flags[:, 0:1], falls_ps[:], 0.0, None, ALU.is_equal).then_inc(flag_ready, 1)

                dve.wait_ge(line_in, 32)
                p = Count(line_ready)
                for l in LISTS:
                    ln = line[l.name]
                    p.inc(dve.tensor_copy(line_i[l.name][:], ln[:, 0, :]))
                    p.wait(dve)
                    p.inc(dve.tensor_scalar(line_i[l.name][:], line_i[l.name][:], P - 1, None, ALU.add))
                    p.wait(dve)
                    p.inc(dve.tensor_scalar(line_i[l.name][:], line_i[l.name][:], 7, None, ALU.logical_shift_right))
                    p.wait(dve)
                    p.inc(dve.tensor_copy(ln[:, 1, :], line_i[l.name][:]))
                    p.inc(dve.memset(ln[:, 4, :], 0.0))
                    p.wait(dve)
                    p.inc(dve.tensor_tensor_scan(ln[:, 2, :], ln[:, 1, :], ln[:, 4, :], 0.0, ALU.add, ALU.add))
                    p.wait(dve)
                    p.inc(dve.tensor_tensor(ln[:, 3, :], ln[:, 2, :], ln[:, 1, :], ALU.subtract))
                    p.wait(dve)
                    p.inc(dve.tensor_scalar(ln[:, 3, :], ln[:, 3, :], float(P), None, ALU.mult))
                    p.inc(dve.scalar_tensor_tensor(ln[:, 5, :], ln[:, 1, :], float(P), ln[:, 0, :], ALU.mult, ALU.subtract))
                dve.wait_ge(ends_done, 3)
                q = Count(table_ready)
                q.inc(dve.tensor_copy(pads[:], pads_ps[:]))
                for l in LISTS:
                    q.inc(dve.tensor_copy(ends[l.name][:], ends_ps[l.name][:]))
                    q.wait(dve)
                    for j in range(l.jt):
                        q.inc(dve.tensor_scalar(prod[l.name][:], ends[l.name][:], rowj[:, j:j + 1], 0.0, ALU.is_le, ALU.add, accum_out=of_chunk[l.name][:, j:j + 1]))
                        q.wait(dve)
                        if l is BY_DST:
                            q.inc(dve.tensor_tensor_reduce(prod[l.name][:], prod[l.name][:], pads[:], 1.0, 0.0, ALU.mult, ALU.add, pads_before[:, j:j + 1]))
                            q.wait(dve)
                    q.inc(dve.tensor_scalar(of_chunk_i[l.name][:], of_chunk[l.name][:], float(l.buckets - 1), None, ALU.min))
                q.wait(dve)
                q.inc(dve.scalar_tensor_tensor(start_f[:, 0, :], rowj[:, 0:BY_DST.jt], float(P), pads_before[:], ALU.mult, ALU.subtract))
                q.wait(dve)
                dve.wait_ge(flag_ready, 2)
                q.inc(dve.tensor_scalar(start_f[:, 1, :], start_f[:, 0, :], flags[:, 0:1], None, ALU.mult))
                q.inc(dve.tensor_scalar(start_i[:], start_f[:, 0, :], float(E - P), None, ALU.min))
                empty_v = empty[:].rearrange("p (c f) -> p c f", f=2)
                q.inc(dve.memset(empty[:], 0))
                q.wait(dve)
                q.inc(dve.memset(empty_v[:, :, 1:2], ABSENT))
                assert q.n == TABLE_STEPS, q.n

                def rank_onehots(i, k, lists):
                    for l in lists:
                        dve.tensor_tensor(onehot[l.name][:, k], bucket[l.name][:, bass.ds(i * G, G)].unsqueeze(2).broadcast_to([P, G, l.bins]),
                                          iota_f[:, 0:l.bins].unsqueeze(1).broadcast_to([P, G, l.bins]), ALU.is_equal).then_inc(onehot_ready, 1)

                def rank_group(i, k, lists):
                    steps = Count(slot_step, i * (SLOT_STEPS * len(lists)))
                    for t in range(G):
                        for l in lists:
                            dve.wait_ge(rank_ready[l.name], i * G + t + 1)
                            dve.tensor_tensor_reduce(prod[l.name][:], onehot[l.name][:, k, t, :], rank[l.name][:], 1.0, 0.0, ALU.mult, ALU.add,
                                                     slot[l.name][:, t:t + 1]).then_inc(rank_read[l.name], 1)
                    for l in lists:
                        si = slot_i[l.name]
                        dve.wait_ge(rank_read[l.name], i * G + G)
                        steps.inc(dve.tensor_copy(si[:, 0, :], slot[l.name][:]))
                        steps.wait(dve)
                        steps.inc(dve.tensor_scalar(si[:, 1, :], si[:, 0, :], P - 1, None, ALU.bitwise_and))
                        steps.inc(dve.tensor_scalar(si[:, 2, :], si[:, 0, :], 7, None, ALU.logical_shift_right))
                        steps.wait(dve)
                        steps.inc(dve.scalar_tensor_tensor(at[l.name][k][:], si[:, 1, :], float(l.chunks), si[:, 2, :], ALU.mult, ALU.add))
                        steps.wait(dve)
                        steps.inc(dve.tensor_copy(stage[l.name][k][:], row[l.name][:, bass.ds(i * G, G), :]))
                    assert steps.n == SLOT_STEPS * len(lists)

                GROUPS = TILES // G
                def ranks(lists):
                    tile = len(lists)
                    rank_onehots(0, 0, lists)
                    rank_onehots(1, 1, lists)
                    rank_group(0, 0, lists)
                    dve.wait_ge(tile_summed, tile * G)
                    rank_onehots(2, 0, lists)
                    rank_group(1, 1, lists)
                    with dve.Fori(2, GROUPS - 3, 2) as i:
                        for k in range(2):
                            dve.wait_ge(tile_summed, (i + k) * (tile * G))
                            rank_onehots(i + k + 1, 1 - k, lists)
                            for l in lists:
                                dve.wait_ge(scattered[l.name][k], i * 8 * G)
                            rank_group(i + k, k, lists)
                    for k in range(2):
                        i = GROUPS - 2 + k
                        if k == 0:
                            dve.wait_ge(tile_summed, i * tile * G)
                            rank_onehots(i + 1, 1, lists)
                        for l in lists:
                            dve.wait_ge(scattered[l.name][k], (GROUPS - 2) * 8 * G)
                        rank_group(i, k, lists)

                with dve.If_eq(load_flag(dve, unsorted, "unsorted_at_ranks"), 0):
                    ranks([BY_SRC])
                with dve.Else():
                    ranks(LISTS)

            @block.tensor
            def _(pe):
                def count_tile(k, t, first=False):
                    return pe.matmul(hist[:], hot_hi[k][:, bass.ds(t, 1), :].squeeze(1), hot_lo[k][:, bass.ds(t, 1), :].squeeze(1), start=first, stop=False, skip_group_check=True)

                def count_group(i, k, first=False):
                    pe.wait_ge(hot_ready, i * 4 + 4)
                    for t in range(HU):
                        ins = count_tile(k, t, first and t == 0)
                    ins.then_inc(hot_used, HU)
                    with pe.Fori(HU, HG - HU + 1, HU) as t:
                        for j in range(HU):
                            ins = count_tile(k, t + j)
                        ins.then_inc(hot_used, HU)

                pe.wait_ge(falls_ready, 1)
                pe.matmul(falls_ps[:], ones[:], falls[:], start=True, stop=True).then_inc(falls_done, 1)
                count_group(0, 0, True)
                count_group(1, 1)
                with pe.Fori(2, 15, 2) as i:
                    count_group(i, 0)
                    count_group(i + 1, 1)

                pe.wait_ge(consts, CONSTS)
                pe.wait_ge(line_ready, LINE_STEPS)
                for l in LISTS:
                    pe.matmul(ends_ps[l.name][:], ones_row[:], line[l.name][:, 2, :], start=True, stop=True).then_inc(ends_done, 1)
                pe.matmul(pads_ps[:], ones_row[:], line["dst"][:, 5, :], start=True, stop=True).then_inc(ends_done, 1)
                for l in LISTS:
                    pe.matmul(rank[l.name][:], ones_row[:], line[l.name][:, 3, :], start=True, stop=False, skip_group_check=True)

                def rank_group(i, k, lists):
                    pe.wait_ge(onehot_ready, i * len(lists) + len(lists))
                    for t in range(G):
                        for l in lists:
                            hot_t = onehot[l.name][:, k, t, :]
                            pe.matmul(rank[l.name][:], before[:], hot_t, start=False, stop=False, skip_group_check=True).then_inc(rank_ready[l.name], 1)
                        for l in lists:
                            hot_t = onehot[l.name][:, k, t, :]
                            pe.wait_ge(rank_read[l.name], i * G + t + 1)
                            pe.matmul(rank[l.name][:], notbefore[:], hot_t, start=False, stop=False, skip_group_check=True).then_inc(tile_summed, 1)

                def ranks(lists):
                    with pe.Fori(0, TILES // G, 2) as i:
                        rank_group(i, 0, lists)
                        rank_group(i + 1, 1, lists)

                pe.wait_ge(flag_ready, 2)
                with pe.If_eq(load_flag(pe, unsorted, "unsorted_at_ranks"), 0):
                    ranks([BY_SRC])
                with pe.Else():
                    ranks(LISTS)

            @block.sync
            def _(sp):
                sp.wait_ge(hist_done, 1)
                for l in LISTS:
                    h, w = first_hi[l.name], first_lo[l.name]
                    sp.dma_start(l_hist[l.name], hist_sb[h:h + l.hi, w:w + LO]).then_inc(spilled, 16)
                sp.wait_ge(spilled, 32)
                for l in LISTS:
                    sp.dma_start(line[l.name][:, 0, :], l_hist[l.name].rearrange("h l -> (h l)").unsqueeze(0)).then_inc(line_in, 16)
                sp.dma_start(edge_rows.rearrange("(p t) f -> p (t f)", p=P), row["dst"][:].rearrange("p t f -> p (t f)")).then_inc(filled, 16)
                sp.wait_ge(table_ready, TABLE_STEPS)
                sp.dma_start(chunk_start.rearrange("(j p) -> p j", p=P), start_i[:], allow_slow_non_contiguous=True).then_inc(filled, 16)
                sp.dma_start(chunk_from.rearrange("(j p) -> p j", p=P), start_f[:, 1, :], allow_slow_non_contiguous=True).then_inc(filled, 16)
                for l in LISTS:
                    sp.dma_start(tables[l.name].rearrange("(p c) f -> p (c f)", p=P), empty[:, 0:l.chunks * l.fields]).then_inc(filled, 16)
                    sp.dma_start(chunk_bucket[l.name].rearrange("(j p) -> p j", p=P), of_chunk_i[l.name][:], allow_slow_non_contiguous=True).then_inc(filled, 16)

            @block.gpsimd
            def _(pool):
                pool.wait_ge(filled, 16 * 7)
                pool.wait_ge(flag_ready, 2)

                def scatter_group(i, k, lists):
                    steps = SLOT_STEPS * len(lists)
                    pool.wait_ge(slot_step, i * steps + steps)
                    pool.nop(nofuse=True)
                    for t in range(G):
                        for l in lists:
                            pool.indirect_dma_start(tables[l.name], bass.IndirectOffsetOnAxis(ap=at[l.name][k][:, t:t + 1], axis=0),
                                                    stage[l.name][k][:, t, :], None).then_inc(scattered[l.name][k], 16)

                def scatter(lists):
                    with pool.Fori(0, TILES // G, 2) as i:
                        scatter_group(i, 0, lists)
                        scatter_group(i + 1, 1, lists)
                    for l in lists:
                        for k in range(2):
                            pool.wait_ge(scattered[l.name][k], TILES // G * 8 * G)

                flag = load_flag(pool, unsorted, "unsorted_at_scatter")
                with pool.If_eq(flag, 0):
                    scatter([BY_SRC])
                with pool.Else():
                    scatter(LISTS)



WEIGHTS = [
    ("L0_gnn_W0", (2 * D, 128)), ("L0_gnn_b0", (128,)), ("L0_gnn_W1", (128, 128)), ("L0_gnn_b1", (128,)),
    ("L0_gnn_W2", (128, D)), ("L0_gnn_b2", (D,)), ("L0_gnn_ln_g", (D,)), ("L0_gnn_ln_b", (D,)),
    ("L1_gnn_W1_l", (D, D)), ("L1_gnn_b1_l", (D,)), ("L1_gnn_W1_r", (D, D)),
    ("L1_gnn_W2_l", (D, D)), ("L1_gnn_b2_l", (D,)), ("L1_gnn_W2_r", (D, D)),
    ("L2_gnn_We2", (D, D)), ("L2_gnn_be2", (D,)), ("L2_gnn_Wm2", (D, D)), ("L2_gnn_bm2", (D,)),
    ("L2_gnn_eps2", (1,)), ("L2_gnn_gamma2", (D,)), ("L2_gnn_beta2", (D,)),
    ("L3_gnn_Wq", (D, 256)), ("L3_gnn_bq", (256,)), ("L3_gnn_Wk", (D, 256)), ("L3_gnn_bk", (256,)),
    ("L3_gnn_Wv", (D, 256)), ("L3_gnn_bv", (256,)), ("L3_gnn_Wo", (256, D)), ("L3_gnn_bo", (D,)),
]
ROWS = ("L0_gnn_b2", "L0_gnn_ln_g", "L0_gnn_ln_b", "L1_gnn_b1_l", "L1_gnn_b2_l", "L2_gnn_gamma2", "L2_gnn_beta2", "L3_gnn_bo")


def load_shared(nc, keep, by_dst, a, tables, chunk_bucket, edge_rows, chunk_start, chunk_from, unsorted):
    s = {}

    def sb(name, shape, dt=F32, stack=keep):
        s[name] = stack.enter_context(nc.sbuf_tensor(name, shape, dt))

    with ExitStack() as ctx:
        loaded = ctx.enter_context(nc.semaphore("shared_loaded"))
        cleared = ctx.enter_context(nc.semaphore("shared_cleared"))
        made = ctx.enter_context(nc.semaphore("shared_made"))
        transposed = ctx.enter_context(nc.semaphore("shared_transposed"))
        sb("X", [P, NT, D])
        sb("W0", [2 * D, 128])
        sb("W1", [128, 128])
        sb("W2", [128, D])
        sb("b0", [128, 1])
        sb("b1", [128, 1])
        sb("sage1", [2 * D, D])
        sb("sage2", [2 * D, D])
        sb("We", [D + 1, D])
        sb("Wm", [D + 1, D])
        sb("eps", [P, 1])
        sb("rows", [P, len(ROWS), D])
        sb("ident", [P, P])
        sb("ones", [P, P])
        sb("iota_row", [P, P])
        sb("Wq", [D + 1, HEADS * D])
        sb("Wk", [D + 1, HEADS * D])
        sb("Wv", [D + 1, HEADS * D])
        sb("Wo", [D, HEADS, D])
        sb("Wqk", [D + 1, HEADS, D + 1])
        sb("influence", [P, NT])
        sb("ln_eps", [P, 1])
        sb("acc", [P, BY_DST.buckets, D + 1], stack=by_dst)
        sb("src_index", [P, BY_DST.chunks + J], I32, stack=by_dst)
        sb("edge_index", [P, BY_DST.chunks + J], I32, stack=by_dst)
        sb("dst_local", [P, BY_DST.chunks], stack=by_dst)
        sb("dst_bucket", [1, BY_DST.jt * P], I32, stack=by_dst)
        sb("chunk_start", [1, BY_DST.jt * P], I32, stack=by_dst)
        s["unsorted"] = unsorted
        table_loaded = [ctx.enter_context(nc.semaphore(f"shared_table_loaded{k}")) for k in range(2)]
        table = ctx.enter_context(nc.sbuf_tensor("shared_table", [P, BY_DST.chunks, BY_DST.fields], I32))
        iota_i = ctx.enter_context(nc.sbuf_tensor("shared_iota", [P, P], I32))
        raw = ctx.enter_context(nc.sbuf_tensor("shared_raw", [D, 4, D], F32))
        flip = [ctx.enter_context(nc.psum_tensor(f"shared_flip{i}", [P, 512], F32)) for i in range(4)]
        flip_k = [ctx.enter_context(nc.psum_tensor(f"shared_flipk{i}", [D, 512], F32)) for i in range(2)]
        turned = [ctx.enter_context(nc.sbuf_tensor(f"shared_turned{i}", [D, HEADS, D + 1], F32)) for i in range(2)]
        both = ctx.enter_context(nc.psum_tensor("shared_both", [D + 1, HEADS, 128], F32))
        last = N - (NT - 1) * P
        n_loads = 2 + 1 + 5 + 4 + 4 + 1 + len(ROWS) + 6 + 1 + 2
        def load_chunks(eng, k):
            with eng.Fori(0, BY_DST.chunks - 3, 4) as c:
                for j in (k, k + 2):
                    e = eng.value_load(s["chunk_start"][0:1, bass.ds(c + j, 1)], min_val=0, max_val=E - P)
                    eng.dma_start(table[:, bass.ds(c + j, 1), :].squeeze(1), edge_rows[bass.ds(e, P), :]).then_inc(table_loaded[k], 16)

        with nc.Block() as block:
            @block.scalar
            def _(act):
                act.wait_ge(table_loaded[0], 16)
                with act.If_eq(load_flag(act, unsorted, "unsorted_at_act_load"), 0):
                    load_chunks(act, 1)
                    act.wait_ge(table_loaded[1], BY_DST.chunks // 2 * 16)

            @block.sync
            def _(sp):
                def load(to, frm, **how):
                    sp.dma_start(to, frm, **how).then_inc(loaded, 16)

                sp.wait_ge(cleared, 2)
                load(s["X"][:, 0:NT - 1, :], a["x"][0:(NT - 1) * P, :].rearrange("(t p) f -> p t f", p=P))
                load(s["X"][0:last, NT - 1, :], a["x"][(NT - 1) * P:N, :])
                sp.dma_start(s["chunk_start"][:], chunk_start.unsqueeze(0)).then_inc(table_loaded[0], 16)
                sp.wait_ge(table_loaded[0], 16)
                flag = load_flag(sp, unsorted, "unsorted_at_load")
                with sp.If_eq(flag, 0):
                    load_chunks(sp, 0)
                    sp.wait_ge(table_loaded[0], BY_DST.chunks // 2 * 16 + 16)
                    sp.wait_ge(table_loaded[1], BY_DST.chunks // 2 * 16)
                with sp.Else():
                    sp.dma_start(table[:], tables["dst"].rearrange("(p c) f -> p c f", p=P)).then_inc(table_loaded[1], 16)
                    sp.wait_ge(table_loaded[1], 16)
                load(s["dst_bucket"][:], chunk_bucket["dst"].unsqueeze(0))
                load(s["W0"][:], a["L0_gnn_W0"])
                load(s["W1"][:], a["L0_gnn_W1"])
                load(s["W2"][:], a["L0_gnn_W2"])
                load(s["b0"][:], a["L0_gnn_b0"].unsqueeze(1))
                load(s["b1"][:], a["L0_gnn_b1"].unsqueeze(1))
                for w, m, b in (("We", "L2_gnn_We2", "L2_gnn_be2"), ("Wm", "L2_gnn_Wm2", "L2_gnn_bm2")):
                    load(s[w][0:D, :], a[m])
                    load(s[w][D:D + 1, :], a[b].unsqueeze(0))
                for i, w in enumerate(("L1_gnn_W1_l", "L1_gnn_W1_r", "L1_gnn_W2_l", "L1_gnn_W2_r")):
                    load(raw[:, i, :], a[w])
                load(s["eps"][:], a["L2_gnn_eps2"].unsqueeze(0).broadcast_to([P, 1]))
                for i, w in enumerate(ROWS):
                    load(s["rows"][:, i, :], a[w].unsqueeze(0).broadcast_to([P, D]))
                for w in "qkv":
                    load(s["W" + w][0:D, :], a["L3_gnn_W" + w])
                    load(s["W" + w][D:D + 1, :], a["L3_gnn_b" + w].unsqueeze(0))
                load(s["Wo"][:], a["L3_gnn_Wo"].rearrange("(h d) f -> d h f", d=D))
                load(s["influence"][:, 0:NT - 1], a["node_vec"][0:(NT - 1) * P].rearrange("(t p) -> p t", p=P), allow_slow_non_contiguous=True)
                load(s["influence"][0:last, NT - 1:NT], a["node_vec"][(NT - 1) * P:N].unsqueeze(1))
                sp.wait_ge(loaded, 16 * n_loads)

            @block.gpsimd
            def _(pool):
                c = Count(made)
                c.inc(pool.iota(iota_i[:], [[1, P]], base=0, channel_multiplier=0))
                c.inc(pool.memset(s["ones"][:], 1.0))
                c.wait(pool)
                c.inc(pool.affine_select(out=s["ident"][:], in_=s["ones"][:], compare_op=ALU.is_equal, fill=0.0, base=0,
                                         pattern=[[-1, P]], channel_multiplier=1))

            @block.tensor
            def _(pe):
                pe.wait_ge(made, 3)
                pe.wait_ge(loaded, 16 * n_loads)
                for i in range(4):
                    pe.transpose(flip[i][0:D, 0:D], raw[:, i, :], s["ident"][0:D, 0:D]).then_inc(transposed, 1)
                for i, w in enumerate(("Wq", "Wk")):
                    for h in range(HEADS):
                        pe.matmul(flip_k[i][:, h * 128:h * 128 + D + 1], s[w][:, h * D:(h + 1) * D], s["ident"][0:D + 1, 0:D + 1], start=True, stop=True).then_inc(transposed, 1)
                pe.wait_ge(cleared, 7 + 2 + 2 * HEADS)
                for h in range(HEADS):
                    pe.matmul(both[:, h, 0:D + 1], turned[0][:, h, :], turned[1][:, h, :], start=True, stop=True).then_inc(transposed, 1)

            @block.vector
            def _(dve):
                dve.memset(s["X"][:], 0.0).then_inc(cleared, 1)
                dve.memset(s["influence"][:], 0.0).then_inc(cleared, 1)
                dve.memset(s["ln_eps"][:], LN_EPS).then_inc(cleared, 1)
                dve.wait_ge(made, 3)
                dve.tensor_copy(s["iota_row"][:], iota_i[:]).then_inc(cleared, 1)
                dve.wait_ge(loaded, 16 * n_loads)
                for index in ("src_index", "edge_index"):
                    dve.memset(s[index][:, BY_DST.chunks:], 0).then_inc(cleared, 1)
                dve.tensor_copy(s["src_index"][:, 0:BY_DST.chunks], table[:, :, 0:1].squeeze(2)).then_inc(cleared, 1)
                dve.tensor_copy(s["dst_local"][:], table[:, :, 1:2].squeeze(2)).then_inc(cleared, 1)
                dve.tensor_copy(s["edge_index"][:, 0:BY_DST.chunks], table[:, :, 2:3].squeeze(2)).then_inc(cleared, 1)
                dve.wait_ge(transposed, 4 + 2 * HEADS)
                for i in range(2):
                    for h in range(HEADS):
                        dve.tensor_copy(turned[i][:, h, :], flip_k[i][:, h * 128:h * 128 + D + 1]).then_inc(cleared, 1)
                dve.wait_ge(transposed, 4 + 3 * HEADS)
                dve.tensor_copy(s["Wqk"][:], both[:, :, 0:D + 1]).then_inc(cleared, 1)
                for i in range(4):
                    dve.tensor_copy(s[("sage1", "sage2")[i // 2]][(i % 2) * D:(i % 2) * D + D, :], flip[i][0:D, 0:D]).then_inc(cleared, 1)
                dve.wait_ge(cleared, 14 + 2 * HEADS)
        CW = BY_DST.chunks // 4
        line = ctx.enter_context(nc.sbuf_tensor("slots_line", [1, 2, BY_DST.jt * P], F32))
        ones_row = ctx.enter_context(nc.sbuf_tensor("slots_ones", [1, P], F32))
        own = ctx.enter_context(nc.sbuf_tensor("slots_own", [P, 2, BY_DST.chunks], F32))
        line_ready = ctx.enter_context(nc.semaphore("slots_line_ready"))
        spread = ctx.enter_context(nc.semaphore("slots_spread"))
        compared = ctx.enter_context(nc.semaphore("slots_compared"))
        wide = flip[0:2]
        with nc.Block() as block:
            @block.sync
            def _(sp):
                sp.dma_start(line[:, 1, :], chunk_from.unsqueeze(0)).then_inc(loaded, 16)

            @block.tensor
            def _(pe):
                pe.wait_ge(line_ready, 2)
                pe.wait_ge(loaded, 16 * n_loads + 16)
                for n in range(8):
                    if n >= 2:
                        pe.wait_ge(compared, n - 1)
                    pe.matmul(wide[n % 2][:, 0:CW], ones_row[:], line[:, n // 4, (n % 4) * CW:(n % 4 + 1) * CW], start=True, stop=True).then_inc(spread, 1)

            @block.vector
            def _(dve):
                dve.tensor_copy(line[:, 0, :], s["dst_bucket"][:]).then_inc(line_ready, 1)
                dve.memset(ones_row[:], 1.0).then_inc(line_ready, 1)
                for n in range(8):
                    dve.wait_ge(spread, n + 1)
                    chunks = slice((n % 4) * CW, (n % 4 + 1) * CW)
                    field = (3, 2)[n // 4]
                    dve.tensor_tensor(own[:, n // 4, chunks], table[:, chunks, field:field + 1].squeeze(2), wide[n % 2][:, 0:CW],
                                      (ALU.is_equal, ALU.is_ge)[n // 4]).then_inc(compared, 1)
                dve.wait_ge(compared, 8)
                c = Count(compared, 8)
                c.inc(dve.tensor_tensor(own[:, 0, :], own[:, 0, :], own[:, 1, :], ALU.mult))
                c.wait(dve)
                c.inc(dve.tensor_scalar(own[:, 0, :], own[:, 0, :], -float(ABSENT), float(ABSENT), ALU.mult, ALU.add))
                c.wait(dve)
                c.inc(dve.tensor_tensor(s["dst_local"][:], s["dst_local"][:], own[:, 0, :], ALU.add))
                c.wait(dve)
    return s


def gather_sum(nc, name, s, rows, index, counted, edge=None, ea=None):
    width = D + 1 if counted else D
    groups = BY_DST.chunks // J
    with ExitStack() as ctx:
        def sb1(n, shape, dt=F32):
            return ctx.enter_context(nc.sbuf_tensor(f"{name}_{n}", shape, dt))

        def sb(n, shape, dt=F32):
            return [sb1(f"{n}{k}", shape, dt) for k in range(2)]

        def ps(n, shape):
            return [ctx.enter_context(nc.psum_tensor(f"{name}_{n}{k}", shape, F32)) for k in range(2)]

        def sem(n):
            return ctx.enter_context(nc.semaphore(f"{name}_{n}"))

        idx = [sb1(f"idx{k}", [P, J], I32) for k in range(GB)]
        got = [sb1(f"got{k}", [P, J, width]) for k in range(GB)]
        onehot = sb("onehot", [P, J, P])
        banks = 2 if counted else 1
        per_bank = J // banks
        total = ps("total", [P, banks, 512])
        idx_copied = sem("idx_copied")
        gathered = [sem(f"gathered{b}") for b in range(GB)]
        onehot_ready = sem("onehot_ready")
        summed = sem("summed")
        added = sem("added")
        started = sem("started")
        if edge:
            flipped = ps("flipped", [D, 512])
            turned = sb("turned", [D + 1, J, P])
            product = ps("product", [P, J, D])
            made = sb("made", [P, J, D])
            flip_ready = sem("flip_ready")
            flip_used = sem("flip_used")
            product_ready = sem("product_ready")
            made_ready = sem("made_ready")
            ea_moved = [sem(f"ea_moved{k}") for k in range(2)]
        if edge == "message":
            attr = sb("attr", [P, J, D])

        def per_group(run):
            def go(eng):
                for b in range(GB):
                    run(b, b, b % 2, b < 2)
                with eng.Fori(GB, groups - GB + 1, GB) as g:
                    for b in range(GB):
                        run(g + b, b, b % 2, False)
            return go

        def dma_count(g, k, n, buffers=2):
            return (g - k) * (16 * n // buffers) + 16 * n

        def load_consecutive(eng, parity):
            def group(g, b, k, first):
                if k != parity:
                    return
                if not isinstance(g, int) or g > 3:
                    eng.wait_ge(summed, g - 3)
                for t in range(J):
                    e = eng.value_load(s["chunk_start"][0:1, bass.ds(g * J + t, 1)], min_val=0, max_val=E - P)
                    eng.dma_start(got[b][:, t, 0:D], rows[bass.ds(e, P), :]).then_inc(gathered[b], 16)
            return group

        with nc.Block() as block:
            @block.gpsimd
            def _(pool):
                def copy_index(g, b):
                    pool.tensor_copy(idx[b][:], index[:, bass.ds(g * J, J)]).then_inc(idx_copied, 1)

                def group(g, b, k, first):
                    if not isinstance(g, int) or g > 2:
                        pool.wait_ge(summed, g - 2)
                    copy_index(g + 1, (b + 1) % GB)
                    pool.wait_ge(idx_copied, g + 1)
                    pool.nop(nofuse=True)
                    for t in range(J):
                        pool.indirect_dma_start(got[b][:, t, 0:D], None, rows, bass.IndirectOffsetOnAxis(ap=idx[b][:, t:t + 1], axis=0)).then_inc(gathered[b], 16)

                if edge == "attr":
                    with pool.If_eq(load_flag(pool, s["unsorted"], "unsorted_at_gather"), 0):
                        per_group(load_consecutive(pool, 1))(pool)
                    with pool.Else():
                        copy_index(0, 0)
                        per_group(group)(pool)
                else:
                    copy_index(0, 0)
                    per_group(group)(pool)

            @block.tensor
            def _(pe):
                pe.wait_ge(started, 1 + GB * counted + 2 * bool(edge))

                def group(g, b, k, first):
                    pe.wait_ge(gathered[b], dma_count(g, b, J, GB))
                    if edge == "message":
                        pe.wait_ge(ea_moved[k], dma_count(g, k, 1))
                    if edge:
                        for h in range(2):
                            if not (first and k == 0):
                                pe.wait_ge(flip_used, 2 * g - 1 + h)
                            for t in range(4 * h, 4 * h + 4):
                                to = flipped[h][:, (t - 4 * h) * P:(t - 4 * h + 1) * P]
                                ins = pe.matmul(to, got[b][:, t, 0:D], s["ident"][:], start=True, stop=edge == "attr")
                                if edge == "message":
                                    ins = pe.matmul(to, attr[k][:, t, :], s["ident"][:], start=False, stop=True)
                            ins.then_inc(flip_ready, 1)
                        if not first:
                            pe.wait_ge(made_ready, g - 1)
                        for h in range(2):
                            pe.wait_ge(flip_used, 2 * g + 1 + h)
                            for t in range(4 * h, 4 * h + 4):
                                ins = pe.matmul(product[k][:, t, :], turned[k][:, t, :], s["We" if edge == "attr" else "Wm"][:], start=True, stop=True)
                        ins.then_inc(product_ready, 1)
                    pe.wait_ge(onehot_ready, g + 1)
                    if not first:
                        pe.wait_ge(added, J * (g - 1))
                    if edge == "message":
                        pe.wait_ge(made_ready, g + 1)
                    for t in range(J):
                        what = made[k][:, t, :] if edge == "message" else got[b][:, t, :]
                        at = (t % per_bank) * width
                        ins = pe.matmul(total[k][:, t // per_bank, at:at + width], onehot[k][:, t, :], what, start=True, stop=True)
                    ins.then_inc(summed, 1)

                per_group(group)(pe)

            @block.vector
            def _(dve):
                dve.memset(s["acc"][:], 0.0).then_inc(started, 1)
                if counted:
                    for b in range(GB):
                        dve.memset(got[b][:, :, D:D + 1], 1.0).then_inc(started, 1)
                if edge:
                    for k in range(2):
                        dve.memset(turned[k][D:D + 1, :, :], 1.0).then_inc(started, 1)
                dve.wait_ge(started, 1 + GB * counted + 2 * bool(edge))

                def compare(g, k):
                    dve.tensor_tensor(onehot[k][:], s["dst_local"][:, bass.ds(g * J, J)].unsqueeze(2).broadcast_to([P, J, P]),
                                      s["iota_row"][:].unsqueeze(1).broadcast_to([P, J, P]), ALU.is_equal).then_inc(onehot_ready, 1)

                def add(g, k):
                    buckets = [dve.value_load(s["dst_bucket"][0:1, bass.ds(g * J + t, 1)], min_val=0, max_val=BY_DST.buckets - 1) for t in range(J)]
                    dve.wait_ge(summed, g + 1)
                    for t in range(J):
                        if not (isinstance(g, int) and g == 0 and t == 0):
                            dve.wait_ge(added, g * J + t)
                        at = (t % per_bank) * width
                        to = s["acc"][:, bass.ds(buckets[t], 1), 0:width].squeeze(1)
                        dve.tensor_tensor(to, to, total[k][:, t // per_bank, at:at + width], ALU.add).then_inc(added, 1)

                def group(g, b, k, first):
                    if not first:
                        dve.wait_ge(summed, g - 1)
                    compare(g, k)
                    add(g, k)

                per_group(group)(dve)

            if edge:
                @block.scalar
                def _(act):
                    act.wait_ge(started, 1 + GB * counted + 2)

                    def group(g, b, k, first):
                        for h in range(2):
                            act.wait_ge(flip_ready, 2 * g + 1 + h)
                            if not first and h == 0:
                                act.wait_ge(product_ready, g - 1)
                            act.activation(turned[k][0:D, 4 * h:4 * h + 4, :].rearrange("d t p -> d (t p)"), flipped[h][:],
                                           ACT.Copy if edge == "attr" else ACT.Relu).then_inc(flip_used, 1)
                        act.wait_ge(product_ready, g + 1)
                        if not first:
                            if edge == "attr":
                                act.wait_ge(ea_moved[k], dma_count(g - 2, k, 1))
                            else:
                                act.wait_ge(summed, g - 1)
                        act.activation(made[k][:], product[k][:], ACT.Silu).then_inc(made_ready, 1)

                    per_group(group)(act)

                @block.sync
                def _(sp):
                    def store(g, k):
                        sp.wait_ge(made_ready, g + 1)
                        sp.dma_start(ea[:, bass.ds(g * J, J), :], made[k][:]).then_inc(ea_moved[k], 16)

                    def store_group(g, b, k, first):
                        store(g, k)

                    load_even = load_consecutive(sp, 0)

                    def load_and_store_group(g, b, k, first):
                        load_even(g, b, k, first)
                        if not first:
                            store(g - 2, k)

                    def load_group(g, b, k, first):
                        if not first:
                            sp.wait_ge(flip_used, 2 * g - 2)
                        sp.dma_start(attr[k][:], ea[:, bass.ds(g * J, J), :]).then_inc(ea_moved[k], 16)

                    if edge == "attr":
                        flag = load_flag(sp, s["unsorted"], "unsorted_at_gather")
                        with sp.If_eq(flag, 0):
                            per_group(load_and_store_group)(sp)
                            for g in (groups - 2, groups - 1):
                                store(g, g % 2)
                        with sp.Else():
                            per_group(store_group)(sp)
                        for k in range(2):
                            sp.wait_ge(ea_moved[k], groups // 2 * 16)
                    else:
                        per_group(load_group)(sp)



def row(s, name, n):
    return s["rows"][:, ROWS.index(name), :].unsqueeze(1).broadcast_to([P, n, D])


class Roots:

    def __init__(self, ctx, nc, name):
        self.asked = ctx.enter_context(nc.semaphore(name + "_var_ready"))
        self.given = ctx.enter_context(nc.semaphore(name + "_root_ready"))


NORM_STEPS = 6


def layer_norm(dve, c, v, sq, stat, out, roots, n_root):
    n = v.shape[1]
    c.wait(dve)
    c.inc(dve.tensor_reduce(stat[:, 0, :], v, AX.X, ALU.add))
    c.wait(dve)
    c.inc(dve.tensor_scalar(stat[:, 1, :], stat[:, 0, :], 1.0 / D, None, ALU.mult))
    c.wait(dve)
    c.inc(dve.tensor_tensor(v, v, stat[:, 1, :].unsqueeze(2).broadcast_to([P, n, D]), ALU.subtract))
    c.wait(dve)
    c.inc(dve.tensor_tensor(sq, v, v, ALU.mult))
    c.wait(dve)
    dve.tensor_reduce(stat[:, 2, :], sq, AX.X, ALU.add).then_inc(roots.asked, 1)
    dve.wait_ge(roots.given, n_root + 1)
    c.inc(dve.reciprocal(stat[:, 3, :], stat[:, 3, :]))
    c.wait(dve)
    c.inc(dve.tensor_tensor(out, v, stat[:, 3, :].unsqueeze(2).broadcast_to([P, n, D]), ALU.mult))


def norm_root(act, s, stat, roots, n_root):
    act.wait_ge(roots.asked, n_root + 1)
    act.activation(stat[:, 3, :], stat[:, 2, :], ACT.Sqrt, bias=s["ln_eps"][:, 0:1], scale=1.0 / D).then_inc(roots.given, 1)


def nodes(nc, name, s, kind, rows_out, H=None):
    SPLIT = ((0, 4), (4, NG))
    hidden = 2 if kind == "mlp" else 0
    with ExitStack() as ctx:
        def sb(n, shape, dt=F32):
            return ctx.enter_context(nc.sbuf_tensor(f"{name}_{n}", shape, dt))

        def ps(n, shape):
            return ctx.enter_context(nc.psum_tensor(f"{name}_{n}", shape, F32))

        def sem(n):
            return ctx.enter_context(nc.semaphore(f"{name}_{n}"))

        joined = sb("joined", [P, NG, 2 * D])
        flipped = ps("flipped", [P, 2, 512])
        act_in = [sb(f"in{n}", [P, NG, P]) for n in range(1 + hidden)]
        dense = [ps(f"dense{n}", [P, 2, 512]) for n in range(hidden)]
        y_ps = ps("y", [P, NG, D])
        v = sb("v", [P, NG, D])
        sq = sb("sq", [P, NG, D])
        stat = sb("stat", [P, 4, NG])
        count = sb("count", [P, NG])
        dense_ready = sem("dense_ready")
        act_ready = sem("act_ready")
        y_ready = sem("y_ready")
        step = sem("step")
        stored = sem("stored")
        norms = {"mlp": 2, "sage1": 0, "sage2": 1}[kind]
        roots = Roots(ctx, nc, name) if norms else None
        if kind == "mlp":
            STEPS, JOIN, weights = 6 + 2 * NORM_STEPS, 2, (s["W0"], s["W1"])
        elif kind == "sage1":
            STEPS, JOIN, weights = 6, 4, ()
        else:
            STEPS, JOIN, weights = 6 + NORM_STEPS, 4, ()

        with nc.Block() as block:
            @block.vector
            def _(dve):
                with dve.Fori(0, NGROUPS) as i:
                    c = Count(step, i * STEPS)
                    tiles = bass.ds(i * NG, NG)
                    if kind == "mlp":
                        c.inc(dve.tensor_copy(joined[:, :, 0:D], s["X"][:, tiles, :]))
                        c.inc(dve.tensor_copy(joined[:, :, D:], s["acc"][:, tiles, 0:D]))
                    else:
                        c.inc(dve.tensor_scalar(count[:], s["acc"][:, tiles, D:D + 1].squeeze(2), 1.0, None, ALU.max))
                        c.wait(dve)
                        c.inc(dve.reciprocal(count[:], count[:]))
                        c.wait(dve)
                        c.inc(dve.tensor_tensor(joined[:, :, 0:D], s["acc"][:, tiles, 0:D], count[:].unsqueeze(2).broadcast_to([P, NG, D]), ALU.mult))
                        c.inc(dve.tensor_copy(joined[:, :, D:], (s["X"] if kind == "sage1" else H)[:, tiles, :]))
                    dve.wait_ge(y_ready, i + 1)
                    if kind == "mlp":
                        c.inc(dve.tensor_tensor(v[:], y_ps[:], row(s, "L0_gnn_b2", NG), ALU.add))
                        layer_norm(dve, c, v[:], sq[:], stat, v[:], roots, i * 2)
                        c.wait(dve)
                        c.inc(dve.tensor_tensor(v[:], v[:], row(s, "L0_gnn_ln_g", NG), ALU.mult))
                        c.wait(dve)
                        c.inc(dve.tensor_tensor(v[:], v[:], row(s, "L0_gnn_ln_b", NG), ALU.add))
                        c.wait(dve)
                        c.inc(dve.scalar_tensor_tensor(v[:], s["X"][:, tiles, :], 2.0, v[:], ALU.mult, ALU.add))
                        layer_norm(dve, c, v[:], sq[:], stat, s["X"][:, tiles, :], roots, i * norms + norms - 1)
                    elif kind == "sage1":
                        c.inc(dve.tensor_tensor(v[:], y_ps[:], row(s, "L1_gnn_b1_l", NG), ALU.add))
                        c.wait(dve)
                        c.inc(dve.tensor_scalar(H[:, tiles, :], v[:], 0.0, None, ALU.max))
                    else:
                        c.inc(dve.tensor_tensor(v[:], y_ps[:], row(s, "L1_gnn_b2_l", NG), ALU.add))
                        c.wait(dve)
                        c.inc(dve.tensor_tensor(v[:], v[:], s["X"][:, tiles, :], ALU.add))
                        layer_norm(dve, c, v[:], sq[:], stat, s["X"][:, tiles, :], roots, i * norms + norms - 1)
                    assert c.n == STEPS, c.n

            @block.tensor
            def _(pe):
                with pe.Fori(0, NGROUPS) as i:
                    pe.wait_ge(step, i * STEPS + JOIN)
                    for b, (t0, t1) in enumerate(SPLIT):
                        for t in range(t0, t1):
                            ins = pe.matmul(flipped[:, b, (t - t0) * P:(t - t0 + 1) * P], joined[:, t, :], s["ident"][:], start=True, stop=True)
                    ins.then_inc(dense_ready, 1)
                    for n, w in enumerate(weights):
                        pe.wait_ge(act_ready, (i * (1 + hidden) + n) * 2 + 2)
                        for b, (t0, t1) in enumerate(SPLIT):
                            ins = pe.matmul(dense[n][:, b, 0:(t1 - t0) * P], w[:], act_in[n][:, t0:t1, :].rearrange("k t p -> k (t p)"), start=True, stop=True)
                        ins.then_inc(dense_ready, 1)
                    pe.wait_ge(act_ready, (i * (1 + hidden) + hidden) * 2 + 2)
                    w = s[{"mlp": "W2", "sage1": "sage1", "sage2": "sage2"}[kind]]
                    for t in range(NG):
                        ins = pe.matmul(y_ps[:, t, :], act_in[hidden][:, t, :], w[:], start=True, stop=True)
                    ins.then_inc(y_ready, 1)

            @block.scalar
            def _(act):
                with act.Fori(0, NGROUPS) as i:
                    for n in range(1 + hidden):
                        act.wait_ge(dense_ready, i * (1 + hidden) + n + 1)
                        frm = dense[n - 1] if n else flipped
                        for b, (t0, t1) in enumerate(SPLIT):
                            to = act_in[n][:, t0:t1, :].rearrange("k t p -> k (t p)")
                            if n:
                                ins = act.activation(to, frm[:, b, 0:(t1 - t0) * P], ACT.Relu, bias=s["b0" if n == 1 else "b1"][:, 0:1])
                            else:
                                ins = act.activation(to, frm[:, b, 0:(t1 - t0) * P], ACT.Copy)
                            ins.then_inc(act_ready, 1)
                    for r in range(norms):
                        norm_root(act, s, stat, roots, i * norms + r)

            @block.sync
            def _(sp):
                with sp.Fori(0, NGROUPS) as i:
                    sp.wait_ge(step, i * STEPS + STEPS)
                    sp.dma_start(rows_out.rearrange("(t p) f -> p t f", p=P)[:, bass.ds(i * NG, NG), :],
                                 (H if kind == "sage1" else s["X"])[:, bass.ds(i * NG, NG), :]).then_inc(stored, 16)
                sp.wait_ge(stored, NGROUPS * 16)


def graph_norm(nc, s, o, rows_out):
    with ExitStack() as ctx:
        def sb(n, shape, dt=F32):
            return ctx.enter_context(nc.sbuf_tensor(f"norm_{n}", shape, dt))

        def sem(n):
            return ctx.enter_context(nc.semaphore(f"norm_{n}"))

        sq = sb("sq", [P, NT, D])
        part = sb("part", [P, 2])
        st = sb("st", [P, 8])
        real = sb("real", [P, 1])
        stat = sb("stat", [P, 4, NT])
        tot = ctx.enter_context(nc.psum_tensor("norm_tot", [P, 2], F32))
        step = sem("step")
        masked = sem("masked")
        parts_ready = sem("parts_ready")
        tot_ready = sem("tot_ready")
        STEPS = 12 + NORM_STEPS
        stored = sem("stored")
        var_ready = sem("all_var_ready")
        root_ready = sem("all_root_ready")
        roots = Roots(ctx, nc, "norm")
        with nc.Block() as block:
            @block.scalar
            def _(act):
                act.wait_ge(var_ready, 1)
                act.activation(st[:, 5:6], st[:, 4:5], ACT.Sqrt, bias=s["ln_eps"][:, 0:1]).then_inc(root_ready, 1)
                norm_root(act, s, stat, roots, 0)

            @block.gpsimd
            def _(pool):
                pool.affine_select(out=real[:], in_=s["ones"][:, 0:1], compare_op=ALU.is_ge, fill=0.0, base=N - (NT - 1) * P - 1,
                                   pattern=[[0, 1]], channel_multiplier=-1).then_inc(masked, 1)

            @block.tensor
            def _(pe):
                pe.wait_ge(parts_ready, 2)
                pe.matmul(tot[:], s["ones"][:], part[:], start=True, stop=True).then_inc(tot_ready, 1)

            @block.vector
            def _(dve):
                c = Count(step)
                X, acc = s["X"], s["acc"][:, 0:NT, 0:D]
                c.inc(dve.tensor_scalar(st[:, 0:1], s["eps"][:], 1.0, None, ALU.add))
                c.wait(dve)
                c.inc(dve.scalar_tensor_tensor(o[:], X[:], st[:, 0:1], acc, ALU.mult, ALU.add))
                dve.wait_ge(masked, 1)
                c.wait(dve)
                c.inc(dve.tensor_scalar(o[:, NT - 1, :], o[:, NT - 1, :], real[:, 0:1], None, ALU.mult))
                c.wait(dve)
                dve.tensor_reduce(part[:, 0:1], o[:].rearrange("p t f -> p (t f)"), AX.X, ALU.add).then_inc(parts_ready, 1)
                c.inc(dve.tensor_tensor(sq[:], o[:], o[:], ALU.mult))
                c.wait(dve)
                dve.tensor_reduce(part[:, 1:2], sq[:].rearrange("p t f -> p (t f)"), AX.X, ALU.add).then_inc(parts_ready, 1)
                dve.wait_ge(tot_ready, 1)
                c.inc(dve.tensor_scalar(st[:, 1:3], tot[:], 1.0 / (N * D), None, ALU.mult))
                c.wait(dve)
                c.inc(dve.tensor_tensor(st[:, 3:4], st[:, 1:2], st[:, 1:2], ALU.mult))
                c.wait(dve)
                dve.tensor_tensor(st[:, 4:5], st[:, 2:3], st[:, 3:4], ALU.subtract).then_inc(var_ready, 1)
                dve.wait_ge(root_ready, 1)
                c.inc(dve.reciprocal(st[:, 5:6], st[:, 5:6]))
                c.wait(dve)
                c.inc(dve.tensor_scalar(o[:], o[:], st[:, 1:2], st[:, 5:6], ALU.subtract, ALU.mult))
                c.wait(dve)
                c.inc(dve.tensor_tensor(o[:], o[:], row(s, "L2_gnn_gamma2", NT), ALU.mult))
                c.wait(dve)
                c.inc(dve.tensor_tensor(o[:], o[:], row(s, "L2_gnn_beta2", NT), ALU.add))
                c.wait(dve)
                c.inc(dve.tensor_tensor(o[:], o[:], X[:], ALU.add))
                c.wait(dve)
                c.inc(dve.scalar_tensor_tensor(o[:], o[:], 0.0, X[:], ALU.max, ALU.add))
                layer_norm(dve, c, o[:], sq[:], stat, X[:], roots, 0)
                assert c.n == STEPS, c.n

            @block.sync
            def _(sp):
                sp.wait_ge(step, STEPS)
                sp.dma_start(rows_out.rearrange("(t p) f -> p t f", p=P), s["X"][:]).then_inc(stored, 16)
                sp.wait_ge(stored, 16)


def score_tables(nc, s, T):
    per_tile = P // BY_SRC.width
    SPLIT = ((0, 4), (4, NG))
    with ExitStack() as ctx:
        def sb(n, shape, dt=F32):
            return ctx.enter_context(nc.sbuf_tensor(f"keys_{n}", shape, dt))

        def ps(n, shape):
            return ctx.enter_context(nc.psum_tensor(f"keys_{n}", shape, F32))

        def sem(n):
            return ctx.enter_context(nc.semaphore(f"keys_{n}"))

        scale = sb("scale", [P, NT])
        xs = sb("xs", [P, NG, D + 1])
        xs_ps = ps("xs_ps", [D + 1, 2, 512])
        xsT = sb("xsT", [D + 1, NG, P])
        t_ps = [ps(f"t_ps{k}", [D + 1, 2, 512]) for k in range(2)]
        Tt = sb("Tt", [D + 1, NG * per_tile, HEADS, BY_SRC.width])
        zero = sb("zero", [D + 1, P])
        scaled = sem("scaled")
        xs_ready = sem("xs_ready")
        dense_ready = sem("dense_ready")
        act_ready = sem("act_ready")
        t_ready = sem("t_ready")
        t_copied = sem("t_copied")
        stored = sem("stored")
        with nc.Block() as block:
            @block.vector
            def _(dve):
                dve.tensor_scalar(scale[:], s["influence"][:], float(D) ** -0.5, None, ALU.mult).then_inc(scaled, 1)
                dve.memset(zero[:], 0.0).then_inc(scaled, 1)
                dve.wait_ge(scaled, 2)
                with dve.Fori(0, NGROUPS) as i:
                    tiles = bass.ds(i * NG, NG)
                    sc = scale[:, tiles].unsqueeze(2)
                    dve.tensor_tensor(xs[:, :, 0:D], s["X"][:, tiles, :], sc.broadcast_to([P, NG, D]), ALU.mult).then_inc(xs_ready, 1)
                    dve.tensor_copy(xs[:, :, D:D + 1], sc).then_inc(xs_ready, 1)
                    for h in range(HEADS):
                        dve.wait_ge(t_ready, i * HEADS + h + 1)
                        if h == 0:
                            dve.wait_ge(stored, i * 16 + 16)
                        for b, (t0, t1) in enumerate(SPLIT):
                            dve.tensor_copy(Tt[:, t0 * per_tile:t1 * per_tile, h, :],
                                            t_ps[h % 2][:, b, 0:(t1 - t0) * P].rearrange("k (b n) -> k b n", n=BY_SRC.width)).then_inc(t_copied, 1)

            @block.tensor
            def _(pe):
                with pe.Fori(0, NGROUPS) as i:
                    pe.wait_ge(xs_ready, i * 2 + 2)
                    for b, (t0, t1) in enumerate(SPLIT):
                        for t in range(t0, t1):
                            ins = pe.matmul(xs_ps[:, b, (t - t0) * P:(t - t0 + 1) * P], xs[:, t, :], s["ident"][:], start=True, stop=True)
                    ins.then_inc(dense_ready, 1)
                    pe.wait_ge(act_ready, i * 2 + 2)
                    for h in range(HEADS):
                        if h >= 2:
                            pe.wait_ge(t_copied, (i * HEADS + h - 1) * 2)
                        for b, (t0, t1) in enumerate(SPLIT):
                            ins = pe.matmul(t_ps[h % 2][:, b, 0:(t1 - t0) * P], s["Wqk"][:, h, :], xsT[:, t0:t1, :].rearrange("k t p -> k (t p)"), start=True, stop=True)
                        ins.then_inc(t_ready, 1)

            @block.scalar
            def _(act):
                with act.Fori(0, NGROUPS) as i:
                    act.wait_ge(dense_ready, i + 1)
                    for b, (t0, t1) in enumerate(SPLIT):
                        act.activation(xsT[:, t0:t1, :].rearrange("k t p -> k (t p)"), xs_ps[:, b, 0:(t1 - t0) * P], ACT.Copy).then_inc(act_ready, 1)

            @block.sync
            def _(sp):
                sp.wait_ge(scaled, 2)
                sp.dma_start(T[:, BY_SRC.buckets - 1, :], zero[:]).then_inc(stored, 16)
                with sp.Fori(0, NGROUPS) as i:
                    sp.wait_ge(t_copied, (i + 1) * HEADS * 2)
                    sp.dma_start(T[:, bass.ds(i * (NG * per_tile), NG * per_tile), :], Tt[:].rearrange("k b h n -> k b (h n)")).then_inc(stored, 16)
                sp.wait_ge(stored, (NGROUPS + 1) * 16)


def load_src_list(nc, keep, s, tables, chunk_bucket):
    def sb(name, shape, dt=F32):
        s[name] = keep.enter_context(nc.sbuf_tensor(name, shape, dt))

    sb("dst_index", [P, BY_SRC.chunks + J], I32)
    sb("src_local", [P, BY_SRC.chunks + J])
    sb("src_bucket", [1, BY_SRC.jt * P], I32)
    sb("U", [P, BY_SRC.buckets, D + 1])
    sb("renew", [P, BY_SRC.chunks])
    with nc.sbuf_tensor("list_table", [P, BY_SRC.chunks, BY_SRC.fields], I32) as table, \
            nc.sbuf_tensor("list_line", [1, 2, BY_SRC.chunks], F32) as line, nc.sbuf_tensor("list_ones", [1, P], F32) as ones_row, \
            nc.semaphore("list_line_ready") as line_ready, nc.semaphore("list_spread") as spread, \
            nc.semaphore("list_loaded") as loaded, nc.semaphore("list_ready") as ready, ExitStack() as ctx:
        pieces = 5
        CW = BY_SRC.chunks // pieces
        wide = [ctx.enter_context(nc.psum_tensor(f"list_wide{n}", [P, 512], F32)) for n in range(pieces)]
        block = ctx.enter_context(nc.Block())

        @block.sync
        def _(sp):
            sp.dma_start(table[:], tables["src"].rearrange("(p c) f -> p c f", p=P)).then_inc(loaded, 16)
            sp.dma_start(s["src_bucket"][:], chunk_bucket["src"].unsqueeze(0)).then_inc(loaded, 16)
            sp.wait_ge(loaded, 32)

        @block.tensor
        def _(pe):
            pe.wait_ge(line_ready, 5)
            for n in range(pieces):
                pe.matmul(wide[n][:, 0:CW], ones_row[:], line[:, 1, n * CW:(n + 1) * CW], start=True, stop=True).then_inc(spread, 1)

        @block.vector
        def _(dve):
            dve.memset(s["U"][:], 0.0).then_inc(ready, 1)
            dve.memset(ones_row[:], 1.0).then_inc(line_ready, 1)
            dve.memset(line[:, 1, 0:1], 1.0).then_inc(line_ready, 1)
            dve.wait_ge(loaded, 32)
            dve.tensor_copy(line[:, 0, :], s["src_bucket"][:, 0:BY_SRC.chunks]).then_inc(line_ready, 1)
            dve.wait_ge(line_ready, 3)
            dve.tensor_tensor(line[:, 1, 1:], line[:, 0, 1:], line[:, 0, 0:BY_SRC.chunks - 1], ALU.not_equal).then_inc(line_ready, 2)
            for n in range(pieces):
                dve.wait_ge(spread, n + 1)
                dve.tensor_scalar(s["renew"][:, n * CW:(n + 1) * CW], wide[n][:, 0:CW], NO_SCORE, None, ALU.mult).then_inc(ready, 1)
            dve.wait_ge(loaded, 32)
            dve.tensor_copy(s["dst_index"][:, 0:BY_SRC.chunks], table[:, :, 0:1].squeeze(2)).then_inc(ready, 1)
            dve.memset(s["dst_index"][:, BY_SRC.chunks:], 0).then_inc(ready, 1)
            dve.tensor_copy(s["src_local"][:, 0:BY_SRC.chunks], table[:, :, 1:2].squeeze(2)).then_inc(ready, 1)
            dve.memset(s["src_local"][:, BY_SRC.chunks:], ABSENT).then_inc(ready, 1)
            dve.wait_ge(ready, 5 + pieces)


def attention(nc, s, rows, T):
    W = BY_SRC.width
    K = D + 1 + W
    UNIT = J // 2
    BODY = 2 * GB
    groups = BY_SRC.chunks // J
    units = 2 * groups
    assert groups % GB == 0
    with ExitStack() as ctx:
        def sb1(n, shape, dt=F32):
            return ctx.enter_context(nc.sbuf_tensor(f"att_{n}", shape, dt))

        def sb(n, shape, dt=F32, count=2):
            return [sb1(f"{n}{k}", shape, dt) for k in range(count)]

        def ps(n):
            return [ctx.enter_context(nc.psum_tensor(f"att_{n}{k}", [P, UNIT, P], F32)) for k in range(2)]

        def sem(n):
            return ctx.enter_context(nc.semaphore(f"att_{n}"))

        idx = sb("idx", [P, J], I32, GB)
        got = sb("got", [P, J, K], F32, GB)
        Tt = sb("Tt", [K, J, P])
        turned = sb("turned", [K, UNIT, P])
        probs = sb("probs", [P, UNIT, P])
        probsT = sb("probsT", [P, UNIT, P])
        top = sb1("top", [P, UNIT])
        floor = sb1("floor", [P, UNIT])
        before = sb1("before", [P, UNIT])
        running = sb("running", [P, 1 + UNIT])
        total = sb("total", [P, UNIT, D + 1])
        minus = sb("minus", [P, UNIT])
        drop = sb("drop", [P, UNIT])
        keep = sb("keep", [P, UNIT], F32, 4)
        maskrow = sb1("maskrow", [W, HEADS, W])
        flipped, scores, flipped2, sums = ps("flipped"), ps("scores"), ps("flipped2"), ps("sums")
        started = sem("started")
        mask_set = sem("mask_set")
        idx_copied = sem("idx_copied")
        gathered = [sem(f"gathered{k}") for k in range(GB)]
        T_loaded = [sem(f"T_loaded{k}") for k in range(2)]
        masked = [sem(f"masked{k}") for k in range(GB)]
        flip_ready = sem("flip_ready")
        turned_ready = sem("turned_ready")
        scores_ready = sem("scores_ready")
        step = sem("step")
        probs_ready = sem("probs_ready")
        keep_ready = sem("keep_ready")
        flip2_ready = sem("flip2_ready")
        probsT_ready = sem("probsT_ready")
        sums_ready = sem("sums_ready")
        added = sem("added")
        flushed = sem("flushed")
        primed = sem("primed")
        STEPS = 7

        def known(n):
            return isinstance(n, int)

        def wait(eng, semaphore, value):
            if not known(value) or value > 0:
                eng.wait_ge(semaphore, value)

        def in_steps(eng, run):
            for u in range(BODY):
                run(u, u)
            with eng.Fori(BODY, units - BODY + 1, BODY) as base:
                for r in range(BODY):
                    run(base + r, r)
            for u in range(units, units + 4):
                run(u, u % BODY)

        def there(v):
            return not known(v) or 0 <= v < units

        def in_groups(eng, n, run):
            for g in range(n):
                run(g, g)
            with eng.Fori(n, groups - n + 1, n) as base:
                for k in range(n):
                    run(base + k, k)

        with nc.Block() as block:
            @block.gpsimd
            def _(pool):
                pool.memset(maskrow[:], 0.0).then_inc(mask_set, 1)
                pool.wait_ge(mask_set, 1)
                pool.affine_select(out=maskrow[:], in_=maskrow[:], compare_op=ALU.not_equal, fill=NO_SCORE, base=0,
                                   pattern=[[0, HEADS], [-1, W]], channel_multiplier=1).then_inc(mask_set, 1)

                def copy_index(g, k):
                    pool.tensor_copy(idx[k][:], s["dst_index"][:, bass.ds(g * J, J)]).then_inc(idx_copied, 1)

                def gather(g, k):
                    wait(pool, sums_ready, 2 * g - 4)
                    copy_index(g + 1, (k + 1) % GB)
                    pool.wait_ge(idx_copied, g + 1)
                    pool.nop(nofuse=True)
                    for t in range(J):
                        pool.indirect_dma_start(got[k][:, t, 0:D], None, rows, bass.IndirectOffsetOnAxis(ap=idx[k][:, t:t + 1], axis=0)).then_inc(gathered[k], 16)

                copy_index(0, 0)
                in_groups(pool, GB, gather)

            @block.sync
            def _(sp):
                sp.wait_ge(mask_set, 2)
                for k in range(2):
                    for t in range(J):
                        sp.dma_start(Tt[k][D + 1:K, t, :], maskrow[:].rearrange("k h n -> k (h n)")).then_inc(started, 16)

                def load(g, k):
                    wait(sp, scores_ready, 2 * g - 2)
                    for t in range(J):
                        b = sp.value_load(s["src_bucket"][0:1, bass.ds(g * J + t, 1)], min_val=0, max_val=BY_SRC.buckets - 1)
                        sp.dma_start(Tt[k][0:D + 1, t, :], T[:, bass.ds(b, 1), :].squeeze(1)).then_inc(T_loaded[k], 16)

                in_groups(sp, 2, load)

            @block.tensor
            def _(pe):
                pe.wait_ge(started, 2 * J * 16 + GB)

                def turn(v, r):
                    k, half = r // 2, r % 2
                    if half == 0:
                        pe.wait_ge(gathered[k], (v - r) * J * 2 + J * 16)
                        pe.wait_ge(masked[k], (v - r) + BODY)
                    wait(pe, turned_ready, v - 1)
                    for t in range(UNIT):
                        ins = pe.matmul(flipped[r % 2][0:K, t, :], got[k][:, half * UNIT + t, :], s["ident"][:], start=True, stop=True)
                    ins.then_inc(flip_ready, 1)

                def turn_probs(v, r):
                    pe.wait_ge(probs_ready, v + 1)
                    wait(pe, probsT_ready, v - 1)
                    for t in range(UNIT):
                        ins = pe.matmul(flipped2[r % 2][:, t, :], probs[r % 2][:, t, :], s["ident"][:], start=True, stop=True)
                    ins.then_inc(flip2_ready, 1)

                def score(v, r):
                    k, half = (r // 2) % 2, r % 2
                    if half == 0:
                        pe.wait_ge(T_loaded[k], (v - r) * (J * 4) + (r // 4 + 1) * J * 16)
                    pe.wait_ge(turned_ready, v + 1)
                    wait(pe, probs_ready, v - 1)
                    for t in range(UNIT):
                        ins = pe.matmul(scores[r % 2][:, t, :], Tt[k][:, half * UNIT + t, :], turned[r % 2][:, t, :], start=True, stop=True)
                    ins.then_inc(scores_ready, 1)

                def sum_up(v, r):
                    k, half = r // 2, r % 2
                    pe.wait_ge(probsT_ready, v + 1)
                    wait(pe, added, (v - 1) * UNIT)
                    for t in range(UNIT):
                        ins = pe.matmul(sums[r % 2][:, t, 0:D + 1], probsT[r % 2][:, t, :], got[k][:, half * UNIT + t, 0:D + 1], start=True, stop=True)
                    ins.then_inc(sums_ready, 1)

                def run(u, r):
                    for lag, what in ((0, turn), (2, turn_probs), (1, score), (3, sum_up)):
                        if there(u - lag):
                            what(u - lag, (r - lag) % BODY)

                in_steps(pe, run)

            @block.scalar
            def _(act):
                def copy_turned(v, r):
                    act.wait_ge(flip_ready, v + 1)
                    wait(act, scores_ready, v - 1)
                    act.activation(turned[r % 2][:], flipped[r % 2][0:K], ACT.Copy).then_inc(turned_ready, 1)

                def copy_probs(v, r):
                    act.wait_ge(flip2_ready, v + 1)
                    wait(act, sums_ready, v - 1)
                    act.activation(probsT[r % 2][:], flipped2[r % 2][:], ACT.Copy).then_inc(probsT_ready, 1)

                def exponentials(v, r):
                    act.wait_ge(step, v * STEPS + STEPS)
                    wait(act, flip2_ready, v - 1)
                    for t in range(UNIT):
                        ins = act.activation(probs[r % 2][:, t, :], scores[r % 2][:, t, :], ACT.Exp, bias=minus[r % 2][:, t:t + 1])
                    ins.then_inc(probs_ready, 1)
                    wait(act, added, (v - 3) * UNIT)
                    act.activation(keep[r % 4][:], drop[r % 2][:], ACT.Exp).then_inc(keep_ready, 1)

                def flush(v, r):
                    buckets = [act.value_load(s["src_bucket"][0:1, bass.ds(v * UNIT + t, 1)], min_val=0, max_val=BY_SRC.buckets - 1) for t in range(UNIT)]
                    act.wait_ge(added, (v + 1) * UNIT)
                    for t in range(UNIT):
                        wait(act, flushed, v * UNIT + t)
                        act.activation(s["U"][:, bass.ds(buckets[t], 1), :].squeeze(1), total[r % 2][:, t, :], ACT.Copy).then_inc(flushed, 1)

                def run(u, r):
                    for lag, what in ((0, copy_turned), (2, copy_probs), (1, exponentials), (4, flush)):
                        if there(u - lag):
                            what(u - lag, (r - lag) % BODY)

                in_steps(act, run)

            @block.vector
            def _(dve):
                for k in range(GB):
                    dve.memset(got[k][:, :, D:D + 1], 1.0).then_inc(started, 1)
                dve.memset(running[1][:], NO_MAX).then_inc(primed, 1)
                dve.memset(total[1][:], 0.0).then_inc(primed, 1)
                dve.wait_ge(primed, 2)

                def mask(v, k):
                    wait(dve, sums_ready, v - 2 * GB + 2)
                    local = s["src_local"][:, bass.ds(v * UNIT, J)].unsqueeze(2).broadcast_to([P, J, W])
                    dve.tensor_tensor(got[k][:, :, D + 1:K], local, s["iota_row"][:, 0:W].unsqueeze(1).broadcast_to([P, J, W]),
                                      ALU.not_equal).then_inc(masked[k], BODY)

                def maxima(v, r):
                    renew = s["renew"][:, bass.ds(v * UNIT, UNIT)]
                    now, last = running[r % 2], running[1 - r % 2]
                    c = Count(step, v * STEPS)
                    dve.wait_ge(scores_ready, v + 1)
                    c.inc(dve.tensor_reduce(top[:], scores[r % 2][:], AX.X, ALU.max))
                    wait(dve, step, v * STEPS - 1)
                    c.inc(dve.tensor_scalar(now[:, 0:1], last[:, UNIT:], 0.0, None, ALU.add))
                    c.wait(dve)
                    c.inc(dve.tensor_scalar(floor[:], top[:], NO_MAX, None, ALU.max))
                    c.wait(dve)
                    c.inc(dve.tensor_tensor_scan(now[:, 1:], renew, floor[:], now[:, 0:1], ALU.add, ALU.max))
                    c.wait(dve)
                    wait(dve, keep_ready, v - 1)
                    c.inc(dve.tensor_scalar(minus[r % 2][:], now[:, 1:], -1.0, None, ALU.mult))
                    c.inc(dve.tensor_tensor(before[:], now[:, 0:UNIT], renew, ALU.add))
                    c.wait(dve)
                    c.inc(dve.tensor_tensor(drop[r % 2][:], before[:], now[:, 1:], ALU.subtract))
                    assert c.n == STEPS, c.n

                def add(v, r):
                    dve.wait_ge(keep_ready, v + 1)
                    dve.wait_ge(sums_ready, v + 1)
                    wait(dve, flushed, (v - 1) * UNIT)
                    for t in range(UNIT):
                        last = total[r % 2][:, t - 1, :] if t else total[1 - r % 2][:, UNIT - 1, :]
                        wait(dve, added, v * UNIT + t)
                        dve.scalar_tensor_tensor(total[r % 2][:, t, :], last, keep[r % 4][:, t:t + 1], sums[r % 2][:, t, 0:D + 1], ALU.mult, ALU.add).then_inc(added, 1)

                mask(0, 0)

                def run(u, r):
                    if there(u + 2) and r % 2 == 0:
                        mask(u + 2, (r // 2 + 1) % GB)
                    for lag, what in ((1, maxima), (3, add)):
                        if there(u - lag):
                            what(u - lag, (r - lag) % BODY)

                in_steps(dve, run)


def attention_out(nc, s, out):
    B = P // BY_SRC.width
    last = N - (NT - 1) * P
    with ExitStack() as ctx:
        def sb(n, shape, dt=F32):
            return ctx.enter_context(nc.sbuf_tensor(f"fin_{n}", shape, dt))

        def ps(n, shape):
            return [ctx.enter_context(nc.psum_tensor(f"fin_{n}{k}", shape, F32)) for k in range(2)]

        def sem(n):
            return ctx.enter_context(nc.semaphore(f"fin_{n}"))

        inv = sb("inv", [P, NG * B])
        un = sb("un", [P, NG * B, D + 1])
        flipped = ps("flipped", [D + 1, B, HEADS, BY_SRC.width])
        uT = [sb(f"uT{k}", [D + 1, HEADS, B, BY_SRC.width]) for k in range(2)]
        o_ps = ps("o", [D, HEADS, P])
        oT = [sb(f"oT{k}", [D, HEADS, P]) for k in range(2)]
        y_ps = ctx.enter_context(nc.psum_tensor("fin_y", [P, NG, D], F32))
        v = sb("v", [P, NG, D])
        res = sb("res", [P, NG, D])
        sq = sb("sq", [P, NG, D])
        stat = sb("stat", [P, 4, NG])
        step = sem("step")
        flip_ready = sem("flip_ready")
        uT_ready = sem("uT_ready")
        o_ready = sem("o_ready")
        oT_ready = sem("oT_ready")
        y_ready = sem("y_ready")
        stored = sem("stored")
        roots = Roots(ctx, nc, "fin")
        DIV = 3
        STEPS = DIV + 2 + NORM_STEPS
        with nc.Block() as block:
            @block.vector
            def _(dve):
                def group(i):
                    c = Count(step, i * STEPS)
                    tiles = bass.ds(i * NG, NG)
                    u = s["U"][:, bass.ds(i * (NG * B), NG * B), :]
                    c.inc(dve.tensor_scalar(inv[:], u[:, :, D:D + 1].squeeze(2), 1e-10, None, ALU.add))
                    c.wait(dve)
                    c.inc(dve.reciprocal(inv[:], inv[:]))
                    c.wait(dve)
                    c.inc(dve.tensor_tensor(un[:], u, inv[:].unsqueeze(2).broadcast_to([P, NG * B, D + 1]), ALU.mult))
                    dve.wait_ge(y_ready, i + 1)
                    c.inc(dve.tensor_tensor(v[:], y_ps[:], row(s, "L3_gnn_bo", NG), ALU.add))
                    c.wait(dve)
                    c.inc(dve.tensor_tensor(v[:], v[:], s["X"][:, tiles, :], ALU.add))
                    if not isinstance(i, int):
                        dve.wait_ge(stored, i * 16)
                    layer_norm(dve, c, v[:], sq[:], stat, res[:], roots, i)
                    assert c.n == STEPS

                group(0)
                with dve.Fori(1, NGROUPS) as i:
                    group(i)

            @block.tensor
            def _(pe):
                with pe.Fori(0, NGROUPS) as i:
                    pe.wait_ge(step, i * STEPS + DIV)
                    for t in range(NG + 2):
                        if t < NG:
                            for b in range(B):
                                ins = pe.matmul(flipped[t % 2][:, b].rearrange("k h n -> k (h n)"), un[:, t * B + b, :], s["ident"][:], start=True, stop=True)
                            ins.then_inc(flip_ready, 1)
                        if 1 <= t < NG + 1:
                            n = t - 1
                            pe.wait_ge(uT_ready, i * NG + n + 1)
                            for h in range(HEADS):
                                ins = pe.matmul(o_ps[n % 2][:, h, :], s["Wv"][:, h * D:(h + 1) * D], uT[n % 2][:, h].rearrange("k b n -> k (b n)"), start=True, stop=True)
                            ins.then_inc(o_ready, 1)
                        if t >= 2:
                            n = t - 2
                            pe.wait_ge(oT_ready, i * NG + n + 1)
                            for h in range(HEADS):
                                ins = pe.matmul(y_ps[:, n, :], oT[n % 2][:, h, :], s["Wo"][:, h, :], start=(h == 0), stop=(h == HEADS - 1))
                    ins.then_inc(y_ready, 1)

            @block.scalar
            def _(act):
                with act.Fori(0, NGROUPS) as i:
                    for t in range(NG + 1):
                        if t < NG:
                            act.wait_ge(flip_ready, i * NG + t + 1)
                            act.activation(uT[t % 2][:].rearrange("k h b n -> k b h n"), flipped[t % 2][:], ACT.Copy).then_inc(uT_ready, 1)
                        if t >= 1:
                            act.wait_ge(o_ready, i * NG + t)
                            act.activation(oT[(t - 1) % 2][:], o_ps[(t - 1) % 2][:], ACT.Copy).then_inc(oT_ready, 1)
                    norm_root(act, s, stat, roots, i)

            @block.sync
            def _(sp):
                with sp.Fori(0, NGROUPS - 1) as i:
                    sp.wait_ge(step, i * STEPS + STEPS)
                    sp.dma_start(out[0:(NT - NG) * P, :].rearrange("(t p) f -> p t f", p=P)[:, bass.ds(i * NG, NG), :], res[:]).then_inc(stored, 16)
                sp.wait_ge(step, NGROUPS * STEPS)
                sp.dma_start(out[(NT - NG) * P:(NT - 1) * P, :].rearrange("(t p) f -> p t f", p=P), res[:, 0:NG - 1, :]).then_inc(stored, 16)
                sp.dma_start(out[(NT - 1) * P:N, :], res[0:last, NG - 1, :]).then_inc(stored, 16)
                sp.wait_ge(stored, (NGROUPS + 1) * 16)


def gnn(nc, a, out):
    def dram(name, shape, dt=F32):
        return nc.dram_tensor(name, shape, dt, kind="Internal").ap()

    tables = {l.name: dram(l.name + "_table", [P * l.chunks, l.fields], I32) for l in LISTS}
    chunk_bucket = {l.name: dram(l.name + "_chunk_bucket", [P * l.jt], I32) for l in LISTS}
    hist = {l.name: dram(l.name + "_hist", [l.hi, LO]) for l in LISTS}
    ea = dram("ea", [P, BY_DST.chunks, D])
    rows = [dram(f"rows{i}", [NPAD, D]) for i in range(4)]
    T = dram("T", [D + 1, BY_SRC.buckets, P])
    edge_rows = dram("rows_of_edges", [P * TILES, BY_DST.fields], I32)
    chunk_start = dram("chunk_start_of_all", [P * BY_DST.jt], I32)
    chunk_from = dram("chunk_from_of_all", [P * BY_DST.jt])
    with ExitStack() as keep:
        unsorted = keep.enter_context(nc.sbuf_tensor("unsorted", [1, 1], I32))
        sort_edges(nc, a["src"], a["dst"], tables, chunk_bucket, hist, edge_rows, chunk_start, chunk_from, unsorted)
        with ExitStack() as by_dst:
            s = load_shared(nc, keep, by_dst, a, tables, chunk_bucket, edge_rows, chunk_start, chunk_from, unsorted)
            H = by_dst.enter_context(nc.sbuf_tensor("H", [P, NT, D], F32))
            gather_sum(nc, "l0", s, a["edge_attr_64"], s["edge_index"], False, "attr", ea)
            nodes(nc, "n0", s, "mlp", rows[0])
            gather_sum(nc, "l1a", s, rows[0], s["src_index"], True)
            nodes(nc, "n1a", s, "sage1", rows[1], H)
            gather_sum(nc, "l1b", s, rows[1], s["src_index"], True)
            nodes(nc, "n1b", s, "sage2", rows[2], H)
            gather_sum(nc, "l2", s, rows[2], s["src_index"], False, "message", ea)
            graph_norm(nc, s, H, rows[3])
        score_tables(nc, s, T)
        load_src_list(nc, keep, s, tables, chunk_bucket)
        attention(nc, s, rows[3], T)
        attention_out(nc, s, out)


_INS = ["x", "src", "dst", "edge_attr_64", "node_vec"] + [n for n, _ in WEIGHTS]


def kernel(**inputs):
    import numpy as _np
    import concourse.bacc as _bacc
    from concourse import mybir as _mybir
    from concourse.bass_utils import run_bass_kernel_spmd as _run

    nc = _bacc.Bacc("TRN2", target_bir_lowering=False, num_devices=1)
    arrays, aps = {}, {}
    for name in _INS:
        a = _np.ascontiguousarray(inputs[name])
        arrays[f"in_{name}_dram"] = a
        aps[name] = nc.dram_tensor(f"in_{name}_dram", a.shape, _mybir.dt.from_np(a.dtype), kind="ExternalInput").ap()
    out = nc.dram_tensor("out_0_dram", (N, D), _mybir.dt.float32, kind="ExternalOutput").ap()
    gnn(nc, aps, out)
    r = _run(nc, [arrays], core_ids=[0])
    return r.results[0]["out_0_dram"]
```
